# Optimizing a Trainium2 kernel written in Bass

```python
import numpy as np
import jax
import jax.numpy as jnp

def _softmax(x, axis=-1):
    return jax.nn.softmax(x, axis=axis)

def _gelu(x):
    return jax.nn.gelu(x, approximate=True)

def _silu(x):
    return jax.nn.silu(x)

def _sigmoid(x):
    return jax.nn.sigmoid(x)

def _layernorm(x, axis=-1, eps=1e-05):
    m = jnp.mean(x, axis=axis, keepdims=True)
    v = jnp.var(x, axis=axis, keepdims=True)
    return (x - m) / jnp.sqrt(v + eps)

def _scatter_add(tgt, idx, src, axis=0):
    return tgt.at[idx].add(src)

def _segment_sum(src, seg, n):
    return jax.ops.segment_sum(src, seg, n)
kernel_name = 'mk_xattn_ffn_d1_seqx_r8_f67cd1'

def setup_inputs(seed: int=0):
    np.random.seed(seed)
    _w = jnp.asarray

    def _rec_inputs():
        import jax
        import jax.numpy as jnp
        _rk = jax.random.key(seed)
        x = -4.161e-06 + 1 * jax.random.normal(jax.random.fold_in(_rk, 1), (16, 128, 256), jnp.float32)
        _lenS = 128 - jax.random.randint(jax.random.fold_in(_rk, 7), (16,), 0, max(1, 128 // 4) + 1, jnp.int32)
        _lenS2 = 128 - jax.random.randint(jax.random.fold_in(_rk, 8), (16,), 0, max(1, 128 // 4) + 1, jnp.int32)
        _ctx_2048P = jax.random.normal(jax.random.fold_in(_rk, 11), (16, 16, 256), jnp.float32)
        _ctx_2048c = jax.random.dirichlet(jax.random.fold_in(_rk, 511), 0.3 * jnp.ones((16,), jnp.float32), (16, 128))
        _ctx_2048t = jnp.einsum('bsk,bkd->bsd', _ctx_2048c, _ctx_2048P)
        _ctx_2048t = _ctx_2048t * jax.lax.rsqrt(jnp.mean(jnp.square(_ctx_2048t)) + 1e-12) * 0.953939
        ctx_2048 = -0.000192764 + 0.999654 * (_ctx_2048t + 0.3 * jax.random.normal(jax.random.fold_in(_rk, 611), (16, 128, 256), jnp.float32))
        return (x, ctx_2048)
    x, ctx_2048 = _rec_inputs()

    def _L0_xattn_setup():
        import jax, jax.numpy as jnp
        import numpy as np
        FP8_MAX = 448.0
        EPS = 1e-05

        def _fp8_roundtrip(x):
            return x.astype(jnp.float8_e4m3fn).astype(jnp.float32)

        def _div_clamp_fp8(x, scale):
            y = jnp.clip(x.astype(jnp.float32) / scale, -FP8_MAX, FP8_MAX)
            y = y.astype(jnp.bfloat16).astype(jnp.float32)
            return _fp8_roundtrip(y)

        def _ln(x, w, b):
            mu = jnp.mean(x, axis=-1, keepdims=True)
            var = jnp.mean(jnp.square(x - mu), axis=-1, keepdims=True)
            return (x - mu) * jax.lax.rsqrt(var + EPS) * w + b

        def _fp8_linear_pertensor(x, wq, w_scale, in_scale):
            xq = _div_clamp_fp8(x, in_scale)
            return jnp.einsum('bsi,oi->bso', xq * in_scale, wq) * w_scale

        def _gqa(q, k, v):
            scale = 1.0 / np.sqrt(q.shape[-1])
            scores = jnp.einsum('bsghd,btgd->bghst', q, k) * scale
            p = jax.nn.softmax(scores, axis=-1)
            return jnp.einsum('bghst,btgd->bsghd', p, v)
        key = jax.random.key(seed)
        ks = jax.random.split(key, 8)
        B, S, SC, H, NH, G, D = (2, 256, 64, 256, 16, 8, 128)

        def qw(k, out_f, in_f):
            w = jax.random.normal(k, (out_f, in_f), jnp.float32) * 0.02
            sc = jnp.max(jnp.abs(w)) / FP8_MAX
            return (_fp8_roundtrip(w / sc), sc.astype(jnp.float32))
        wq, wq_s = qw(ks[0], NH * D, H)
        wqx, wqx_s = qw(ks[1], NH * D, H)
        wk, wk_s = qw(ks[2], G * D, H)
        wv, wv_s = qw(ks[3], G * D, H)
        wproj, wp_s = qw(ks[4], H, 2 * NH * D)
        return {'hidden_states': jax.random.normal(ks[5], (B, S, H), jnp.float32), 'cond': jax.random.normal(ks[6], (B, SC, H), jnp.float32), 'ln_w': jnp.ones((H,), jnp.float32), 'ln_b': jnp.zeros((H,), jnp.float32), 'wq': wq, 'wq_scale': wq_s, 'q_in_scale': jnp.full((H,), 0.05, jnp.float32), 'wqx': wqx, 'wqx_scale': wqx_s, 'qx_in_scale': jnp.full((H,), 0.05, jnp.float32), 'wk': wk, 'wk_scale': wk_s, 'k_in_scale': jnp.full((H,), 0.05, jnp.float32), 'wv': wv, 'wv_scale': wv_s, 'v_in_scale': jnp.full((H,), 0.05, jnp.float32), 'w_kv_x': jax.random.normal(ks[7], (2 * G * D, H), jnp.float32) * 0.02, 'qln_w': jnp.ones((D,), jnp.float32), 'qln_b': jnp.zeros((D,), jnp.float32), 'kln_w': jnp.ones((D,), jnp.float32), 'kln_b': jnp.zeros((D,), jnp.float32), 'qxln_w': jnp.ones((D,), jnp.float32), 'qxln_b': jnp.zeros((D,), jnp.float32), 'kxln_w': jnp.ones((D,), jnp.float32), 'kxln_b': jnp.zeros((D,), jnp.float32), 'wproj': wproj, 'proj_w_scale': wp_s, 'proj_in_scale': jnp.asarray(0.05, jnp.float32), 'proj_smooth': jnp.full((2 * NH * D,), 0.05, jnp.float32)}
    _L0_xattn_all = _L0_xattn_setup()
    _L0_xattn_in = {k: v for k, v in _L0_xattn_all.items() if k in ('ln_w', 'ln_b', 'wq', 'wq_scale', 'q_in_scale', 'wqx', 'wqx_scale', 'qx_in_scale', 'wk', 'wk_scale', 'k_in_scale', 'wv', 'wv_scale', 'v_in_scale', 'w_kv_x', 'qln_w', 'qln_b', 'kln_w', 'kln_b', 'qxln_w', 'qxln_b', 'kxln_w', 'kxln_b', 'wproj', 'proj_w_scale', 'proj_in_scale', 'proj_smooth')}
    del _L0_xattn_all

    def _L0_ffn_setup():
        import jax, jax.numpy as jnp
        import numpy as np
        HIDDEN = 256
        FFN = 512
        E = 8
        TOP_K = 2
        key = jax.random.key(seed)
        ks = jax.random.split(key, 5)
        x = jax.random.normal(ks[0], (2, 256, HIDDEN), dtype=jnp.float32)
        gate_w = jax.random.normal(ks[1], (E, HIDDEN), dtype=jnp.float32) * 0.02
        w1 = jax.random.normal(ks[2], (E, FFN, HIDDEN), dtype=jnp.float32) * 0.02
        w3 = jax.random.normal(ks[3], (E, FFN, HIDDEN), dtype=jnp.float32) * 0.02
        w2 = jax.random.normal(ks[4], (E, HIDDEN, FFN), dtype=jnp.float32) * 0.02
        return {'x': x, 'gate_w': gate_w, 'w1': w1, 'w2': w2, 'w3': w3}
    _L0_ffn_all = _L0_ffn_setup()
    _L0_ffn_in = {k: v for k, v in _L0_ffn_all.items() if k in ('gate_w', 'w1', 'w2', 'w3')}
    del _L0_ffn_all
    return {'x': x, 'ctx_2048': ctx_2048, 'L0_xattn_ln_w': _L0_xattn_in['ln_w'], 'L0_xattn_ln_b': _L0_xattn_in['ln_b'], 'L0_xattn_wq': _L0_xattn_in['wq'], 'L0_xattn_wq_scale': _L0_xattn_in['wq_scale'], 'L0_xattn_q_in_scale': _L0_xattn_in['q_in_scale'], 'L0_xattn_wqx': _L0_xattn_in['wqx'], 'L0_xattn_wqx_scale': _L0_xattn_in['wqx_scale'], 'L0_xattn_qx_in_scale': _L0_xattn_in['qx_in_scale'], 'L0_xattn_wk': _L0_xattn_in['wk'], 'L0_xattn_wk_scale': _L0_xattn_in['wk_scale'], 'L0_xattn_k_in_scale': _L0_xattn_in['k_in_scale'], 'L0_xattn_wv': _L0_xattn_in['wv'], 'L0_xattn_wv_scale': _L0_xattn_in['wv_scale'], 'L0_xattn_v_in_scale': _L0_xattn_in['v_in_scale'], 'L0_xattn_w_kv_x': _L0_xattn_in['w_kv_x'], 'L0_xattn_qln_w': _L0_xattn_in['qln_w'], 'L0_xattn_qln_b': _L0_xattn_in['qln_b'], 'L0_xattn_kln_w': _L0_xattn_in['kln_w'], 'L0_xattn_kln_b': _L0_xattn_in['kln_b'], 'L0_xattn_qxln_w': _L0_xattn_in['qxln_w'], 'L0_xattn_qxln_b': _L0_xattn_in['qxln_b'], 'L0_xattn_kxln_w': _L0_xattn_in['kxln_w'], 'L0_xattn_kxln_b': _L0_xattn_in['kxln_b'], 'L0_xattn_wproj': _L0_xattn_in['wproj'], 'L0_xattn_proj_w_scale': _L0_xattn_in['proj_w_scale'], 'L0_xattn_proj_in_scale': _L0_xattn_in['proj_in_scale'], 'L0_xattn_proj_smooth': _L0_xattn_in['proj_smooth'], 'L0_ffn_gate_w': _L0_ffn_in['gate_w'], 'L0_ffn_w1': _L0_ffn_in['w1'], 'L0_ffn_w2': _L0_ffn_in['w2'], 'L0_ffn_w3': _L0_ffn_in['w3']}

def reference(x, ctx_2048, L0_xattn_ln_w, L0_xattn_ln_b, L0_xattn_wq, L0_xattn_wq_scale, L0_xattn_q_in_scale, L0_xattn_wqx, L0_xattn_wqx_scale, L0_xattn_qx_in_scale, L0_xattn_wk, L0_xattn_wk_scale, L0_xattn_k_in_scale, L0_xattn_wv, L0_xattn_wv_scale, L0_xattn_v_in_scale, L0_xattn_w_kv_x, L0_xattn_qln_w, L0_xattn_qln_b, L0_xattn_kln_w, L0_xattn_kln_b, L0_xattn_qxln_w, L0_xattn_qxln_b, L0_xattn_kxln_w, L0_xattn_kxln_b, L0_xattn_wproj, L0_xattn_proj_w_scale, L0_xattn_proj_in_scale, L0_xattn_proj_smooth, L0_ffn_gate_w, L0_ffn_w1, L0_ffn_w2, L0_ffn_w3):
    import jax
    import jax.numpy as jnp

    def _L0_xattn_ref(hidden_states, cond, ln_w, ln_b, wq, wq_scale, q_in_scale, wqx, wqx_scale, qx_in_scale, wk, wk_scale, k_in_scale, wv, wv_scale, v_in_scale, w_kv_x, qln_w, qln_b, kln_w, kln_b, qxln_w, qxln_b, kxln_w, kxln_b, wproj, proj_w_scale, proj_in_scale, proj_smooth):
        import jax, jax.numpy as jnp
        import numpy as np
        FP8_MAX = 448.0
        EPS = 1e-05

        def _fp8_roundtrip(x):
            return x.astype(jnp.float8_e4m3fn).astype(jnp.float32)

        def _div_clamp_fp8(x, scale):
            y = jnp.clip(x.astype(jnp.float32) / scale, -FP8_MAX, FP8_MAX)
            y = y.astype(jnp.bfloat16).astype(jnp.float32)
            return _fp8_roundtrip(y)

        def _ln(x, w, b):
            mu = jnp.mean(x, axis=-1, keepdims=True)
            var = jnp.mean(jnp.square(x - mu), axis=-1, keepdims=True)
            return (x - mu) * jax.lax.rsqrt(var + EPS) * w + b

        def _fp8_linear_pertensor(x, wq, w_scale, in_scale):
            xq = _div_clamp_fp8(x, in_scale)
            return jnp.einsum('bsi,oi->bso', xq * in_scale, wq) * w_scale

        def _gqa(q, k, v):
            scale = 1.0 / np.sqrt(q.shape[-1])
            scores = jnp.einsum('bsghd,btgd->bghst', q, k) * scale
            p = jax.nn.softmax(scores, axis=-1)
            return jnp.einsum('bghst,btgd->bsghd', p, v)
        b, s, _ = hidden_states.shape
        sc = cond.shape[1]
        d = qln_w.shape[0]
        nh = wq.shape[0] // d
        g = wk.shape[0] // d
        hpg = nh // g
        ln_out = _ln(hidden_states, ln_w, ln_b)
        q = _fp8_linear_pertensor(ln_out, wq, wq_scale, q_in_scale).reshape(b, s, g, hpg, d)
        q = _ln(q, qln_w, qln_b)
        k = _fp8_linear_pertensor(ln_out, wk, wk_scale, k_in_scale).reshape(b, s, g, d)
        k = _ln(k, kln_w, kln_b)
        v = _fp8_linear_pertensor(ln_out, wv, wv_scale, v_in_scale).reshape(b, s, g, d)
        core = _gqa(q, k, v).reshape(b, s, nh * d)
        qx = _fp8_linear_pertensor(ln_out, wqx, wqx_scale, qx_in_scale).reshape(b, s, g, hpg, d)
        qx = _ln(qx, qxln_w, qxln_b)
        kvx = jnp.einsum('bsi,oi->bso', cond, w_kv_x)
        kx, vx = jnp.split(kvx, 2, axis=-1)
        kx = _ln(kx.reshape(b, sc, g, d), kxln_w, kxln_b)
        vx = vx.reshape(b, sc, g, d)
        xout = _gqa(qx, kx, vx).reshape(b, s, nh * d)
        cat = jnp.concatenate([core, xout], axis=-1)
        catq = _div_clamp_fp8(cat, proj_smooth)
        return jnp.einsum('bsi,oi->bso', catq, wproj) * (proj_in_scale * proj_w_scale)

    def _L0_ffn_ref(x, gate_w, w1, w2, w3):
        import jax, jax.numpy as jnp
        import numpy as np
        HIDDEN = 256
        FFN = 512
        E = 8
        TOP_K = 2
        input_shape = x.shape
        xf = x.reshape(-1, input_shape[-1])
        logits = xf @ gate_w.T
        probs = jax.nn.softmax(logits.astype(jnp.float32), axis=-1)
        weights, selected = jax.lax.top_k(probs, TOP_K)
        weights = weights / weights.sum(axis=-1, keepdims=True)
        weights = weights.astype(x.dtype)
        onehot = jax.nn.one_hot(selected, E, dtype=x.dtype)
        cw = jnp.einsum('tk,tke->te', weights, onehot)
        out = jnp.zeros_like(xf)
        for e in range(E):
            g = jax.nn.silu(xf @ w1[e].T)
            u = xf @ w3[e].T
            y = g * u @ w2[e].T
            out = out + cw[:, e:e + 1] * y
        return out.reshape(input_shape)
    x = x + _L0_xattn_ref(_layernorm(x, axis=-1), ctx_2048, L0_xattn_ln_w, L0_xattn_ln_b, L0_xattn_wq, L0_xattn_wq_scale, L0_xattn_q_in_scale, L0_xattn_wqx, L0_xattn_wqx_scale, L0_xattn_qx_in_scale, L0_xattn_wk, L0_xattn_wk_scale, L0_xattn_k_in_scale, L0_xattn_wv, L0_xattn_wv_scale, L0_xattn_v_in_scale, L0_xattn_w_kv_x, L0_xattn_qln_w, L0_xattn_qln_b, L0_xattn_kln_w, L0_xattn_kln_b, L0_xattn_qxln_w, L0_xattn_qxln_b, L0_xattn_kxln_w, L0_xattn_kxln_b, L0_xattn_wproj, L0_xattn_proj_w_scale, L0_xattn_proj_in_scale, L0_xattn_proj_smooth)
    x = x + _L0_ffn_ref(_layernorm(x, axis=-1), L0_ffn_gate_w, L0_ffn_w1, L0_ffn_w2, L0_ffn_w3)
    return x

_drawn_inputs = setup_inputs


def setup_inputs(seed=0):
    import zlib

    import numpy as np

    out = dict(_drawn_inputs(seed))
    spreads = {'L0_xattn_ln_w': (1.0, 0.6),
     'L0_xattn_ln_b': (0.0, 0.1),
     'L0_xattn_q_in_scale': (0.05000000074505806, 0.6),
     'L0_xattn_qx_in_scale': (0.05000000074505806, 0.6),
     'L0_xattn_k_in_scale': (0.05000000074505806, 0.6),
     'L0_xattn_v_in_scale': (0.05000000074505806, 0.6),
     'L0_xattn_qln_w': (1.0, 0.6),
     'L0_xattn_qln_b': (0.0, 0.8),
     'L0_xattn_kln_w': (1.0, 0.6),
     'L0_xattn_kln_b': (0.0, 0.8),
     'L0_xattn_qxln_w': (1.0, 0.6),
     'L0_xattn_qxln_b': (0.0, 0.8),
     'L0_xattn_kxln_w': (1.0, 0.6),
     'L0_xattn_kxln_b': (0.0, 0.8),
     'L0_xattn_proj_smooth': (0.05000000074505806, 0.2)}
    factors = {'L0_ffn_gate_w': 3.873, 'L0_ffn_w1': 3.401, 'L0_ffn_w2': 3.356, 'L0_ffn_w3': 3.35}
    for name, (base, spread) in spreads.items():
        noise = np.random.default_rng([zlib.crc32(name.encode()), seed]).standard_normal(out[name].shape)
        drawn = base * np.exp(spread * noise) if base else spread * noise
        out[name] = jnp.asarray(drawn.astype(out[name].dtype))
    for name, factor in factors.items():
        out[name] = (out[name] * factor).astype(out[name].dtype)
    return out
```

```python
import numpy as np
import concourse.bass as bass
from concourse import mybir
from collections import namedtuple
from contextlib import ExitStack

B, S, H = 16, 128, 256
D, NH, G = 128, 16, 8
E_, F_ = 8, 512
P = 128
KC = H // P
UH = 4
UG = UH * G // NH
HALF = NH // UH
NU = 2 * HALF
QW, KW = UH * D, UG * D
NL = UH + UG
LW = NL * D
CORE, CROSS = 0, 1
L_NORM, L_QKT, L_SCORE, L_PT, L_HEAD, L_OUT = 1, 2, 3, 4, 5, 6
FC = F_ // P
TB = 4
NTB = B // TB
EPS = 1e-5
FP8_MAX = 448.0
FP8_TINY = 2.0 ** -6
SCORE = float(1.0 / np.sqrt(D))
WS = 16.0

C_LNW, C_LNB, C_IN, C_SMOOTH = 0, KC, 2 * KC, 2 * KC + 4 * KC
C_LN = C_SMOOTH + 2 * NH
C_S = C_LN + 8
NCST = C_S + 6
V_Q, V_K, V_V, V_QX = range(4)


def attention(nc: bass.Bass, h_all, ident, x, ctxT, wunit, wpunit, cst, eye):
    fp32, f16, bf16, u16 = mybir.dt.float32, mybir.dt.float16, mybir.dt.bfloat16, mybir.dt.uint16
    u32 = mybir.dt.uint32
    ALU, ACT, AX = mybir.AluOpType, mybir.ActivationFunctionType, mybir.AxisListType

    with ExitStack() as es:
        def sb(name, shape, dt=fp32):
            return es.enter_context(nc.sbuf_tensor(name, shape, dt))

        def ps(name, shape, dt=fp32):
            return es.enter_context(nc.psum_tensor(name, shape, dt))

        def sem(name):
            return es.enter_context(nc.semaphore(name))

        w_hi = sb("w_hi", [P, NU, KC, QW + 2 * KW], f16)
        w_lo = sb("w_lo", [P, NU, KC, QW + 2 * KW], f16)
        wp_hi = sb("wp_hi", [P, NU, UH, H], f16)
        wp_lo = sb("wp_lo", [P, NU, UH, H], f16)
        c_sb = sb("c_sb", [P, NCST])
        rin = sb("rin", [P, 4 * KC])
        rsm = sb("rsm", [P, 2 * NH])
        ws = sb("ws", [P, 2, NL])
        epsw = sb("epsw", [P, 2, NL])
        neghalf = sb("neghalf", [P, NL])
        psc = sb("psc", [P, 1])
        w_raw = sb("w_raw", [P, 2, KC, QW + 2 * KW])
        wp_raw = sb("wp_raw", [P, 2, UH, H])
        w_sum = sb("w_sum", [P, 2, KC * NL])
        w_mean = sb("w_mean", [P, 2, KC * NL])
        xst = sb("xst", [P, 6])
        xmv = sb("xmv", [P, 2])
        xr = sb("xr", [P, 2])
        xc = sb("xc", [P, H])
        tT = sb("tT", [P, KC, P])
        xy = sb("xy", [P, 3 * KC, P])
        xyb = sb("xyb", [P, 3 * KC, P], bf16)
        xm = sb("xm", [P, 3 * KC, P], bf16)
        xs = sb("xs", [P, 3 * KC, P], bf16)
        xq = sb("xq", [P, 4, KC, P], bf16)
        ctx_raw = sb("ctx_raw", [P, KC, P])
        ctx_hi = sb("ctx_hi", [P, KC, P], f16)
        ctx_lo = sb("ctx_lo", [P, KC, P], f16)
        raw = sb("raw", [P, 2, LW])
        sq = sb("sq", [P, LW])
        ssum = sb("ssum", [P, NL])
        svar = sb("svar", [P, NL])
        sfac = sb("sfac", [P, NL])
        qn = sb("qn", [P, 2, LW])
        vv = sb("vv", [P, NU, KW])
        qkT = sb("qkT", [P, 2, LW])
        smax = sb("smax", [P, 2, UH])
        nmax = sb("nmax", [P, 2, UH])
        esum = sb("esum", [P, 2, UH])
        rinv = sb("rinv", [P, 2, UH])
        pp = sb("pp", [P, 2, UH, P])
        pT = sb("pT", [P, 2, UH, P])
        y32 = sb("y32", [P, 2, UH, P])
        yb = sb("yb", [P, UH * P], bf16)
        ym = sb("ym", [P, UH * P], bf16)
        ya = sb("ya", [P, UH * P], bf16)
        catq = sb("catq", [P, 2, UH * P], bf16)

        ps_q = ps("ps_q", [P, 512])
        ps_kv = ps("ps_kv", [P, 512])
        ps_qT = ps("ps_qT", [P, 512])
        ps_kT = ps("ps_kT", [P, 512])
        ps_s = ps("ps_s", [P, 512])
        ps_pT = ps("ps_pT", [P, 512])
        ps_o = ps("ps_o", [P, 512])
        ps_y = ps("ps_y", [P, 512])

        names = ("half_ok c_in x0_in x_in w_in0 w_in1 ctx_in setup rsm_ok wscaled wsummed wmeaned wcentred w_hi_ok w_lo_ok wp_lo_ok "
                 "xstat xmean xvar xfac xc_ok xT_ok tT_ok xdiv xclip xmask xmagic xadd xq_core xq_cross "
                 "ctx_hi_ok ctx_ok proj copied squared summed var fac normed qkT_ps qkT_ok "
                     "scores maxed negmax exped inverted probs pT_ps pT_ok heads y_ok clipped masked magic added catq_ok "
                     "attn h_ok"
                 ).split()
        s = namedtuple("Semaphores", names)(*[sem(name) for name in names])

        def need(eng, sm, b, k):
            if isinstance(b, int):
                if NU * b + k > 0:
                    eng.wait_ge(sm, NU * b + k)
            else:
                eng.wait_ge(sm, b * NU + k)

        def need_b(eng, sm, b, k=0, per=1):
            if isinstance(b, int):
                if per * (b + k) > 0:
                    eng.wait_ge(sm, per * (b + k))
            else:
                eng.wait_ge(sm, b * per + per * k)

        def live(b, k):
            return not isinstance(b, int) or 0 <= NU * b + k < B * NU

        def batches(eng, slot):
            for u in range(NU):
                slot(0, u)
            with eng.Fori(1, B - 1) as b:
                for u in range(NU):
                    slot(b, u)
            for u in range(NU):
                slot(B - 1, u)
            for u in range(L_OUT + 1):
                slot(B, u)

        block = es.enter_context(nc.Block())

        @block.sync
        def _(sp):
            sp.dma_start(c_sb[:, :], cst[:, :]).then_inc(s.c_in, 16)
            sp.dma_start(ident[:, :], eye[:, :]).then_inc(s.c_in, 16)
            sp.dma_start(h_all[:, 0, :], x[0]).then_inc(s.x0_in, 16)
            for u in range(NU):
                if u >= 2:
                    sp.wait_ge(s.w_lo_ok, u - 1)
                    sp.wait_ge(s.wp_lo_ok, u - 1)
                w_in = (s.w_in0, s.w_in1)[u % 2]
                sp.dma_start(w_raw[:, u % 2, :, :], wunit[u]).then_inc(w_in, 16)
                sp.dma_start(wp_raw[:, u % 2, :, :], wpunit[u]).then_inc(w_in, 16)
                if u == 0:
                    sp.dma_start(ctx_raw[:, :, :], ctxT[0]).then_inc(s.ctx_in, 16)
                    sp.dma_start(h_all[:, 1:, :], x[1:].rearrange("b p i -> p b i")).then_inc(s.x_in, 16)
            with sp.Fori(1, B) as b:
                sp.wait_ge(s.ctx_ok, b)
                sp.dma_start(ctx_raw[:, :, :], ctxT[b]).then_inc(s.ctx_in, 16)

        @block.tensor
        def _(pe):
            def input_transposed(bx):
                need_b(pe, s.xc_ok, bx, 1)
                for c in range(KC):
                    last = nc.tensor.transpose(ps_kT[:, KW + c * P:KW + (c + 1) * P], xc[:, c * P:(c + 1) * P], ident[:, :])
                last.then_inc(s.xT_ok, 1)

            def slot(b, u):
                k = u - L_SCORE
                if live(b, k):
                    need(pe, s.qkT_ok, b, k + 1)
                    need(pe, s.exped, b, k)
                    for j in range(UH):
                        kv = QW + (j // (UH // UG)) * D
                        last = nc.tensor.matmul(ps_s[:, j * P:(j + 1) * P], qkT[:, k % 2, j * P:(j + 1) * P],
                                                qkT[:, k % 2, kv:kv + P], start=True, stop=True)
                    last.then_inc(s.scores, 1)
                if live(b, u):
                    if isinstance(b, int) and b == 0:
                        pe.wait_ge(s.w_hi_ok, u + 1)
                        pe.wait_ge(s.w_lo_ok, u + 1)
                        pe.wait_ge(s.wp_lo_ok, u + 1)
                    if u == 0:
                        need_b(pe, s.xq_core, b, 1)
                    if u == HALF:
                        need_b(pe, s.xq_cross, b, 1)
                        need_b(pe, s.ctx_ok, b, 1)
                    need(pe, s.copied, b, u)
                    cross = u >= HALF
                    def project(dst, version, lo, w):
                        for c in range(KC):
                            for half, wt in enumerate((w_hi, w_lo)):
                                last = nc.tensor.matmul(dst, xq[:, version, c, :], wt[:, u, c, lo:lo + w],
                                                        start=(c == 0 and half == 0), stop=(c == KC - 1 and half == 1))
                        return last
                    last = project(ps_q[:, :], V_QX if cross else V_Q, 0, QW)
                    if not cross:
                        project(ps_kv[:, 0:KW], V_K, QW, KW)
                        last = project(ps_kv[:, KW:2 * KW], V_V, QW + KW, KW)
                    else:
                        for c in range(KC):
                            for i, (a, w) in enumerate(((ctx_hi, w_hi), (ctx_hi, w_lo), (ctx_lo, w_hi))):
                                last = nc.tensor.matmul(ps_kv[:, :], a[:, c, :], w[:, u, c, QW:QW + 2 * KW],
                                                        start=(c == 0 and i == 0), stop=(c == KC - 1 and i == 2))
                    last.then_inc(s.proj, 1)
                k = u - L_PT
                if live(b, k):
                    need(pe, s.probs, b, k + 1)
                    need(pe, s.pT_ok, b, k)
                    for j in range(UH):
                        last = nc.tensor.transpose(ps_pT[:, j * P:(j + 1) * P], pp[:, k % 2, j, :], ident[:, :])
                    last.then_inc(s.pT_ps, 1)
                k = u - L_QKT
                if live(b, k):
                    need(pe, s.normed, b, k + 1)
                    need(pe, s.qkT_ok, b, k)
                    if u == 2 and live(b, 0):
                        need_b(pe, s.tT_ok, b, 1)
                    if u == 3 and live(b, NU):
                        need_b(pe, s.tT_ok, b, 2)
                    if u == 2 and live(b, NU):
                        input_transposed(b + 1)
                    for j in range(NL):
                        dst = ps_qT[:, j * P:(j + 1) * P] if j < UH else ps_kT[:, (j - UH) * P:(j - UH + 1) * P]
                        last = nc.tensor.transpose(dst, qn[:, k % 2, j * P:(j + 1) * P], ident[:, :])
                    last.then_inc(s.qkT_ps, 1)
                k = u - L_HEAD
                if live(b, k):
                    need(pe, s.pT_ok, b, k + 1)
                    need(pe, s.copied, b, k + 1)
                    need(pe, s.y_ok, b, k)
                    per = UH // UG
                    for g in range(UG):
                        last = nc.tensor.matmul(ps_o[:, g * per * P:(g + 1) * per * P], vv[:, k % NU, g * D:(g + 1) * D],
                                                pT[:, k % 2, g * per:(g + 1) * per, :], start=True, stop=True)
                    last.then_inc(s.heads, 1)
                k = u - L_OUT
                if live(b, k):
                    uu = k % NU
                    need(pe, s.catq_ok, b, k + 1)
                    if uu == 0:
                        need_b(pe, s.h_ok, b, 0)
                    for j in range(UH):
                        for half, wt in enumerate((wp_hi, wp_lo)):
                            last = nc.tensor.matmul(ps_y[:, 0:H], catq[:, k % 2, j * P:(j + 1) * P], wt[:, uu, j, :],
                                                    start=(uu == 0 and j == 0 and half == 0),
                                                    stop=(uu == NU - 1 and j == UH - 1 and half == 1))
                    last.then_inc(s.attn, 1)

            pe.wait_ge(s.c_in, 32)
            input_transposed(0)
            batches(pe, slot)

        @block.scalar
        def _(act):
            def col(i):
                return c_sb[:, i:i + 1]

            def input_evacuated(bx):
                need_b(act, s.xT_ok, bx, 1)
                need_b(act, s.xq_cross, bx, 0)
                for c in range(KC):
                    last = nc.scalar.activation(tT[:, c, :], ps_kT[:, KW + c * P:KW + (c + 1) * P], ACT.Identity,
                                                bias=col(C_LNB + c), scale=col(C_LNW + c))
                last.then_inc(s.tT_ok, 1)

            def high_parts(u):
                act.wait_ge(s.wcentred, u + 1)
                nc.scalar.activation(wp_hi[:, u, :, :], wp_raw[:, u % 2, :, :], ACT.Copy)
                nc.scalar.activation(w_hi[:, u, :, :], w_raw[:, u % 2, :, :], ACT.Copy).then_inc(s.w_hi_ok, 1)

            def slot(b, u):
                if isinstance(b, int) and b == 0 and u + 1 < NU:
                    high_parts(u + 1)
                if u == 1 and live(b, 0):
                    need_b(act, s.ctx_in, b, 1, 16)
                    need(act, s.proj, b, 0)
                    nc.scalar.activation(ctx_hi[:, :, :], ctx_raw[:, :, :], ACT.Copy).then_inc(s.ctx_hi_ok, 1)
                k = u - L_SCORE
                if live(b, k):
                    need(act, s.negmax, b, k + 1)
                    need(act, s.pT_ps, b, k - 1)
                    for j in range(UH):
                        last = nc.scalar.activation(pp[:, k % 2, j, :], ps_s[:, j * P:(j + 1) * P], ACT.Exp,
                                                    bias=nmax[:, k % 2, j:j + 1], scale=SCORE,
                                                    accum_out=esum[:, k % 2, j:j + 1])
                    last.then_inc(s.exped, 1)
                if live(b, u):
                    need(act, s.proj, b, u + 1)
                    need(act, s.normed, b, u - 1)
                    need(act, s.squared, b, u - 1)
                    need(act, s.heads, b, u - NU + 1)
                    nc.scalar.activation(raw[:, u % 2, 0:QW], ps_q[:, :], ACT.Copy)
                    nc.scalar.activation(raw[:, u % 2, QW:LW], ps_kv[:, 0:KW], ACT.Copy)
                    nc.scalar.activation(vv[:, u, :], ps_kv[:, KW:2 * KW], ACT.Copy).then_inc(s.copied, 1)
                k = u - L_PT
                if live(b, k):
                    need(act, s.pT_ps, b, k + 1)
                    need(act, s.heads, b, k - 1)
                    nc.scalar.activation(pT[:, k % 2, :, :], ps_pT[:, :], ACT.Copy).then_inc(s.pT_ok, 1)
                k = u - L_QKT
                if live(b, k):
                    o = C_LN + 4 * (1 if k % NU >= HALF else 0)
                    need(act, s.qkT_ps, b, k + 1)
                    need(act, s.scores, b, k - 1)
                    nc.scalar.activation(qkT[:, k % 2, 0:QW], ps_qT[:, :], ACT.Identity, bias=col(o + 1), scale=col(o))
                    nc.scalar.activation(qkT[:, k % 2, QW:LW], ps_kT[:, 0:KW], ACT.Identity, bias=col(o + 3),
                                         scale=col(o + 2)).then_inc(s.qkT_ok, 1)
                    if u == 2 and live(b, NU):
                        input_evacuated(b + 1)
                k = u - L_HEAD
                if live(b, k):
                    need(act, s.heads, b, k + 1)
                    need(act, s.clipped, b, k - 1)
                    for j in range(UH):
                        h = (k % NU) * UH + j
                        last = nc.scalar.activation(y32[:, k % 2, j, :], ps_o[:, j * P:(j + 1) * P], ACT.Copy,
                                                    scale=rsm[:, h:h + 1])
                    last.then_inc(s.y_ok, 1)

            act.wait_ge(s.c_in, 32)
            act.wait_ge(s.rsm_ok, 2)
            input_evacuated(0)
            high_parts(0)
            batches(act, slot)

        @block.vector
        def _(dve):
            def scaled(dst, src, col_, **kw):
                return nc.vector.tensor_scalar(dst, src, col_, None, ALU.mult, **kw)

            def col(i):
                return c_sb[:, i:i + 1]

            def weights(u):
                i = u % 2
                dve.wait_ge((s.w_in0, s.w_in1)[i], 32 * (u // 2 + 1))
                cross = u >= HALF
                parts = [(V_QX, 0, QW)] if cross else [(V_Q, 0, QW), (V_K, QW, KW), (V_V, QW + KW, KW)]
                for v, lo, w in parts:
                    for c in range(KC):
                        last = scaled(w_raw[:, i, c, lo:lo + w], w_raw[:, i, c, lo:lo + w], col(C_IN + v * KC + c))
                last.then_inc(s.wscaled, 1)
                dve.wait_ge(s.wscaled, u + 1)
                for c in range(KC):
                    last = nc.vector.tensor_reduce(w_sum[:, i, c * NL:(c + 1) * NL],
                                                   w_raw[:, i, c, 0:LW].rearrange("p (h d) -> p h d", d=D), AX.X, ALU.add)
                last.then_inc(s.wsummed, 1)
                dve.wait_ge(s.wsummed, u + 1)
                if u >= 2:
                    dve.wait_ge(s.wcentred, u - 1)
                nc.vector.tensor_scalar(w_mean[:, i, :], w_sum[:, i, :], 1.0 / D, None, ALU.mult).then_inc(s.wmeaned, 1)

            def low_parts(u):
                dve.wait_ge(s.w_hi_ok, u + 1)
                nc.vector.tensor_tensor(w_lo[:, u, :, :], w_raw[:, u % 2, :, :], w_hi[:, u, :, :], ALU.subtract).then_inc(s.w_lo_ok, 1)

            def input_normalised(bx):
                dve.wait_ge(s.x0_in if isinstance(bx, int) and bx == 0 else s.x_in, 16)
                row = h_all[:, bx, :]
                nc.vector.bn_stats(xst[:, :], row).then_inc(s.xstat, 1)
                need_b(dve, s.xstat, bx, 1)
                nc.vector.memset(xr[:, 0:1], 0.0)
                nc.vector.bn_aggr(xmv[:, :], xst[:, :]).then_inc(s.xmean, 1)
                need_b(dve, s.xmean, bx, 1)
                nc.vector.tensor_scalar(xr[:, 0:1], xmv[:, 1:2], 1.0 + EPS, EPS * EPS, ALU.mult, ALU.add).then_inc(s.xvar, 1)
                need_b(dve, s.xfac, bx, 1)
                need_b(dve, s.xT_ok, bx, 0)
                nc.vector.tensor_scalar(xc[:, :], row, xmv[:, 0:1], xr[:, 1:2], ALU.subtract, ALU.mult).then_inc(s.xc_ok, 1)

            def input_quantised(bx, versions, done):
                n = len(versions) * KC
                odd = 0 if done is s.xq_core else 1
                need_b(dve, s.tT_ok, bx, 1)
                nv, v = len(versions), versions[0]
                scales = rin[:, v * KC:(v + nv) * KC].rearrange("p (v c) -> p v c", c=KC)
                nc.vector.tensor_tensor(xy[:, 0:n, :].rearrange("p (v c) s -> p v c s", c=KC),
                                        tT[:, :, :].unsqueeze(1).to_broadcast([P, nv, KC, P]),
                                        scales.unsqueeze(3).to_broadcast([P, nv, KC, P]), ALU.mult).then_inc(s.xdiv, 1)

                def step(sm):
                    if isinstance(bx, int):
                        dve.wait_ge(sm, 2 * bx + odd + 1)
                    else:
                        dve.wait_ge(sm, bx * 2 + (odd + 1))
                step(s.xdiv)
                nc.vector.tensor_scalar(xyb[:, 0:n, :], xy[:, 0:n, :], FP8_MAX, -FP8_MAX, ALU.min, ALU.max).then_inc(s.xclip, 1)
                step(s.xclip)
                nc.vector.tensor_scalar(xm[:, 0:n, :].bitcast(u16), xyb[:, 0:n, :].bitcast(u16), 0x7F80, None,
                                        ALU.bitwise_and).then_inc(s.xmask, 1)
                step(s.xmask)
                nc.vector.tensor_scalar(xm[:, 0:n, :], xm[:, 0:n, :], FP8_TINY, 24.0, ALU.max, ALU.mult).then_inc(s.xmagic, 1)
                step(s.xmagic)
                nc.vector.tensor_tensor(xs[:, 0:n, :], xyb[:, 0:n, :], xm[:, 0:n, :], ALU.add).then_inc(s.xadd, 1)
                step(s.xadd)
                if done is s.xq_core:
                    need(dve, s.proj, bx, HALF - NU)
                    dst = xq[:, 0:3, :, :]
                else:
                    need(dve, s.proj, bx, 0)
                    dst = xq[:, 3:4, :, :]
                dst = dst.rearrange("p v c s -> p (v c) s")
                nc.vector.tensor_tensor(dst, xs[:, 0:n, :], xm[:, 0:n, :], ALU.subtract).then_inc(done, 1)

            def slot(b, u):
                if isinstance(b, int) and b == 0:
                    if u + 1 < NU:
                        low_parts(u + 1)
                    if u + 2 < NU:
                        weights(u + 2)
                k = u - L_SCORE
                if live(b, k):
                    need(dve, s.scores, b, k + 1)
                    nc.vector.tensor_reduce(smax[:, k % 2, :], ps_s[:, :].rearrange("p (h t) -> p h t", t=P), AX.X,
                                            ALU.max).then_inc(s.maxed, 1)
                    need(dve, s.maxed, b, k + 1)
                    need(dve, s.exped, b, k - 1)
                    nc.vector.tensor_scalar(nmax[:, k % 2, :], smax[:, k % 2, :], -SCORE, None, ALU.mult).then_inc(s.negmax, 1)
                if u == (L_OUT + NU) % NU and not (isinstance(b, int) and b == 0):
                    need(dve, s.attn, b, 0)
                    row = h_all[:, b - 1, :]
                    nc.vector.scalar_tensor_tensor(out=row, in0=ps_y[:, 0:H], scalar=psc[:, :], in1=row,
                                                   op0=ALU.mult, op1=ALU.add).then_inc(s.h_ok, 1)
                k = u - L_OUT
                if live(b, k):
                    need(dve, s.y_ok, b, k + 1)
                    nc.vector.tensor_scalar(yb[:, :], y32[:, k % 2, :, :].rearrange("p h t -> p (h t)"), FP8_MAX, -FP8_MAX,
                                            ALU.min, ALU.max).then_inc(s.clipped, 1)
                    need(dve, s.clipped, b, k + 1)
                    nc.vector.tensor_scalar(ym[:, :].bitcast(u16), yb[:, :].bitcast(u16), 0x7F80, None,
                                            ALU.bitwise_and).then_inc(s.masked, 1)
                    need(dve, s.masked, b, k + 1)
                    nc.vector.tensor_scalar(ym[:, :], ym[:, :], FP8_TINY, 24.0, ALU.max, ALU.mult).then_inc(s.magic, 1)
                    need(dve, s.magic, b, k + 1)
                    nc.vector.tensor_tensor(ya[:, :], yb[:, :], ym[:, :], ALU.add).then_inc(s.added, 1)
                    need(dve, s.added, b, k + 1)
                    need(dve, s.attn, b, k - 1)
                    nc.vector.tensor_tensor(catq[:, k % 2, :], ya[:, :], ym[:, :], ALU.subtract).then_inc(s.catq_ok, 1)
                kn = u - L_NORM
                kind = CROSS if kn % NU >= HALF else CORE
                if live(b, kn):
                    need(dve, s.squared, b, kn + 1)
                    nc.vector.tensor_reduce(ssum[:, :], sq[:, :].rearrange("p (h d) -> p h d", d=D), AX.X,
                                            ALU.add).then_inc(s.summed, 1)
                    need(dve, s.summed, b, kn + 1)
                    need(dve, s.fac, b, kn)
                    nc.vector.scalar_tensor_tensor(out=svar[:, :], in0=ssum[:, :], scalar=1.0 / D, in1=epsw[:, kind, :],
                                                   op0=ALU.mult, op1=ALU.add).then_inc(s.var, 1)
                k = u - L_SCORE
                if live(b, k):
                    need(dve, s.exped, b, k + 1)
                    need(dve, s.probs, b, k - 1)
                    nc.vector.reciprocal(rinv[:, k % 2, :], esum[:, k % 2, :]).then_inc(s.inverted, 1)
                if live(b, kn):
                    need(dve, s.fac, b, kn + 1)
                    need(dve, s.qkT_ps, b, kn - 1)
                    nc.vector.tensor_tensor(qn[:, kn % 2, :].rearrange("p (h d) -> p h d", d=D),
                                            raw[:, kn % 2, :].rearrange("p (h d) -> p h d", d=D),
                                            sfac[:, :].unsqueeze(2).to_broadcast([P, NL, D]), ALU.mult).then_inc(s.normed, 1)
                if u == 1 and live(b, 0):
                    input_quantised(b, [V_QX], s.xq_cross)
                    if live(b, NU):
                        input_normalised(b + 1)
                if u == 5 and live(b, NU):
                    input_quantised(b + 1, [V_Q, V_K, V_V], s.xq_core)

            dve.wait_ge(s.c_in, 32)
            nc.vector.reciprocal(rsm[:, :], c_sb[:, C_SMOOTH:C_SMOOTH + 2 * NH])
            nc.vector.reciprocal(rin[:, :], c_sb[:, C_IN:C_IN + 4 * KC])
            nc.vector.tensor_tensor(psc[:, :], col(C_S + 4), col(C_S + 5), ALU.mult)
            nc.vector.memset(ws[:, CROSS, UH:NL], 1.0)
            for kind, lo, n, c in ((CORE, 0, UH, C_S), (CORE, UH, UG, C_S + 1), (CROSS, 0, UH, C_S + 3)):
                last = nc.vector.tensor_copy(ws[:, kind, lo:lo + n], col(c).to_broadcast([P, n]))
            last.then_inc(s.rsm_ok, 1)
            dve.wait_ge(s.rsm_ok, 1)
            nc.vector.tensor_scalar(rsm[:, 0:NH], rsm[:, 0:NH], col(C_S + 2), None, ALU.mult).then_inc(s.rsm_ok, 1)
            nc.vector.tensor_tensor(epsw[:, :, :], ws[:, :, :], ws[:, :, :], ALU.mult).then_inc(s.setup, 1)
            dve.wait_ge(s.setup, 1)
            nc.vector.reciprocal(epsw[:, :, :], epsw[:, :, :]).then_inc(s.setup, 1)
            dve.wait_ge(s.setup, 2)
            nc.vector.tensor_scalar(epsw[:, :, :], epsw[:, :, :], EPS, None, ALU.mult).then_inc(s.setup, 1)
            dve.wait_ge(s.setup, 3)
            input_normalised(0)
            weights(0)
            weights(1)
            input_quantised(0, [V_Q, V_K, V_V], s.xq_core)
            low_parts(0)
            batches(dve, slot)

        @block.gpsimd
        def _(pool):
            def input_factor(bx):
                need_b(pool, s.xvar, bx, 1)
                nc.gpsimd.tensor_tensor(xr[:, 1:2], xr[:, 0:1], neghalf[:, 0:1], ALU.pow).then_inc(s.xfac, 1)

            def centred(u):
                pool.wait_ge(s.wmeaned, u + 1)
                for c in range(KC):
                    v = w_raw[:, u % 2, c, 0:LW].rearrange("p (h d) -> p h d", d=D)
                    m = w_mean[:, u % 2, c * NL:(c + 1) * NL].unsqueeze(2).to_broadcast([P, NL, D])
                    last = nc.gpsimd.tensor_tensor(v, v, m, ALU.subtract)
                last.then_inc(s.wcentred, 1)

            def low_parts(u):
                pool.wait_ge(s.w_hi_ok, u + 1)
                nc.gpsimd.tensor_tensor(wp_lo[:, u, :, :], wp_raw[:, u % 2, :, :], wp_hi[:, u, :, :], ALU.subtract).then_inc(s.wp_lo_ok, 1)

            def slot(b, u):
                if isinstance(b, int) and b == 0:
                    if u + 1 < NU:
                        low_parts(u + 1)
                    if u + 2 < NU:
                        centred(u + 2)
                k = u - L_NORM
                if live(b, k):
                    need(pool, s.var, b, k + 1)
                    need(pool, s.normed, b, k)
                    nc.gpsimd.tensor_tensor(sfac[:, :], svar[:, :], neghalf[:, :], ALU.pow).then_inc(s.fac, 1)
                if u == 1 and live(b, NU):
                    input_factor(b + 1)
                if u == 1 and live(b, 0):
                    need_b(pool, s.ctx_hi_ok, b, 1)
                    nc.gpsimd.tensor_tensor(ctx_lo[:, :, :], ctx_raw[:, :, :], ctx_hi[:, :, :], ALU.subtract).then_inc(s.ctx_ok, 1)
                k = u - L_SCORE
                if live(b, k):
                    need(pool, s.inverted, b, k + 1)
                    need(pool, s.exped, b, k + 1)
                    nc.gpsimd.tensor_tensor(pp[:, k % 2, :, :], pp[:, k % 2, :, :],
                                            rinv[:, k % 2, :].unsqueeze(2).to_broadcast([P, UH, P]),
                                            ALU.mult).then_inc(s.probs, 1)
                if live(b, u):
                    need(pool, s.copied, b, u + 1)
                    need(pool, s.summed, b, u)
                    nc.gpsimd.tensor_tensor(sq[:, :], raw[:, u % 2, :], raw[:, u % 2, :], ALU.mult).then_inc(s.squared, 1)

            nc.gpsimd.memset(neghalf[:, :], -0.5).then_inc(s.half_ok, 1)
            pool.wait_ge(s.half_ok, 1)
            input_factor(0)
            centred(0)
            centred(1)
            low_parts(0)
            batches(pool, slot)


def experts(nc: bass.Bass, h_all, ident, wexp, gateT, iota, out):
    fp32, f16, u32 = mybir.dt.float32, mybir.dt.float16, mybir.dt.uint32
    ALU, ACT, AX = mybir.AluOpType, mybir.ActivationFunctionType, mybir.AxisListType
    WE = 2 * KC * F_ + FC * H
    O1, O3, O2 = 0, KC * F_, 2 * KC * F_
    TN = TB * S

    with ExitStack() as es:
        def sb(name, shape, dt=fp32):
            return es.enter_context(nc.sbuf_tensor(name, shape, dt))

        def ps(name, shape, dt=fp32):
            return es.enter_context(nc.psum_tensor(name, shape, dt))

        st = sb("f_st", [P, B, 6])
        mv = sb("f_mv", [P, B, 2])
        var = sb("f_var", [P, B])
        rs = sb("f_rs", [P, B])
        negh = sb("f_negh", [P, B])
        x2 = sb("f_x2", [P, 2, H])
        xT_hi = sb("f_xT_hi", [P, KC, B * S], f16)
        xT_lo = sb("f_xT_lo", [P, KC, B * S], f16)
        g_raw = sb("f_g_raw", [P, KC, E_])
        g_hi = sb("f_g_hi", [P, KC, E_], f16)
        g_lo = sb("f_g_lo", [P, KC, E_], f16)
        ids = sb("f_ids", [P, E_])
        logit = sb("f_logit", [P, B, E_])
        top = sb("f_top", [P, B, 8])
        topi = sb("f_topi", [P, B, 8], u32)
        topf = sb("f_topf", [P, B, 8])
        dl = sb("f_dl", [P, B])
        ed = sb("f_ed", [P, B])
        p1 = sb("f_p1", [P, B])
        p2 = sb("f_p2", [P, B])
        den = sb("f_den", [P, B])
        m1 = sb("f_m1", [P, B, E_])
        m2 = sb("f_m2", [P, B, E_])
        cw = sb("f_cw", [P, B, E_])
        e_raw = sb("e_raw", [P, 2, WE])
        e_hi = sb("e_hi", [P, 2, WE], f16)
        e_lo = sb("e_lo", [P, 2, WE], f16)
        sg = sb("f_sg", [P, 2, TN])
        hf = sb("f_hf", [P, 2, TN])
        hT_hi = sb("f_hT_hi", [P, 2, FC, TN], f16)
        hT_lo = sb("f_hT_lo", [P, 2, FC, TN], f16)
        ps_x = [ps("f_ps_x0", [P, 512]), ps("f_ps_x1", [P, 512])]
        ps_g = [ps("f_ps_g0", [P, TN]), ps("f_ps_g1", [P, TN])]
        ps_u = [ps("f_ps_u0", [P, TN]), ps("f_ps_u1", [P, TN])]
        ps_d = [ps("f_ps_d0", [P, 512]), ps("f_ps_d1", [P, 512])]

        names = ("g_in e_in0 e_in1 half st mv var rs x2_ok xT_ps hi_ok lo_ok ghi glo gates logit_ok top1 top2 topf_ok dl_ok ed_ok "
                     "den_ok p1_ok p2_ok m1_ok m2_ok n1_ok n2_ok cw_ok ehi elo g_ok u_ok silu hf_ok hhi hlo down acc stored").split()
        s = namedtuple("Semaphores", names)(*[es.enter_context(nc.semaphore("f_" + name)) for name in names])

        block = es.enter_context(nc.Block())
        NF = E_ * NTB * FC

        @block.sync
        def _(sp):
            sp.dma_start(g_raw[:, :, :], gateT[:, :, :]).then_inc(s.g_in, 16)
            sp.dma_start(ids[:, :], iota[:, :]).then_inc(s.g_in, 16)
            for e in range(E_):
                if e >= 2:
                    sp.wait_ge(s.elo, e - 1)
                    sp.wait_ge(s.ehi, e - 1)
                sp.dma_start(e_raw[:, e % 2, :], wexp[e]).then_inc((s.e_in0, s.e_in1)[e % 2], 16)
            for t in range(B):
                sp.wait_ge(s.acc, (E_ - 1) * B + t + 1)
                sp.dma_start(out[t], h_all[:, t, :]).then_inc(s.stored, 16)
            sp.wait_ge(s.stored, 16 * B)

        @block.gpsimd
        def _(pool):
            nc.gpsimd.memset(negh[:, :], -0.5).then_inc(s.half, 1)
            pool.wait_ge(s.half, 1)
            pool.wait_ge(s.var, 1)
            nc.gpsimd.tensor_tensor(rs[:, :], var[:, :], negh[:, :], ALU.pow).then_inc(s.rs, 1)

        @block.tensor
        def _(pe):
            for t in range(B):
                pe.wait_ge(s.x2_ok, t + 1)
                if t >= 2:
                    pe.wait_ge(s.lo_ok, t - 1)
                for c in range(KC):
                    last = nc.tensor.transpose(ps_x[t % 2][:, c * P:(c + 1) * P], x2[:, t % 2, c * P:(c + 1) * P], ident[:, :])
                last.then_inc(s.xT_ps, 1)
            pe.wait_ge(s.glo, 1)
            pe.wait_ge(s.ghi, 1)
            pe.wait_ge(s.lo_ok, B)
            for t in range(B):
                for c in range(KC):
                    for i, (a, w) in enumerate(((xT_hi, g_hi), (xT_hi, g_lo), (xT_lo, g_hi))):
                        last = nc.tensor.matmul(ps_g[0][:, t * E_:(t + 1) * E_], a[:, c, t * P:(t + 1) * P], w[:, c, :],
                                                start=(c == 0 and i == 0), stop=(c == KC - 1 and i == 2))
            last.then_inc(s.gates, 1)
            pe.wait_ge(s.logit_ok, 1)

            def down(e, tb):
                n = e * NTB + tb
                pe.wait_ge(s.hlo, (n + 1) * FC)
                pe.wait_ge(s.hhi, (n + 1) * FC)
                for j in range(TB):
                    i = n * TB + j
                    if i >= 2:
                        pe.wait_ge(s.acc, i - 1)
                    for f in range(FC):
                        for q, (a, w) in enumerate(((hT_hi, e_hi), (hT_hi, e_lo), (hT_lo, e_hi))):
                            last = nc.tensor.matmul(ps_d[j % 2][:, 0:H], a[:, tb % 2, f, j * P:(j + 1) * P],
                                                    w[:, e % 2, O2 + f * H:O2 + (f + 1) * H],
                                                    start=(f == 0 and q == 0), stop=(f == FC - 1 and q == 2))
                    last.then_inc(s.down, 1)

            prev = None
            for e in range(E_):
                pe.wait_ge(s.ehi, e + 1)
                pe.wait_ge(s.elo, e + 1)
                for tb in range(NTB):
                    for f in range(FC):
                        n = (e * NTB + tb) * FC + f
                        if n >= 2:
                            pe.wait_ge(s.hf_ok, n - 1)
                        for o, bank, done in ((O1, ps_g, s.g_ok), (O3, ps_u, s.u_ok)):
                            for c in range(KC):
                                for q, (w, a) in enumerate(((e_hi, xT_hi), (e_hi, xT_lo), (e_lo, xT_hi))):
                                    last = nc.tensor.matmul(bank[n % 2][:, :], w[:, e % 2, o + c * F_ + f * P:o + c * F_ + (f + 1) * P],
                                                            a[:, c, tb * TN:(tb + 1) * TN],
                                                            start=(c == 0 and q == 0), stop=(c == KC - 1 and q == 2))
                            last.then_inc(done, 1)
                    if prev:
                        down(*prev)
                    prev = (e, tb)
            down(*prev)

        @block.scalar
        def _(act):
            act.wait_ge(s.g_in, 32)
            nc.scalar.activation(g_hi[:, :, :], g_raw[:, :, :], ACT.Copy, scale=WS).then_inc(s.ghi, 1)
            for t in range(B):
                act.wait_ge(s.xT_ps, t + 1)
                nc.scalar.activation(xT_hi[:, :, t * P:(t + 1) * P], ps_x[t % 2][:, 0:H].rearrange("p (c s) -> p c s", c=KC),
                                     ACT.Copy).then_inc(s.hi_ok, 1)
            act.wait_ge(s.dl_ok, 1)
            nc.scalar.activation(ed[:, :], dl[:, :], ACT.Exp).then_inc(s.ed_ok, 1)

            def high(e):
                act.wait_ge((s.e_in0, s.e_in1)[e % 2], 16 * (e // 2 + 1))
                if e >= 2:
                    act.wait_ge(s.down, (e - 1) * B)
                nc.scalar.activation(e_hi[:, e % 2, :], e_raw[:, e % 2, :], ACT.Copy, scale=WS).then_inc(s.ehi, 1)

            high(0)
            for e in range(E_):
                for tb in range(NTB):
                    for f in range(FC):
                        n = (e * NTB + tb) * FC + f
                        act.wait_ge(s.g_ok, n + 1)
                        if n >= 2:
                            act.wait_ge(s.hf_ok, n - 1)
                        nc.scalar.activation(sg[:, n % 2, :], ps_g[n % 2][:, :], ACT.Silu, scale=1.0 / WS).then_inc(s.silu, 1)
                        act.wait_ge(s.hf_ok, n + 1)
                        if n >= 2 * FC:
                            act.wait_ge(s.down, (n // FC - 1) * TB)
                        nc.scalar.activation(hT_hi[:, tb % 2, f, :], hf[:, n % 2, :], ACT.Copy).then_inc(s.hhi, 1)
                    if tb == 0 and e + 1 < E_:
                        high(e + 1)

        @block.vector
        def _(dve):
            for t in range(B):
                last = nc.vector.bn_stats(st[:, t, :], h_all[:, t, :])
            last.then_inc(s.st, 1)
            dve.wait_ge(s.st, 1)
            for t in range(B):
                last = nc.vector.bn_aggr(mv[:, t, :], st[:, t, :])
            last.then_inc(s.mv, 1)
            dve.wait_ge(s.mv, 1)
            nc.vector.tensor_scalar(var[:, :], mv[:, :, 1], EPS, None, ALU.add).then_inc(s.var, 1)
            dve.wait_ge(s.g_in, 32)
            dve.wait_ge(s.ghi, 1)
            nc.vector.scalar_tensor_tensor(out=g_lo[:, :, :], in0=g_raw[:, :, :], scalar=WS, in1=g_hi[:, :, :],
                                           op0=ALU.mult, op1=ALU.subtract).then_inc(s.glo, 1)
            dve.wait_ge(s.rs, 1)

            def low(t):
                dve.wait_ge(s.hi_ok, t + 1)
                nc.vector.tensor_tensor(xT_lo[:, :, t * P:(t + 1) * P], ps_x[t % 2][:, 0:H].rearrange("p (c s) -> p c s", c=KC),
                                        xT_hi[:, :, t * P:(t + 1) * P], ALU.subtract).then_inc(s.lo_ok, 1)
            for t in range(B):
                if t >= 2:
                    dve.wait_ge(s.xT_ps, t - 1)
                nc.vector.tensor_scalar(x2[:, t % 2, :], h_all[:, t, :], mv[:, t, 0:1], rs[:, t:t + 1],
                                        ALU.subtract, ALU.mult).then_inc(s.x2_ok, 1)
                if t >= 1:
                    low(t - 1)
            low(B - 1)
            dve.wait_ge(s.gates, 1)
            nc.vector.tensor_scalar(logit[:, :, :].rearrange("p t e -> p (t e)"), ps_g[0][:, 0:B * E_], 1.0 / WS, None,
                                    ALU.mult).then_inc(s.logit_ok, 1)
            dve.wait_ge(s.logit_ok, 1)
            for t in range(B):
                last = nc.vector.max(top[:, t, :], logit[:, t, :])
            last.then_inc(s.top1, 1)
            dve.wait_ge(s.top1, 1)
            nc.vector.tensor_tensor(dl[:, :], top[:, :, 1], top[:, :, 0], ALU.subtract).then_inc(s.dl_ok, 1)
            for t in range(B):
                last = nc.vector.max_index(topi[:, t, :], top[:, t, :], logit[:, t, :])
            last.then_inc(s.top2, 1)
            dve.wait_ge(s.top2, 1)
            nc.vector.tensor_copy(topf[:, :, :], topi[:, :, :]).then_inc(s.topf_ok, 1)
            dve.wait_ge(s.ed_ok, 1)
            nc.vector.tensor_scalar(den[:, :], ed[:, :], 1.0, None, ALU.add).then_inc(s.den_ok, 1)
            dve.wait_ge(s.den_ok, 1)
            nc.vector.reciprocal(p1[:, :], den[:, :]).then_inc(s.p1_ok, 1)
            dve.wait_ge(s.p1_ok, 1)
            nc.vector.tensor_tensor(p2[:, :], p1[:, :], ed[:, :], ALU.mult).then_inc(s.p2_ok, 1)
            dve.wait_ge(s.topf_ok, 1)
            dve.wait_ge(s.p2_ok, 1)
            shape = [P, B, E_]
            ids_b = ids[:, :].unsqueeze(1).to_broadcast(shape)
            for m, i, pr, sa, sb_ in ((m1, 0, p1, s.m1_ok, s.n1_ok), (m2, 1, p2, s.m2_ok, s.n2_ok)):
                nc.vector.tensor_tensor(m[:, :, :], topf[:, :, i:i + 1].to_broadcast(shape), ids_b, ALU.is_equal).then_inc(sa, 1)
                dve.wait_ge(sa, 1)
                nc.vector.tensor_tensor(m[:, :, :], m[:, :, :], pr[:, :].unsqueeze(2).to_broadcast(shape), ALU.mult).then_inc(sb_, 1)
                dve.wait_ge(sb_, 1)
            nc.vector.tensor_tensor(m1[:, :, :], m1[:, :, :], m2[:, :, :], ALU.add).then_inc(s.m1_ok, 1)
            dve.wait_ge(s.m1_ok, 2)
            nc.vector.tensor_scalar(cw[:, :, :], m1[:, :, :], 1.0 / WS, None, ALU.mult).then_inc(s.cw_ok, 1)
            dve.wait_ge(s.cw_ok, 1)

            def low_parts(e):
                dve.wait_ge(s.ehi, e + 1)
                nc.vector.scalar_tensor_tensor(out=e_lo[:, e % 2, :], in0=e_raw[:, e % 2, :], scalar=WS, in1=e_hi[:, e % 2, :],
                                               op0=ALU.mult, op1=ALU.subtract).then_inc(s.elo, 1)

            def add(e, tb):
                for j in range(TB):
                    i = (e * NTB + tb) * TB + j
                    t = tb * TB + j
                    dve.wait_ge(s.down, i + 1)
                    if e:
                        dve.wait_ge(s.acc, i + 1 - B)
                    nc.vector.scalar_tensor_tensor(out=h_all[:, t, :], in0=ps_d[j % 2][:, 0:H], scalar=cw[:, t, e:e + 1],
                                                   in1=h_all[:, t, :], op0=ALU.mult, op1=ALU.add).then_inc(s.acc, 1)

            low_parts(0)
            prev = None
            for e in range(E_):
                for tb in range(NTB):
                    for f in range(FC):
                        n = (e * NTB + tb) * FC + f
                        dve.wait_ge(s.silu, n + 1)
                        dve.wait_ge(s.u_ok, n + 1)
                        if n >= 2:
                            dve.wait_ge(s.hhi, n - 1)
                            dve.wait_ge(s.hlo, n - 1)
                        nc.vector.scalar_tensor_tensor(out=hf[:, n % 2, :], in0=sg[:, n % 2, :], scalar=1.0 / WS,
                                                       in1=ps_u[n % 2][:, :], op0=ALU.mult, op1=ALU.mult).then_inc(s.hf_ok, 1)
                        dve.wait_ge(s.hhi, n + 1)
                        nc.vector.tensor_tensor(hT_lo[:, tb % 2, f, :], hf[:, n % 2, :], hT_hi[:, tb % 2, f, :],
                                                ALU.subtract).then_inc(s.hlo, 1)
                    if prev:
                        add(*prev)
                    prev = (e, tb)
                    if tb == 0 and e + 1 < E_:
                        low_parts(e + 1)
            add(*prev)


def build(nc: bass.Bass, x, ctxT, wunit, wpunit, wexp, gateT, cst, eye, iota, out):
    with ExitStack() as es:
        h_all = es.enter_context(nc.sbuf_tensor("h_all", [P, B, H], mybir.dt.float32))
        ident = es.enter_context(nc.sbuf_tensor("ident", [P, P], mybir.dt.float32))
        attention(nc, h_all, ident, x, ctxT, wunit, wpunit, cst, eye)
        experts(nc, h_all, ident, wexp, gateT, iota, out)


def _layout(a):
    def chunks(w):
        o, i = w.shape
        return w.T.reshape(i // P, P, o).transpose(1, 0, 2)

    A = {k.replace("L0_xattn_", ""): np.asarray(v) for k, v in a.items()}
    kx, vx = A["w_kv_x"][:G * D], A["w_kv_x"][G * D:]
    units, outs = [], []
    wp = A["wproj"].T.reshape(2 * NH, P, H).transpose(1, 0, 2)
    for u in range(NU):
        j = u % HALF
        q, k, v = (A["wq"], A["wk"], A["wv"]) if u < HALF else (A["wqx"], kx, vx)
        w = np.concatenate([q[j * QW:(j + 1) * QW], k[j * KW:(j + 1) * KW], v[j * KW:(j + 1) * KW]], 0)
        units.append(chunks(w))
        outs.append(wp[:, u * UH:(u + 1) * UH])
    exps = []
    for e in range(E_):
        parts = [chunks(A["L0_ffn_w1"][e]), chunks(A["L0_ffn_w3"][e]), chunks(A["L0_ffn_w2"][e])]
        exps.append(np.concatenate([p.reshape(P, -1) for p in parts], 1))

    def cols(v):
        return v.reshape(-1, P).T
    cst = [cols(A["ln_w"]), cols(A["ln_b"])] + [cols(A[n + "_in_scale"]) for n in ("q", "k", "v", "qx")] + [cols(A["proj_smooth"])]
    cst += [cols(A[n]) for n in ("qln_w", "qln_b", "kln_w", "kln_b", "qxln_w", "qxln_b", "kxln_w", "kxln_b")]
    cst += [np.broadcast_to(A[n].reshape(1, 1), (P, 1)) for n in
            ("wq_scale", "wk_scale", "wv_scale", "wqx_scale", "proj_in_scale", "proj_w_scale")]
    return {
        "x": A["x"],
        "ctxT": A["ctx_2048"].transpose(0, 2, 1).reshape(B, KC, P, S).transpose(0, 2, 1, 3),
        "wunit": np.stack(units), "wpunit": np.stack(outs), "wexp": np.stack(exps),
        "gateT": chunks(A["L0_ffn_gate_w"]), "cst": np.concatenate(cst, 1),
        "eye": np.eye(P, dtype=np.float32), "iota": np.broadcast_to(np.arange(E_, dtype=np.float32), (P, E_)),
    }


def kernel(**inputs):
    import concourse.bacc as _bacc
    from concourse.bass_utils import run_bass_kernel_spmd as _run

    nc = _bacc.Bacc("TRN2", target_bir_lowering=False, num_devices=1)
    arrays, args = {}, {}
    for name, a in _layout(inputs).items():
        a = np.ascontiguousarray(a)
        arrays[f"in_{name}"] = a
        args[name] = nc.dram_tensor(f"in_{name}", a.shape, mybir.dt.from_np(a.dtype), kind="ExternalInput").ap()
    args["out"] = nc.dram_tensor("out_0", (B, S, H), mybir.dt.float32, kind="ExternalOutput").ap()
    build(nc, **args)
    r = _run(nc, [arrays], core_ids=[0])
    return r.results[0]["out_0"]
```

```python
import numpy as np
import concourse.bass as bass
from concourse import mybir
from collections import namedtuple
from contextlib import ExitStack

B, S, H = 16, 128, 256
D, NH, G = 128, 16, 8
E_, F_ = 8, 512
P = 128
KC = H // P
UH = 4
UG = UH * G // NH
HALF = NH // UH
NU = 2 * HALF
QW, KW = UH * D, UG * D
NL = UH + UG
LW = NL * D
CORE, CROSS = 0, 1
R_SUM, R_STAT, R_T, R_LOGIT, R_TOP, R_RANK, R_PLACE, R_SEND0, R_SEND1 = 7, 0, 1, 2, 3, 4, 5, 5, 7
U_XQX, U_XT = 2, 3
PEELED = 3
L_NORM, L_QKT, L_SCORE, L_PT, L_HEAD, L_QUANT, L_OUT = 1, 2, 4, 5, 6, 7, 8
FC = F_ // P
T_ALL = B * S
K_TOP = 2
REG = T_ALL + P
NT = K_TOP * T_ALL // P + E_ - 1
SPARE = E_ - 1
RW = H + 2
EPS = 1e-5
FP8_MAX = 448.0
FP8_TINY = 2.0 ** -6
SCORE = float(1.0 / np.sqrt(D))
WS = 16.0

C_LNW, C_LNB, C_IN, C_SMOOTH = 0, KC, 2 * KC, 2 * KC + 4 * KC
C_LN = C_SMOOTH + 2 * NH
C_S = C_LN + 8
C_E = C_S + 6
C_BASE = C_E + E_
C_TILE = C_BASE + E_
C_P = C_TILE + NT
C_DEST = C_P + 1
NCST = C_DEST + B * K_TOP
V_Q, V_K, V_V, V_QX = range(4)


def attention(nc: bass.Bass, m, x, ctxT, wunit, wpunit, wup, wdown, gateT, tri, pads, cst, eye):
    h_all, ident, c_sb, w_hi, w_lo, wp_hi, wp_lo, cntb = m.h_all, m.ident, m.c_sb, m.w_hi, m.w_lo, m.wp_hi, m.wp_lo, m.cntb
    fp32, f16, bf16, u16 = mybir.dt.float32, mybir.dt.float16, mybir.dt.bfloat16, mybir.dt.uint16
    u32, i32 = mybir.dt.uint32, mybir.dt.int32
    ALU, ACT, AX = mybir.AluOpType, mybir.ActivationFunctionType, mybir.AxisListType

    with ExitStack() as es:
        def sb(name, shape, dt=fp32):
            return es.enter_context(nc.sbuf_tensor(name, shape, dt))

        def ps(name, shape, dt=fp32):
            return es.enter_context(nc.psum_tensor(name, shape, dt))

        def sem(name):
            return es.enter_context(nc.semaphore(name))

        mark = sb("mark", [P, 1])
        pmark = sb("pmark", [P, K_TOP])
        rin = sb("rin", [P, 4 * KC])
        rsm = sb("rsm", [P, 2 * NH])
        ws = sb("ws", [P, 2, NL])
        epsw = sb("epsw", [P, 2, NL])
        neghalf = sb("neghalf", [P, NL])
        psc = sb("psc", [P, 1])
        w_raw = sb("w_raw", [P, 2, KC, QW + 2 * KW])
        wp_raw = sb("wp_raw", [P, 2, UH, H])
        w_sum = sb("w_sum", [P, 2, KC * NL])
        w_mean = sb("w_mean", [P, 2, KC * NL])
        xst = sb("xst", [P, 6])
        xmv = sb("xmv", [P, 2])
        xr = sb("xr", [P, 2])
        xc = sb("xc", [P, H])
        tT = sb("tT", [P, KC, P])
        xy = sb("xy", [P, 3 * KC, P])
        xyb = sb("xyb", [P, 3 * KC, P], bf16)
        xm = sb("xm", [P, 3 * KC, P], bf16)
        xs = sb("xs", [P, 3 * KC, P], bf16)
        xq = sb("xq", [P, 4, KC, P], bf16)
        ctx_raw = sb("ctx_raw", [P, KC, P])
        ctx_hi = sb("ctx_hi", [P, KC, P], f16)
        ctx_lo = sb("ctx_lo", [P, KC, P], f16)
        work = sb("work", [P, 4 * LW])
        raw = work[:, 0:2 * LW].rearrange("p (a n) -> p a n", a=2)
        qn = work[:, 2 * LW:].rearrange("p (a n) -> p a n", a=2)
        padrow = work[:, 0:E_ * RW].rearrange("p (e r) -> p e r", e=E_)
        sq = sb("sq", [P, LW])
        ssum = sb("ssum", [P, NL])
        svar = sb("svar", [P, NL])
        sfac = sb("sfac", [P, NL])
        vv = sb("vv", [P, NU, KW])
        qkT = sb("qkT", [P, 2, LW])
        smax = sb("smax", [P, 2, UH])
        nmax = sb("nmax", [P, 2, UH])
        esum = sb("esum", [P, 2, UH])
        rinv = sb("rinv", [P, 2, UH])
        pp = sb("pp", [P, 2, UH, P])
        pT = sb("pT", [P, 2, UH, P])
        y32 = sb("y32", [P, 2, UH, P])
        yb = sb("yb", [P, UH * P], bf16)
        ym = sb("ym", [P, UH * P], bf16)
        ya = sb("ya", [P, UH * P], bf16)
        catq = sb("catq", [P, 2, UH * P], bf16)

        gate = sb("gate", [P, KC, E_])
        upper32 = sb("upper32", [P, P])
        upper = sb("upper", [P, P], bf16)
        ones = sb("ones", [P, P], bf16)
        hst = sb("hst", [P, 6])
        hmv = sb("hmv", [P, 2])
        hr = sb("hr", [P, 2])
        row = sb("row", [P, RW])
        x2T = sb("x2T", [P, KC, P])
        lg = sb("lg", [P, E_])
        top = sb("top", [P, 8])
        topi = sb("topi", [P, 8], u32)
        topf = sb("topf", [P, 8])
        dl = sb("dl", [P, 1])
        ed = sb("ed", [P, 1])
        den = sb("den", [P, 1])
        pr = sb("pr", [P, K_TOP])
        chosen = sb("chosen", [P, K_TOP, E_])
        member = sb("member", [P, E_], bf16)
        rank = sb("rank", [P, 2, E_])
        place = sb("place", [P, E_])
        placed = sb("placed", [P, K_TOP, E_])
        posf = sb("posf", [P, K_TOP])
        posi = sb("posi", [P, K_TOP], i32)
        padf = sb("padf", [P, E_])
        padi = sb("padi", [P, E_], i32)
        tail = sb("tail", [P, K_TOP, 2])

        ps_q = ps("ps_q", [P, 512])
        ps_kv = ps("ps_kv", [P, 512])
        ps_qT = ps("ps_qT", [P, 512])
        ps_kT = ps("ps_kT", [P, 512])
        ps_s = ps("ps_s", [P, 512])
        ps_pT = ps("ps_pT", [P, 512])
        ps_o = ps("ps_o", [P, 512])
        ps_y = ps("ps_y", [P, 512])

        names = ("half_ok c_in x0_in x_in w_in0 w_in1 ctx_in setup rsm_ok wscaled wsummed wmeaned wcentred w_hi_ok w_lo_ok wp_lo_ok "
                 "xstat xmean xvar xfac xc_ok xT_ok tT_ok xdiv xclip xmask xmagic xadd xq_core xq_cross "
                 "ctx_hi_ok ctx_ok proj copied squared summed var fac normed qkT_ps qkT_ok "
                     "scores maxed negmax exped inverted probs pT_ps pT_ok heads y_ok clipped masked magic added catq_ok "
                     "attn h_ok r_in h_st h_mv h_var h_fac x2_ok x2T_ps x2T_ok lg_ps lg_ok top_ok topi_ok topf_ok dl_ok ed_ok "
                 "den_ok p0_ok p1_ok chosen_ok member_ok rank_ps rank_ok place_ok count_ok placed_ok posf_ok pos_ok "
                 "tail_ok tail0 tail1 sent0 sent1 padf_ok padi_ok pads_in pads_sent spare_in "
                 "xw_in0 xw_in1 xp_in0 xp_in1 xw_hi xw_lo xp_hi xp_lo"
                 ).split()
        s = namedtuple("Semaphores", names)(*[sem(name) for name in names])

        def need(eng, sm, b, k):
            if isinstance(b, int):
                if NU * b + k > 0:
                    eng.wait_ge(sm, min(NU * b + k, NU * B))
            else:
                eng.wait_ge(sm, b * NU + k)

        def need_b(eng, sm, b, k=0, per=1):
            if isinstance(b, int):
                if per * (b + k) > 0:
                    eng.wait_ge(sm, per * (b + k))
            else:
                eng.wait_ge(sm, b * per + per * k)

        def live(b, k):
            return not isinstance(b, int) or 0 <= NU * b + k < B * NU

        def has(b):
            return not isinstance(b, int) or 0 <= b < B

        def batches(eng, slot):
            for b in range(PEELED):
                for u in range(NU):
                    slot(b, u)
            with eng.Fori(PEELED, B - 1) as b:
                for u in range(NU):
                    slot(b, u)
            for n in range(NU * (B - 1), NU * (B + 1) + R_SEND1 + 1):
                slot(n // NU, n % NU)

        block = es.enter_context(nc.Block())

        @block.sync
        def _(sp):
            sp.dma_start(c_sb[:, :], cst[:, :]).then_inc(s.c_in, 16)
            sp.dma_start(ident[:, :], eye[:, :]).then_inc(s.c_in, 16)
            sp.dma_start(h_all[:, 0, :], x[0]).then_inc(s.x0_in, 16)
            for u in range(NU):
                if u >= 2:
                    sp.wait_ge(s.w_lo_ok, u - 1)
                    sp.wait_ge(s.wp_lo_ok, u - 1)
                w_in = (s.w_in0, s.w_in1)[u % 2]
                sp.dma_start(w_raw[:, u % 2, :, :], wunit[u]).then_inc(w_in, 16)
                sp.dma_start(wp_raw[:, u % 2, :, :], wpunit[u]).then_inc(w_in, 16)
                if u == 0:
                    sp.dma_start(ctx_raw[:, :, :], ctxT[0]).then_inc(s.ctx_in, 16)
                    sp.dma_start(gate[:, :, :], gateT[:, :, :]).then_inc(s.r_in, 16)
                    sp.dma_start(upper32[:, :], tri[:, :]).then_inc(s.r_in, 16)
                    sp.dma_start(h_all[:, 1:, :], x[1:].rearrange("b p i -> p b i")).then_inc(s.x_in, 16)
            sp.dma_start(m.rows[E_ * REG:, :], pads[E_:].rearrange("t p r -> (t p) r")).then_inc(s.spare_in, 16)

            def expert_up(e):
                sp.dma_start(w_raw[:, e % 2, :, :].rearrange("p c n -> p (c n)"), wup[e]).then_inc((s.xw_in0, s.xw_in1)[e % 2], 16)

            def expert_down(e):
                sp.dma_start(wp_raw[:, e % 2, :, :].rearrange("p c n -> p (c n)"), wdown[e]).then_inc((s.xp_in0, s.xp_in1)[e % 2], 16)

            for e in range(2):
                sp.wait_ge(s.w_lo_ok, NU - 1 + e)
                sp.wait_ge(s.wp_lo_ok, NU - 1 + e)
                expert_up(e)
                expert_down(e)
            with sp.Fori(1, B) as b:
                sp.wait_ge(s.ctx_ok, b)
                sp.dma_start(ctx_raw[:, :, :], ctxT[b]).then_inc(s.ctx_in, 16)
            for e in range(2, E_):
                sp.wait_ge(s.xw_lo, e - 1)
                expert_up(e)
            for e in range(2, E_):
                sp.wait_ge(s.xp_lo, e - 1)
                expert_down(e)
            sp.wait_ge(s.squared, NU * B)
            sp.wait_ge(s.normed, NU * B)
            sp.wait_ge(s.qkT_ps, NU * B)
            sp.dma_start(padrow[:, :, :], pads[0:E_].rearrange("e p r -> p e r")).then_inc(s.pads_in, 16)
            sp.wait_ge(s.spare_in, 16)

        @block.tensor
        def _(pe):
            def input_transposed(bx):
                need_b(pe, s.xc_ok, bx, 1)
                for c in range(KC):
                    last = nc.tensor.transpose(ps_kT[:, KW + c * P:KW + (c + 1) * P], xc[:, c * P:(c + 1) * P], ident[:, :])
                last.then_inc(s.xT_ok, 1)

            def routing(b, u):
                if u == R_T and has(b - 2):
                    need(pe, s.qkT_ok, b, u - L_QKT)
                    need_b(pe, s.x2_ok, b, -1)
                    for c in range(KC):
                        last = nc.tensor.transpose(ps_kT[:, KW + c * P:KW + (c + 1) * P], row[:, c * P:(c + 1) * P], ident[:, :])
                    last.then_inc(s.x2T_ps, 1)
                if u == R_LOGIT and has(b - 2):
                    need_b(pe, s.x2T_ok, b, -1)
                    for c in range(KC):
                        last = nc.tensor.matmul(ps_kT[:, KW:KW + E_], x2T[:, c, :], gate[:, c, :], start=(c == 0), stop=(c == KC - 1))
                    last.then_inc(s.lg_ps, 1)
                if u == R_LOGIT + 1 and has(b - 2):
                    need_b(pe, s.lg_ok, b, -1)
                if u == R_RANK and has(b - 2):
                    need_b(pe, s.member_ok, b, -1)
                    nc.tensor.matmul(ps_kT[:, KW:KW + E_], upper[:, :], member[:, :], start=True, stop=True)
                    nc.tensor.matmul(ps_kT[:, KW + E_:KW + 2 * E_], ones[:, :], member[:, :], start=True, stop=True).then_inc(s.rank_ps, 1)
                if u == R_RANK + 1 and has(b - 2):
                    need_b(pe, s.rank_ok, b, -1)

            def slot(b, u):
                k = u - L_SCORE
                if live(b, k):
                    need(pe, s.qkT_ok, b, k + 1)
                    need(pe, s.exped, b, k)
                    for j in range(UH):
                        kv = QW + (j // (UH // UG)) * D
                        last = nc.tensor.matmul(ps_s[:, j * P:(j + 1) * P], qkT[:, k % 2, j * P:(j + 1) * P],
                                                qkT[:, k % 2, kv:kv + P], start=True, stop=True)
                    last.then_inc(s.scores, 1)
                if live(b, u):
                    if isinstance(b, int) and b == 0:
                        pe.wait_ge(s.w_hi_ok, u + 1)
                        pe.wait_ge(s.w_lo_ok, u + 1)
                        pe.wait_ge(s.wp_lo_ok, u + 1)
                    if u == 0:
                        need_b(pe, s.xq_core, b, 1)
                    if u == HALF:
                        need_b(pe, s.xq_cross, b, 1)
                        need_b(pe, s.ctx_ok, b, 1)
                    need(pe, s.copied, b, u)
                    cross = u >= HALF
                    def project(dst, version, lo, w):
                        for c in range(KC):
                            for half, wt in enumerate((w_hi, w_lo)):
                                last = nc.tensor.matmul(dst, xq[:, version, c, :], wt[:, u, c, lo:lo + w],
                                                        start=(c == 0 and half == 0), stop=(c == KC - 1 and half == 1))
                        return last
                    last = project(ps_q[:, :], V_QX if cross else V_Q, 0, QW)
                    if not cross:
                        project(ps_kv[:, 0:KW], V_K, QW, KW)
                        last = project(ps_kv[:, KW:2 * KW], V_V, QW + KW, KW)
                    else:
                        for c in range(KC):
                            for i, (a, w) in enumerate(((ctx_hi, w_hi), (ctx_hi, w_lo), (ctx_lo, w_hi))):
                                last = nc.tensor.matmul(ps_kv[:, :], a[:, c, :], w[:, u, c, QW:QW + 2 * KW],
                                                        start=(c == 0 and i == 0), stop=(c == KC - 1 and i == 2))
                    last.then_inc(s.proj, 1)
                k = u - L_PT
                if live(b, k):
                    need(pe, s.probs, b, k + 1)
                    need(pe, s.pT_ok, b, k)
                    for j in range(UH):
                        last = nc.tensor.transpose(ps_pT[:, j * P:(j + 1) * P], pp[:, k % 2, j, :], ident[:, :])
                    last.then_inc(s.pT_ps, 1)
                k = u - L_QKT
                if live(b, k):
                    need(pe, s.normed, b, k + 1)
                    need(pe, s.qkT_ok, b, k)
                    if u == 2 and isinstance(b, int) and b == 0:
                        need_b(pe, s.tT_ok, 0, 1)
                    if u == U_XT + 1 and has(b + 1):
                        need_b(pe, s.tT_ok, b, 2)
                    routing(b, u)
                    if u == U_XT and has(b + 1):
                        input_transposed(b + 1)
                    for j in range(NL):
                        dst = ps_qT[:, j * P:(j + 1) * P] if j < UH else ps_kT[:, (j - UH) * P:(j - UH + 1) * P]
                        last = nc.tensor.transpose(dst, qn[:, k % 2, j * P:(j + 1) * P], ident[:, :])
                    last.then_inc(s.qkT_ps, 1)
                else:
                    routing(b, u)
                k = u - L_OUT
                if live(b, k):
                    uu = k % NU
                    need(pe, s.catq_ok, b, k + 1)
                    if uu == 0:
                        need_b(pe, s.h_ok, b, -1)
                    for j in range(UH):
                        for half, wt in enumerate((wp_hi, wp_lo)):
                            last = nc.tensor.matmul(ps_y[:, 0:H], catq[:, k % 2, j * P:(j + 1) * P], wt[:, uu, j, :],
                                                    start=(uu == 0 and j == 0 and half == 0),
                                                    stop=(uu == NU - 1 and j == UH - 1 and half == 1))
                    last.then_inc(s.attn, 1)
                k = u - L_HEAD
                if live(b, k):
                    need(pe, s.pT_ok, b, k + 1)
                    need(pe, s.copied, b, k + 1)
                    need(pe, s.y_ok, b, k)
                    per = UH // UG
                    for g in range(UG):
                        last = nc.tensor.matmul(ps_o[:, g * per * P:(g + 1) * per * P], vv[:, k % NU, g * D:(g + 1) * D],
                                                pT[:, k % 2, g * per:(g + 1) * per, :], start=True, stop=True)
                    last.then_inc(s.heads, 1)

            pe.wait_ge(s.c_in, 32)
            pe.wait_ge(s.r_in, 32)
            input_transposed(0)
            batches(pe, slot)

        @block.scalar
        def _(act):
            def col(i):
                return c_sb[:, i:i + 1]

            def input_evacuated(bx):
                need_b(act, s.xT_ok, bx, 1)
                need_b(act, s.xdiv, bx, 0, 2)
                for c in range(KC):
                    last = nc.scalar.activation(tT[:, c, :], ps_kT[:, KW + c * P:KW + (c + 1) * P], ACT.Identity,
                                                bias=col(C_LNB + c), scale=col(C_LNW + c))
                last.then_inc(s.tT_ok, 1)

            def high_parts(u):
                act.wait_ge(s.wcentred, u + 1)
                nc.scalar.activation(wp_hi[:, u, :, :], wp_raw[:, u % 2, :, :], ACT.Copy)
                nc.scalar.activation(w_hi[:, u, :, :], w_raw[:, u % 2, :, :], ACT.Copy).then_inc(s.w_hi_ok, 1)

            def expert_high_parts(n):
                e = n - NU * (B - 1) - 1
                if 0 <= e < E_:
                    act.wait_ge((s.xw_in0, s.xw_in1)[e % 2], 16 * (e // 2 + 1))
                    act.wait_ge(s.proj, NU * (B - 1) + e + 1)
                    nc.scalar.activation(w_hi[:, e, :, :], w_raw[:, e % 2, :, :], ACT.Copy, scale=WS).then_inc(s.xw_hi, 1)
                e -= L_OUT
                if 0 <= e < E_:
                    act.wait_ge((s.xp_in0, s.xp_in1)[e % 2], 16 * (e // 2 + 1))
                    act.wait_ge(s.attn, NU * (B - 1) + e + 1)
                    nc.scalar.activation(wp_hi[:, e, :, :], wp_raw[:, e % 2, :, :], ACT.Copy, scale=WS).then_inc(s.xp_hi, 1)

            def routing(b, u):
                if u == R_T and has(b - 2):
                    need_b(act, s.x2T_ps, b, -1)
                    nc.scalar.activation(x2T[:, :, :], ps_kT[:, KW:KW + KC * P].rearrange("p (c s) -> p c s", c=KC),
                                         ACT.Copy).then_inc(s.x2T_ok, 1)
                if u == R_LOGIT and has(b - 2):
                    need_b(act, s.lg_ps, b, -1)
                    nc.scalar.activation(lg[:, :], ps_kT[:, KW:KW + E_], ACT.Copy).then_inc(s.lg_ok, 1)
                if u == R_RANK and has(b - 2):
                    need_b(act, s.rank_ps, b, -1)
                    nc.scalar.activation(rank[:, :, :].rearrange("p a e -> p (a e)"), ps_kT[:, KW:KW + 2 * E_], ACT.Copy).then_inc(s.rank_ok, 1)
                    need_b(act, s.dl_ok, b, -1)
                    nc.scalar.activation(ed[:, :], dl[:, :], ACT.Exp).then_inc(s.ed_ok, 1)
                if u == R_SEND0 and has(b - 2):
                    need_b(act, s.tail_ok, b, -1)
                    nc.scalar.activation(row[:, H:RW], tail[:, 0, :], ACT.Copy).then_inc(s.tail0, 1)
                if u == R_SEND1 and has(b - 2):
                    need_b(act, s.sent0, b, -1, 16)
                    nc.scalar.activation(row[:, H:RW], tail[:, 1, :], ACT.Copy).then_inc(s.tail1, 1)

            def slot(b, u):
                if isinstance(b, int) and b == 0 and u + 1 < NU:
                    high_parts(u + 1)
                if isinstance(b, int):
                    expert_high_parts(NU * b + u)
                if u == 1 and live(b, 0):
                    need_b(act, s.ctx_in, b, 1, 16)
                    need(act, s.proj, b, 0)
                    nc.scalar.activation(ctx_hi[:, :, :], ctx_raw[:, :, :], ACT.Copy).then_inc(s.ctx_hi_ok, 1)
                k = u - L_SCORE
                if live(b, k):
                    need(act, s.negmax, b, k + 1)
                    need(act, s.pT_ps, b, k - 1)
                    for j in range(UH):
                        last = nc.scalar.activation(pp[:, k % 2, j, :], ps_s[:, j * P:(j + 1) * P], ACT.Exp,
                                                    bias=nmax[:, k % 2, j:j + 1], scale=SCORE,
                                                    accum_out=esum[:, k % 2, j:j + 1])
                    last.then_inc(s.exped, 1)
                if live(b, u):
                    need(act, s.proj, b, u + 1)
                    need(act, s.normed, b, u - 1)
                    need(act, s.squared, b, u - 1)
                    need(act, s.heads, b, u - NU + 1)
                    nc.scalar.activation(raw[:, u % 2, 0:QW], ps_q[:, :], ACT.Copy)
                    nc.scalar.activation(raw[:, u % 2, QW:LW], ps_kv[:, 0:KW], ACT.Copy)
                    nc.scalar.activation(vv[:, u, :], ps_kv[:, KW:2 * KW], ACT.Copy).then_inc(s.copied, 1)
                k = u - L_PT
                if live(b, k):
                    need(act, s.pT_ps, b, k + 1)
                    need(act, s.heads, b, k - 1)
                    nc.scalar.activation(pT[:, k % 2, :, :], ps_pT[:, :], ACT.Copy).then_inc(s.pT_ok, 1)
                k = u - L_QKT
                if live(b, k):
                    o = C_LN + 4 * (1 if k % NU >= HALF else 0)
                    need(act, s.qkT_ps, b, k + 1)
                    need(act, s.scores, b, k - 1)
                    nc.scalar.activation(qkT[:, k % 2, 0:QW], ps_qT[:, :], ACT.Identity, bias=col(o + 1), scale=col(o))
                    nc.scalar.activation(qkT[:, k % 2, QW:LW], ps_kT[:, 0:KW], ACT.Identity, bias=col(o + 3),
                                         scale=col(o + 2)).then_inc(s.qkT_ok, 1)
                    if u == U_XT and has(b + 1):
                        input_evacuated(b + 1)
                routing(b, u)
                k = u - L_HEAD
                if live(b, k):
                    need(act, s.heads, b, k + 1)
                    need(act, s.clipped, b, k - 1)
                    for j in range(UH):
                        h = (k % NU) * UH + j
                        last = nc.scalar.activation(y32[:, k % 2, j, :], ps_o[:, j * P:(j + 1) * P], ACT.Copy,
                                                    scale=rsm[:, h:h + 1])
                    last.then_inc(s.y_ok, 1)

            act.wait_ge(s.c_in, 32)
            act.wait_ge(s.rsm_ok, 2)
            input_evacuated(0)
            high_parts(0)
            batches(act, slot)

        @block.vector
        def _(dve):
            def scaled(dst, src, col_, **kw):
                return nc.vector.tensor_scalar(dst, src, col_, None, ALU.mult, **kw)

            def col(i):
                return c_sb[:, i:i + 1]

            def weights(u):
                i = u % 2
                dve.wait_ge((s.w_in0, s.w_in1)[i], 32 * (u // 2 + 1))
                cross = u >= HALF
                parts = [(V_QX, 0, QW)] if cross else [(V_Q, 0, QW), (V_K, QW, KW), (V_V, QW + KW, KW)]
                for v, lo, w in parts:
                    for c in range(KC):
                        last = scaled(w_raw[:, i, c, lo:lo + w], w_raw[:, i, c, lo:lo + w], col(C_IN + v * KC + c))
                last.then_inc(s.wscaled, 1)
                dve.wait_ge(s.wscaled, u + 1)
                for c in range(KC):
                    last = nc.vector.tensor_reduce(w_sum[:, i, c * NL:(c + 1) * NL],
                                                   w_raw[:, i, c, 0:LW].rearrange("p (h d) -> p h d", d=D), AX.X, ALU.add)
                last.then_inc(s.wsummed, 1)
                dve.wait_ge(s.wsummed, u + 1)
                if u >= 2:
                    dve.wait_ge(s.wcentred, u - 1)
                nc.vector.tensor_scalar(w_mean[:, i, :], w_sum[:, i, :], 1.0 / D, None, ALU.mult).then_inc(s.wmeaned, 1)

            def low_parts(u):
                dve.wait_ge(s.w_hi_ok, u + 1)
                nc.vector.tensor_tensor(w_lo[:, u, :, :], w_raw[:, u % 2, :, :], w_hi[:, u, :, :], ALU.subtract).then_inc(s.w_lo_ok, 1)

            def expert_low_parts(n):
                e = n - NU * (B - 1) - 1
                if 0 <= e < E_:
                    dve.wait_ge(s.xw_hi, e + 1)
                    nc.vector.scalar_tensor_tensor(out=w_lo[:, e, :, :], in0=w_raw[:, e % 2, :, :], scalar=WS, in1=w_hi[:, e, :, :],
                                                   op0=ALU.mult, op1=ALU.subtract).then_inc(s.xw_lo, 1)
                e -= L_OUT
                if 0 <= e < E_:
                    dve.wait_ge(s.xp_hi, e + 1)
                    nc.vector.scalar_tensor_tensor(out=wp_lo[:, e, :, :], in0=wp_raw[:, e % 2, :, :], scalar=WS, in1=wp_hi[:, e, :, :],
                                                   op0=ALU.mult, op1=ALU.subtract).then_inc(s.xp_lo, 1)

            def statistics(b):
                need_b(dve, s.h_ok, b, 0)
                nc.vector.memset(mark[:, :], 0.0)
                nc.vector.bn_stats(hst[:, :], h_all[:, b - 1, :]).then_inc(s.h_st, 1)
                need_b(dve, s.h_st, b, 0)
                nc.vector.memset(mark[:, :], 0.0)
                nc.vector.bn_aggr(hmv[:, :], hst[:, :]).then_inc(s.h_mv, 1)
                need_b(dve, s.h_mv, b, 0)
                nc.vector.tensor_scalar(hr[:, 0:1], hmv[:, 1:2], EPS, None, ALU.add).then_inc(s.h_var, 1)

            def choice(b):
                need_b(dve, s.lg_ok, b, -1)
                nc.vector.memset(mark[:, :], 0.0)
                nc.vector.max(top[:, :], lg[:, :]).then_inc(s.top_ok, 1)
                need_b(dve, s.top_ok, b, -1)
                need_b(dve, s.ed_ok, b, -2)
                nc.vector.tensor_tensor(dl[:, :], top[:, 1:2], top[:, 0:1], ALU.subtract).then_inc(s.dl_ok, 1)
                nc.vector.max_index(topi[:, :], top[:, :], lg[:, :]).then_inc(s.topi_ok, 1)
                need_b(dve, s.topi_ok, b, -1)
                nc.vector.tensor_copy(topf[:, :], topi[:, :]).then_inc(s.topf_ok, 1)
                need_b(dve, s.topf_ok, b, -1)
                shape = [P, K_TOP, E_]
                nc.vector.tensor_tensor(chosen[:, :, :], topf[:, 0:K_TOP].unsqueeze(2).to_broadcast(shape),
                                        c_sb[:, C_E:C_E + E_].unsqueeze(1).to_broadcast(shape), ALU.is_equal).then_inc(s.chosen_ok, 1)
                need_b(dve, s.chosen_ok, b, -1)
                nc.vector.tensor_tensor(member[:, :], chosen[:, 0, :], chosen[:, 1, :], ALU.add).then_inc(s.member_ok, 1)

            def placing(b):
                need_b(dve, s.rank_ok, b, -1)
                nc.vector.tensor_tensor(place[:, :], rank[:, 0, :], cntb[:, :], ALU.add).then_inc(s.place_ok, 1)
                need_b(dve, s.ed_ok, b, -1)
                nc.vector.tensor_scalar(den[:, :], ed[:, :], 1.0, WS, ALU.add, ALU.mult).then_inc(s.den_ok, 1)
                need_b(dve, s.place_ok, b, -1)
                nc.vector.tensor_tensor(cntb[:, :], cntb[:, :], rank[:, 1, :], ALU.add).then_inc(s.count_ok, 1)
                need_b(dve, s.den_ok, b, -1)
                nc.vector.reciprocal(pr[:, 0:1], den[:, :]).then_inc(s.p0_ok, 1)
                shape = [P, K_TOP, E_]
                nc.vector.tensor_tensor(placed[:, :, :], chosen[:, :, :], place[:, :].unsqueeze(1).to_broadcast(shape),
                                        ALU.mult).then_inc(s.placed_ok, 1)
                need_b(dve, s.p0_ok, b, -1)
                nc.vector.tensor_tensor(pr[:, 1:2], pr[:, 0:1], ed[:, :], ALU.mult).then_inc(s.p1_ok, 1)
                need_b(dve, s.placed_ok, b, -1)
                nc.vector.tensor_reduce(posf[:, :], placed[:, :, :], AX.X, ALU.add).then_inc(s.posf_ok, 1)
                need_b(dve, s.p1_ok, b, -1)
                need_b(dve, s.tail1, b, -2)
                nc.vector.tensor_copy(tail[:, :, 0], pr[:, :])
                dest = c_sb[:, C_DEST:C_DEST + B * K_TOP].rearrange("p (b k) -> p b k", k=K_TOP)
                nc.vector.tensor_copy(tail[:, :, 1], dest[:, b - 2, :]).then_inc(s.tail_ok, 1)
                need_b(dve, s.posf_ok, b, -1)
                need_b(dve, s.sent1, b, -2, 16)
                nc.vector.tensor_copy(posi[:, :], posf[:, :]).then_inc(s.pos_ok, 1)

            def input_statistics(bx):
                dve.wait_ge(s.x0_in if isinstance(bx, int) and bx == 0 else s.x_in, 16)
                nc.vector.bn_stats(xst[:, :], h_all[:, bx, :]).then_inc(s.xstat, 1)
                need_b(dve, s.xstat, bx, 1)
                nc.vector.memset(mark[:, :], 0.0)
                nc.vector.bn_aggr(xmv[:, :], xst[:, :]).then_inc(s.xmean, 1)
                need_b(dve, s.xmean, bx, 1)
                nc.vector.tensor_scalar(xr[:, 0:1], xmv[:, 1:2], 1.0 + EPS, EPS * EPS, ALU.mult, ALU.add).then_inc(s.xvar, 1)

            def input_normalised(bx):
                need_b(dve, s.xfac, bx, 1)
                need_b(dve, s.xT_ok, bx, 0)
                nc.vector.tensor_scalar(xc[:, :], h_all[:, bx, :], xmv[:, 0:1], xr[:, 1:2], ALU.subtract, ALU.mult).then_inc(s.xc_ok, 1)

            def input_quantised(bx, done, *steps):
                core = done is s.xq_core
                v, nv = (V_Q, 3) if core else (V_QX, 1)
                n = nv * KC

                def after(sm):
                    if isinstance(bx, int):
                        dve.wait_ge(sm, 2 * bx + (1 if core else 2))
                    else:
                        dve.wait_ge(sm, bx * 2 + (1 if core else 2))
                if 0 in steps:
                    need_b(dve, s.tT_ok, bx, 1)
                    scales = rin[:, v * KC:(v + nv) * KC].rearrange("p (v c) -> p v c", c=KC)
                    nc.vector.tensor_tensor(xy[:, 0:n, :].rearrange("p (v c) s -> p v c s", c=KC),
                                            tT[:, :, :].unsqueeze(1).to_broadcast([P, nv, KC, P]),
                                            scales.unsqueeze(3).to_broadcast([P, nv, KC, P]), ALU.mult).then_inc(s.xdiv, 1)
                if 1 in steps:
                    after(s.xdiv)
                    nc.vector.tensor_scalar(xyb[:, 0:n, :], xy[:, 0:n, :], FP8_MAX, -FP8_MAX, ALU.min, ALU.max).then_inc(s.xclip, 1)
                if 2 in steps:
                    after(s.xclip)
                    nc.vector.tensor_scalar(xm[:, 0:n, :].bitcast(u16), xyb[:, 0:n, :].bitcast(u16), 0x7F80, None,
                                            ALU.bitwise_and).then_inc(s.xmask, 1)
                if 3 in steps:
                    after(s.xmask)
                    nc.vector.tensor_scalar(xm[:, 0:n, :], xm[:, 0:n, :], FP8_TINY, 24.0, ALU.max, ALU.mult).then_inc(s.xmagic, 1)
                if 4 in steps:
                    after(s.xmagic)
                    nc.vector.tensor_tensor(xs[:, 0:n, :], xyb[:, 0:n, :], xm[:, 0:n, :], ALU.add).then_inc(s.xadd, 1)
                if 5 in steps:
                    after(s.xadd)
                    need(dve, s.proj, bx, HALF - NU if core else 0)
                    dst = (xq[:, 0:3, :, :] if core else xq[:, 3:4, :, :]).rearrange("p v c s -> p (v c) s")
                    nc.vector.tensor_tensor(dst, xs[:, 0:n, :], xm[:, 0:n, :], ALU.subtract).then_inc(done, 1)

            def inputs(b, u, place):
                if has(b):
                    if (u, place) == (0, 1):
                        input_quantised(b, s.xq_cross, 0)
                    if (u, place) == (0, 2):
                        input_quantised(b, s.xq_cross, 1)
                    if (u, place) == (1, 1):
                        input_quantised(b, s.xq_cross, 2)
                    if (u, place) == (2, 0):
                        input_quantised(b, s.xq_cross, 3)
                    if (u, place) == (2, 1):
                        input_quantised(b, s.xq_cross, 4)
                    if (u, place) == (2, 2):
                        input_quantised(b, s.xq_cross, 5)
                if has(b + 1):
                    if (u, place) == (U_XQX, 2):
                        input_statistics(b + 1)
                    if (u, place) == (U_XT, 1):
                        input_normalised(b + 1)
                    if (u, place) == (4, 1):
                        input_quantised(b + 1, s.xq_core, 0)
                    if (u, place) == (4, 2):
                        input_quantised(b + 1, s.xq_core, 1)
                    if (u, place) == (5, 1):
                        input_quantised(b + 1, s.xq_core, 2)
                    if (u, place) == (6, 0):
                        input_quantised(b + 1, s.xq_core, 3)
                    if (u, place) == (6, 1):
                        input_quantised(b + 1, s.xq_core, 4)
                    if (u, place) == (7, 1):
                        input_quantised(b + 1, s.xq_core, 5)

            def slot(b, u):
                if isinstance(b, int) and b == 0:
                    if u + 1 < NU:
                        low_parts(u + 1)
                    if u + 2 < NU:
                        weights(u + 2)
                if isinstance(b, int):
                    expert_low_parts(NU * b + u)
                k = u - L_QKT
                if live(b, k):
                    need(dve, s.fac, b, k + 1)
                    need(dve, s.qkT_ps, b, k - 1)
                    nc.vector.tensor_tensor(qn[:, k % 2, :].rearrange("p (h d) -> p h d", d=D),
                                            raw[:, k % 2, :].rearrange("p (h d) -> p h d", d=D),
                                            sfac[:, :].unsqueeze(2).to_broadcast([P, NL, D]), ALU.mult).then_inc(s.normed, 1)
                inputs(b, u, 0)
                ko, ks, kv = u - L_QUANT, u - L_SCORE, u - L_NORM
                kind = CROSS if kv % NU >= HALF else CORE
                if live(b, ks):
                    need(dve, s.scores, b, ks + 1)
                    nc.vector.tensor_reduce(smax[:, ks % 2, :], ps_s[:, :].rearrange("p (h t) -> p h t", t=P), AX.X,
                                            ALU.max).then_inc(s.maxed, 1)
                if live(b, ks):
                    need(dve, s.maxed, b, ks + 1)
                    need(dve, s.exped, b, ks - 1)
                    nc.vector.tensor_scalar(nmax[:, ks % 2, :], smax[:, ks % 2, :], -SCORE, None, ALU.mult).then_inc(s.negmax, 1)
                if live(b, ko):
                    need(dve, s.y_ok, b, ko + 1)
                    nc.vector.tensor_scalar(yb[:, :], y32[:, ko % 2, :, :].rearrange("p h t -> p (h t)"), FP8_MAX, -FP8_MAX,
                                            ALU.min, ALU.max).then_inc(s.clipped, 1)
                if live(b, ko):
                    need(dve, s.clipped, b, ko + 1)
                    nc.vector.tensor_scalar(ym[:, :].bitcast(u16), yb[:, :].bitcast(u16), 0x7F80, None,
                                            ALU.bitwise_and).then_inc(s.masked, 1)
                if live(b, ko):
                    need(dve, s.masked, b, ko + 1)
                    nc.vector.tensor_scalar(ym[:, :], ym[:, :], FP8_TINY, 24.0, ALU.max, ALU.mult).then_inc(s.magic, 1)
                if u == R_T and has(b - 2):
                    need_b(dve, s.h_fac, b, -1)
                    need_b(dve, s.sent1, b, -2, 16)
                    need_b(dve, s.x2T_ps, b, -2)
                    nc.vector.tensor_scalar(row[:, 0:H], h_all[:, b - 2, :], hmv[:, 0:1], hr[:, 1:2], ALU.subtract,
                                            ALU.mult).then_inc(s.x2_ok, 1)
                inputs(b, u, 1)
                if live(b, kv):
                    need(dve, s.squared, b, kv + 1)
                    nc.vector.tensor_reduce(ssum[:, :], sq[:, :].rearrange("p (h d) -> p h d", d=D), AX.X,
                                            ALU.add).then_inc(s.summed, 1)
                if live(b, ko):
                    need(dve, s.magic, b, ko + 1)
                    nc.vector.tensor_tensor(ya[:, :], yb[:, :], ym[:, :], ALU.add).then_inc(s.added, 1)
                if live(b, kv):
                    need(dve, s.summed, b, kv + 1)
                    need(dve, s.fac, b, kv)
                    nc.vector.scalar_tensor_tensor(out=svar[:, :], in0=ssum[:, :], scalar=1.0 / D, in1=epsw[:, kind, :],
                                                   op0=ALU.mult, op1=ALU.add).then_inc(s.var, 1)
                if live(b, ko):
                    need(dve, s.added, b, ko + 1)
                    need(dve, s.attn, b, ko - 1)
                    nc.vector.tensor_tensor(catq[:, ko % 2, :], ya[:, :], ym[:, :], ALU.subtract).then_inc(s.catq_ok, 1)
                if live(b, ks):
                    need(dve, s.exped, b, ks + 1)
                    need(dve, s.probs, b, ks - 1)
                    nc.vector.reciprocal(rinv[:, ks % 2, :], esum[:, ks % 2, :]).then_inc(s.inverted, 1)
                if u == R_SUM and has(b - 1):
                    need(dve, s.attn, b, 0)
                    h = h_all[:, b - 1, :]
                    nc.vector.scalar_tensor_tensor(out=h, in0=ps_y[:, 0:H], scalar=psc[:, :], in1=h,
                                                   op0=ALU.mult, op1=ALU.add).then_inc(s.h_ok, 1)
                if u == R_STAT and has(b - 2):
                    statistics(b - 1)
                if u == R_TOP and has(b - 2):
                    choice(b)
                if u == R_PLACE and has(b - 2):
                    placing(b)
                inputs(b, u, 2)

            dve.wait_ge(s.c_in, 32)
            nc.vector.reciprocal(rsm[:, :], c_sb[:, C_SMOOTH:C_SMOOTH + 2 * NH])
            nc.vector.reciprocal(rin[:, :], c_sb[:, C_IN:C_IN + 4 * KC])
            nc.vector.tensor_tensor(psc[:, :], col(C_S + 4), col(C_S + 5), ALU.mult)
            nc.vector.memset(ws[:, CROSS, UH:NL], 1.0)
            for kind, lo, n, c in ((CORE, 0, UH, C_S), (CORE, UH, UG, C_S + 1), (CROSS, 0, UH, C_S + 3)):
                last = nc.vector.tensor_copy(ws[:, kind, lo:lo + n], col(c).to_broadcast([P, n]))
            last.then_inc(s.rsm_ok, 1)
            dve.wait_ge(s.rsm_ok, 1)
            nc.vector.tensor_scalar(rsm[:, 0:NH], rsm[:, 0:NH], col(C_S + 2), None, ALU.mult).then_inc(s.rsm_ok, 1)
            nc.vector.tensor_tensor(epsw[:, :, :], ws[:, :, :], ws[:, :, :], ALU.mult).then_inc(s.setup, 1)
            dve.wait_ge(s.setup, 1)
            nc.vector.reciprocal(epsw[:, :, :], epsw[:, :, :]).then_inc(s.setup, 1)
            dve.wait_ge(s.setup, 2)
            nc.vector.tensor_scalar(epsw[:, :, :], epsw[:, :, :], EPS, None, ALU.mult).then_inc(s.setup, 1)
            dve.wait_ge(s.setup, 3)
            nc.vector.tensor_copy(cntb[:, :], c_sb[:, C_BASE:C_BASE + E_]).then_inc(s.setup, 1)
            nc.vector.memset(ones[:, :], 1.0)
            input_statistics(0)
            weights(0)
            input_normalised(0)
            weights(1)
            input_quantised(0, s.xq_core, 0, 1, 2, 3, 4, 5)
            low_parts(0)
            dve.wait_ge(s.r_in, 32)
            nc.vector.tensor_copy(upper[:, :], upper32[:, :])
            batches(dve, slot)
            dve.wait_ge(s.count_ok, B)
            nc.vector.tensor_scalar(padf[:, :], cntb[:, :], col(C_P), None, ALU.add).then_inc(s.padf_ok, 1)
            dve.wait_ge(s.padf_ok, 1)
            nc.vector.tensor_copy(padi[:, :], padf[:, :]).then_inc(s.padi_ok, 1)

        @block.gpsimd
        def _(pool):
            def input_factor(bx):
                need_b(pool, s.xvar, bx, 1)
                nc.gpsimd.tensor_tensor(xr[:, 1:2], xr[:, 0:1], neghalf[:, 0:1], ALU.pow).then_inc(s.xfac, 1)

            def send(k, done):
                nc.gpsimd.tensor_tensor(pmark[:, k:k + 1], neghalf[:, 0:1], neghalf[:, 0:1], ALU.mult)
                nc.gpsimd.indirect_dma_start(out=m.rows[:, :], out_offset=bass.IndirectOffsetOnAxis(ap=posi[:, k:k + 1], axis=0),
                                             in_=row[:, :], in_offset=None).then_inc(done, 16)

            def centred(u):
                pool.wait_ge(s.wmeaned, u + 1)
                for c in range(KC):
                    v = w_raw[:, u % 2, c, 0:LW].rearrange("p (h d) -> p h d", d=D)
                    m = w_mean[:, u % 2, c * NL:(c + 1) * NL].unsqueeze(2).to_broadcast([P, NL, D])
                    last = nc.gpsimd.tensor_tensor(v, v, m, ALU.subtract)
                last.then_inc(s.wcentred, 1)

            def low_parts(u):
                pool.wait_ge(s.w_hi_ok, u + 1)
                nc.gpsimd.tensor_tensor(wp_lo[:, u, :, :], wp_raw[:, u % 2, :, :], wp_hi[:, u, :, :], ALU.subtract).then_inc(s.wp_lo_ok, 1)

            def slot(b, u):
                if isinstance(b, int) and b == 0:
                    if u + 1 < NU:
                        low_parts(u + 1)
                    if u + 2 < NU:
                        centred(u + 2)
                k = u - L_NORM
                if live(b, k):
                    need(pool, s.var, b, k + 1)
                    need(pool, s.normed, b, k)
                    nc.gpsimd.tensor_tensor(sfac[:, :], svar[:, :], neghalf[:, :], ALU.pow).then_inc(s.fac, 1)
                if u == 1 and live(b, 0):
                    need_b(pool, s.ctx_hi_ok, b, 1)
                    nc.gpsimd.tensor_tensor(ctx_lo[:, :, :], ctx_raw[:, :, :], ctx_hi[:, :, :], ALU.subtract).then_inc(s.ctx_ok, 1)
                k = u - L_SCORE
                if live(b, k):
                    need(pool, s.inverted, b, k + 1)
                    need(pool, s.exped, b, k + 1)
                    nc.gpsimd.tensor_tensor(pp[:, k % 2, :, :], pp[:, k % 2, :, :],
                                            rinv[:, k % 2, :].unsqueeze(2).to_broadcast([P, UH, P]),
                                            ALU.mult).then_inc(s.probs, 1)
                if u == U_XQX and has(b + 1):
                    input_factor(b + 1)
                if u == R_STAT and has(b - 2):
                    need_b(pool, s.h_var, b, -1)
                    nc.gpsimd.tensor_tensor(hr[:, 1:2], hr[:, 0:1], neghalf[:, 0:1], ALU.pow).then_inc(s.h_fac, 1)
                if live(b, u):
                    need(pool, s.copied, b, u + 1)
                    need(pool, s.summed, b, u)
                    nc.gpsimd.tensor_tensor(sq[:, :], raw[:, u % 2, :], raw[:, u % 2, :], ALU.mult).then_inc(s.squared, 1)
                if u == R_SEND0 and has(b - 2):
                    need_b(pool, s.tail0, b, -1)
                    need_b(pool, s.pos_ok, b, -1)
                    send(0, s.sent0)
                if u == R_SEND1 and has(b - 2):
                    need_b(pool, s.tail1, b, -1)
                    send(1, s.sent1)

            nc.gpsimd.memset(neghalf[:, :], -0.5).then_inc(s.half_ok, 1)
            pool.wait_ge(s.half_ok, 1)
            input_factor(0)
            centred(0)
            centred(1)
            low_parts(0)
            batches(pool, slot)
            pool.wait_ge(s.padi_ok, 1)
            pool.wait_ge(s.pads_in, 16)
            pool.wait_ge(s.sent0, 16 * B)
            pool.wait_ge(s.sent1, 16 * B)
            for e in range(E_):
                nc.gpsimd.indirect_dma_start(out=m.rows[:, :], out_offset=bass.IndirectOffsetOnAxis(ap=padi[:, e:e + 1], axis=0),
                                             in_=padrow[:, e, :], in_offset=None).then_inc(s.pads_sent, 16)
            pool.wait_ge(s.pads_sent, 16 * E_)


def experts(nc: bass.Bass, m, out):
    fp32, f16, i32 = mybir.dt.float32, mybir.dt.float16, mybir.dt.int32
    ALU, ACT, AX = mybir.AluOpType, mybir.ActivationFunctionType, mybir.AxisListType
    R = 4
    L_UP, L_HT, L_DOWN = 1, 2, 3
    LAST = NT + L_DOWN
    ROUNDS = NT // R

    with ExitStack() as es:
        def sb(name, shape, dt=fp32):
            return es.enter_context(nc.sbuf_tensor(name, shape, dt))

        def ps(name, shape, dt=fp32):
            return es.enter_context(nc.psum_tensor(name, shape, dt))

        cnt = sb("t_cnt", [P, E_])
        half = sb("t_half", [P, E_])
        tiles = sb("t_tiles", [P, E_])
        scan = [sb(f"t_scan{i}", [P, E_]) for i in range(3)]
        skip = sb("t_skip", [P, E_])
        past = sb("t_past", [P, NT, E_])
        jump = sb("t_jump", [P, NT, E_])
        expf = sb("t_expf", [P, NT])
        rowf = sb("t_rowf", [P, NT])
        rowg = sb("t_rowg", [P, NT])
        expi = sb("t_expi", [P, NT], i32)
        rowi = sb("t_rowi", [P, NT], i32)
        xg = sb("t_xg", [P, R, RW])
        xT_hi = sb("t_xT_hi", [P, 2, KC, P], f16)
        xT_lo = sb("t_xT_lo", [P, 2, KC, P], f16)
        sg = sb("t_sg", [P, 2, F_])
        hf = sb("t_hf", [P, 2, F_])
        hT_hi = sb("t_hT_hi", [P, 2, FC, P], f16)
        hT_lo = sb("t_hT_lo", [P, 2, FC, P], f16)
        y = sb("t_y", [P, R, H])
        meta = sb("t_meta", [P, R, 2])
        dest = sb("t_dest", [P, R], i32)
        pmark = sb("t_mark", [P, 1])
        yy = sb("t_yy", [P, R, K_TOP, H])
        ps_x = ps("t_ps_x", [P, 512])
        ps_g = [ps(f"t_ps_g{i}", [P, F_]) for i in range(2)]
        ps_u = [ps(f"t_ps_u{i}", [P, F_]) for i in range(2)]
        ps_h = ps("t_ps_h", [P, F_])
        ps_d = ps("t_ps_d", [P, 512])

        names = ("cnt_ok half_ok tiles_ok scan0 scan1 scan2 skip_ok past_ok jump_ok expf_ok rowf_ok rowg_ok exp_ok row_ok "
                 "in0 in1 in2 in3 xT_ps x_hi x_lo g_ok u_ok silu h_ok hT_ps h_hi h_lo down y_ok meta_ok dest_ok marked sent0 sent1 sent2 sent3 "
                 "y_in0 y_in1 y_in2 y_in3 sum0 sum1 stored").split()
        s = namedtuple("Semaphores", names)(*[es.enter_context(nc.semaphore("t_" + name)) for name in names])
        x_in = (s.in0, s.in1, s.in2, s.in3)
        y_in = (s.y_in0, s.y_in1, s.y_in2, s.y_in3)
        sent = (s.sent0, s.sent1, s.sent2, s.sent3)

        def need(eng, sm, r, k, per=1):
            if isinstance(r, int):
                if R * r + k > 0:
                    eng.wait_ge(sm, per * min(R * r + k, NT))
            else:
                eng.wait_ge(sm, r * (R * per) + per * k)

        def live(r, k):
            return not isinstance(r, int) or 0 <= R * r + k < NT

        def at(r, k):
            return R * r + k if isinstance(r, int) else r * R + k

        def rounds(eng, slot, last):
            for n in range(2 * R):
                slot(n // R, n % R)
            with eng.Fori(2, ROUNDS) as r:
                for u in range(R):
                    slot(r, u)
            for n in range(R * ROUNDS, last):
                slot(n // R, n % R)

        block = es.enter_context(nc.Block())

        @block.sync
        def _(sp):
            def slot(r, u):
                if live(r, u):
                    start = sp.value_load(rowi[0:1, bass.ds(at(r, u), 1)], min_val=0, max_val=E_ * REG + (SPARE - 1) * P)
                    need(sp, s.xT_ps, r, u - R + 1)
                    need(sp, s.meta_ok, r, u - R + 1)
                    sp.dma_start(xg[:, u, :], m.rows[bass.ds(start, P), :]).then_inc(x_in[u], 16)

            sp.wait_ge(s.row_ok, 1)
            rounds(sp, slot, NT)
            for i in range(R):
                sp.wait_ge(sent[i], 16 * ((NT - i + R - 1) // R))
            src = m.ybuf[0:K_TOP * T_ALL, :].rearrange("(k b s) d -> b s k d", k=K_TOP, b=B)
            for b in range(B):
                if b >= R:
                    sp.wait_ge(s.sum1, b - R + 1)
                sp.dma_start(yy[:, b % R, :, :], src[b]).then_inc(y_in[b % R], 16)

        @block.tensor
        def _(pe):
            def slot(r, u):
                k = u - L_UP
                if live(r, k):
                    e = pe.value_load(expi[0:1, bass.ds(at(r, k), 1)], min_val=0, max_val=E_ - 1)
                    need(pe, s.x_hi, r, k + 1)
                    need(pe, s.x_lo, r, k + 1)
                    need(pe, s.h_ok, r, k - 1)
                    for first, bank, done in ((0, ps_g, s.g_ok), (1, ps_u, s.u_ok)):
                        for c in range(KC):
                            for i, (a, w) in enumerate(((xT_hi, m.w_hi), (xT_lo, m.w_hi), (xT_hi, m.w_lo))):
                                last = nc.tensor.matmul(bank[k % 2][:, :], a[:, k % 2, c, :], w[:, e, first, c * F_:(c + 1) * F_],
                                                        start=(c == 0 and i == 0), stop=(c == KC - 1 and i == 2))
                        last.then_inc(done, 1)
                if live(r, u):
                    pe.wait_ge(x_in[u], (r + 1) * 16) if isinstance(r, int) else pe.wait_ge(x_in[u], r * 16 + 16)
                    need(pe, s.x_lo, r, u)
                    for c in range(KC):
                        last = nc.tensor.transpose(ps_x[:, c * P:(c + 1) * P], xg[:, u, c * P:(c + 1) * P], m.ident[:, :])
                    last.then_inc(s.xT_ps, 1)
                k = u - L_HT
                if live(r, k):
                    need(pe, s.h_ok, r, k + 1)
                    need(pe, s.h_lo, r, k)
                    for f in range(FC):
                        last = nc.tensor.transpose(ps_h[:, f * P:(f + 1) * P], hf[:, k % 2, f * P:(f + 1) * P], m.ident[:, :])
                    last.then_inc(s.hT_ps, 1)
                k = u - L_DOWN
                if live(r, k):
                    e = pe.value_load(expi[0:1, bass.ds(at(r, k), 1)], min_val=0, max_val=E_ - 1)
                    need(pe, s.h_lo, r, k + 1)
                    need(pe, s.h_hi, r, k + 1)
                    need(pe, s.y_ok, r, k)
                    for f in range(FC):
                        for i, (a, w) in enumerate(((hT_hi, m.wp_hi), (hT_lo, m.wp_hi), (hT_hi, m.wp_lo))):
                            last = nc.tensor.matmul(ps_d[:, 0:H], a[:, k % 2, f, :], w[:, e, f, :],
                                                    start=(f == 0 and i == 0), stop=(f == FC - 1 and i == 2))
                    last.then_inc(s.down, 1)

            pe.wait_ge(s.exp_ok, 1)
            rounds(pe, slot, LAST)

        @block.scalar
        def _(act):
            def slot(r, u):
                k = u - L_UP
                if live(r, k):
                    need(act, s.g_ok, r, k + 1)
                    need(act, s.h_ok, r, k - 1)
                    nc.scalar.activation(sg[:, k % 2, :], ps_g[k % 2][:, :], ACT.Silu, scale=1.0 / WS).then_inc(s.silu, 1)
                if live(r, u):
                    need(act, s.xT_ps, r, u + 1)
                    need(act, s.u_ok, r, u - 1)
                    nc.scalar.activation(xT_hi[:, u % 2, :, :], ps_x[:, 0:KC * P].rearrange("p (c s) -> p c s", c=KC),
                                         ACT.Copy).then_inc(s.x_hi, 1)
                k = u - L_HT
                if live(r, k):
                    need(act, s.hT_ps, r, k + 1)
                    need(act, s.down, r, k - 1)
                    nc.scalar.activation(hT_hi[:, k % 2, :, :], ps_h[:, :].rearrange("p (f s) -> p f s", f=FC),
                                         ACT.Copy).then_inc(s.h_hi, 1)
                k = u - L_DOWN
                if live(r, k):
                    need(act, s.down, r, k + 1)
                    uses = r + k // R
                    if not isinstance(r, int) or uses > 0:
                        act.wait_ge(sent[k % R], uses * 16)
                    nc.scalar.activation(y[:, k % R, :], ps_d[:, 0:H], ACT.Copy, scale=meta[:, k % R, 0:1]).then_inc(s.y_ok, 1)

            rounds(act, slot, LAST)
            for b in range(B):
                act.wait_ge(s.sum1, b + 1)
                act.dma_start(out[b], m.h_all[:, b, :]).then_inc(s.stored, 16)
            act.wait_ge(s.stored, 16 * B)

        @block.vector
        def _(dve):
            def c(lo, n):
                return m.c_sb[:, lo:lo + n]

            nc.vector.tensor_tensor(cnt[:, :], m.cntb[:, :], c(C_BASE, E_), ALU.subtract).then_inc(s.cnt_ok, 1)
            dve.wait_ge(s.cnt_ok, 1)
            nc.vector.tensor_scalar(half[:, :], cnt[:, :], 1.0 / P, 0.5 - 0.5 / P, ALU.mult, ALU.add).then_inc(s.half_ok, 1)
            dve.wait_ge(s.half_ok, 1)
            nc.vector.tensor_scalar(tiles[:, :], half[:, :], 2.0 ** 23, 2.0 ** 23, ALU.add, ALU.subtract).then_inc(s.tiles_ok, 1)
            dve.wait_ge(s.tiles_ok, 1)
            nc.vector.tensor_scalar(skip[:, :], tiles[:, :], -float(P), float(REG), ALU.mult, ALU.add).then_inc(s.skip_ok, 1)
            src = tiles
            for i, done in enumerate((s.scan0, s.scan1, s.scan2)):
                d = 1 << i
                nc.vector.tensor_copy(scan[i][:, 0:d], src[:, 0:d])
                nc.vector.tensor_tensor(scan[i][:, d:E_], src[:, d:E_], src[:, 0:E_ - d], ALU.add).then_inc(done, 1)
                dve.wait_ge(done, 1)
                src = scan[i]
            shape = [P, NT, E_]
            nc.vector.tensor_tensor(past[:, :, :], src[:, :].unsqueeze(1).to_broadcast(shape),
                                    c(C_TILE, NT).unsqueeze(2).to_broadcast(shape), ALU.is_le).then_inc(s.past_ok, 1)
            dve.wait_ge(s.past_ok, 1)
            dve.wait_ge(s.skip_ok, 1)
            nc.vector.tensor_tensor(jump[:, :, :], past[:, :, :], skip[:, :].unsqueeze(1).to_broadcast(shape), ALU.mult).then_inc(s.jump_ok, 1)
            nc.vector.tensor_reduce(expf[:, :], past[:, :, :], AX.X, ALU.add).then_inc(s.expf_ok, 1)
            dve.wait_ge(s.jump_ok, 1)
            nc.vector.tensor_reduce(rowf[:, :], jump[:, :, :], AX.X, ALU.add).then_inc(s.rowf_ok, 1)
            dve.wait_ge(s.rowf_ok, 1)
            nc.vector.scalar_tensor_tensor(out=rowg[:, :], in0=c(C_TILE, NT), scalar=float(P), in1=rowf[:, :],
                                           op0=ALU.mult, op1=ALU.add).then_inc(s.rowg_ok, 1)
            dve.wait_ge(s.rowg_ok, 1)
            nc.vector.tensor_copy(rowi[:, :], rowg[:, :]).then_inc(s.row_ok, 1)
            dve.wait_ge(s.expf_ok, 1)
            nc.vector.tensor_scalar(expi[:, :], expf[:, :], float(E_ - 1), None, ALU.min).then_inc(s.exp_ok, 1)

            def slot(r, u):
                k = u - L_UP
                if live(r, k):
                    need(dve, s.silu, r, k + 1)
                    need(dve, s.u_ok, r, k + 1)
                    need(dve, s.hT_ps, r, k - 1)
                    nc.vector.scalar_tensor_tensor(out=hf[:, k % 2, :], in0=sg[:, k % 2, :], scalar=1.0 / WS, in1=ps_u[k % 2][:, :],
                                                   op0=ALU.mult, op1=ALU.mult).then_inc(s.h_ok, 1)
                if live(r, u):
                    need(dve, s.x_hi, r, u + 1)
                    need(dve, s.y_ok, r, u - R + 1)
                    need(dve, s.dest_ok, r, u - R + 1)
                    nc.vector.tensor_copy(meta[:, u, :], xg[:, u, H:RW]).then_inc(s.meta_ok, 1)
                    nc.vector.tensor_tensor(xT_lo[:, u % 2, :, :], ps_x[:, 0:KC * P].rearrange("p (c s) -> p c s", c=KC),
                                            xT_hi[:, u % 2, :, :], ALU.subtract).then_inc(s.x_lo, 1)
                k = u - L_HT
                if live(r, k):
                    need(dve, s.h_hi, r, k + 1)
                    nc.vector.tensor_tensor(hT_lo[:, k % 2, :, :], ps_h[:, :].rearrange("p (f s) -> p f s", f=FC),
                                            hT_hi[:, k % 2, :, :], ALU.subtract).then_inc(s.h_lo, 1)
                k = u - L_DOWN
                if live(r, k):
                    need(dve, s.meta_ok, r, k + 1)
                    uses = r + k // R
                    if not isinstance(r, int) or uses > 0:
                        dve.wait_ge(sent[k % R], uses * 16)
                    nc.vector.tensor_copy(dest[:, k % R:k % R + 1], meta[:, k % R, 1:2]).then_inc(s.dest_ok, 1)

            rounds(dve, slot, LAST)
            for b in range(B):
                dve.wait_ge(y_in[b % R], 16 * (b // R + 1))
                h = m.h_all[:, b, :]
                nc.vector.tensor_tensor(h, h, yy[:, b % R, 0, :], ALU.add).then_inc(s.sum0, 1)
                dve.wait_ge(s.sum0, b + 1)
                nc.vector.tensor_tensor(h, h, yy[:, b % R, 1, :], ALU.add).then_inc(s.sum1, 1)

        @block.gpsimd
        def _(pool):
            def slot(r, u):
                k = u - L_DOWN
                if live(r, k):
                    need(pool, s.y_ok, r, k + 1)
                    need(pool, s.dest_ok, r, k + 1)
                    need(pool, s.marked, r, k)
                    nc.gpsimd.tensor_tensor(pmark[:, 0:1], m.ident[:, 0:1], m.ident[:, 0:1], ALU.mult).then_inc(s.marked, 1)
                    nc.gpsimd.indirect_dma_start(out=m.ybuf[:, :], out_offset=bass.IndirectOffsetOnAxis(ap=dest[:, k % R:k % R + 1], axis=0),
                                                 in_=y[:, k % R, :], in_offset=None).then_inc(sent[k % R], 16)

            rounds(pool, slot, LAST)


def build(nc: bass.Bass, x, ctxT, wunit, wpunit, wup, wdown, gateT, tri, pads, cst, eye, out):
    fp32, f16 = mybir.dt.float32, mybir.dt.float16
    with ExitStack() as es:
        def sb(name, shape, dt=fp32):
            return es.enter_context(nc.sbuf_tensor(name, shape, dt))

        names = "h_all ident c_sb w_hi w_lo wp_hi wp_lo cntb rows ybuf"
        m = namedtuple("Memory", names)(
            sb("h_all", [P, B, H]),
            sb("ident", [P, P]),
            sb("c_sb", [P, NCST]),
            sb("w_hi", [P, NU, KC, QW + 2 * KW], f16),
            sb("w_lo", [P, NU, KC, QW + 2 * KW], f16),
            sb("wp_hi", [P, NU, UH, H], f16),
            sb("wp_lo", [P, NU, UH, H], f16),
            sb("cntb", [P, E_]),
            nc.dram_tensor("rows", (E_ * REG + SPARE * P, RW), fp32).ap(),
            nc.dram_tensor("ybuf", (K_TOP * T_ALL + (E_ + SPARE) * P, H), fp32).ap(),
        )
        attention(nc, m, x, ctxT, wunit, wpunit, wup, wdown, gateT, tri, pads, cst, eye)
        experts(nc, m, out)


def _layout(a):
    def chunks(w):
        o, i = w.shape
        return w.T.reshape(i // P, P, o).transpose(1, 0, 2)

    A = {k.replace("L0_xattn_", ""): np.asarray(v) for k, v in a.items()}
    kx, vx = A["w_kv_x"][:G * D], A["w_kv_x"][G * D:]
    units, outs = [], []
    wp = A["wproj"].T.reshape(2 * NH, P, H).transpose(1, 0, 2)
    for u in range(NU):
        j = u % HALF
        q, k, v = (A["wq"], A["wk"], A["wv"]) if u < HALF else (A["wqx"], kx, vx)
        w = np.concatenate([q[j * QW:(j + 1) * QW], k[j * KW:(j + 1) * KW], v[j * KW:(j + 1) * KW]], 0)
        units.append(chunks(w))
        outs.append(wp[:, u * UH:(u + 1) * UH])
    up = [np.concatenate([chunks(A["L0_ffn_w1"][e]).reshape(P, -1), chunks(A["L0_ffn_w3"][e]).reshape(P, -1)], 1) for e in range(E_)]
    down = [chunks(A["L0_ffn_w2"][e]).reshape(P, -1) for e in range(E_)]

    def cols(v):
        return v.reshape(-1, P).T
    cst = [cols(A["ln_w"]), cols(A["ln_b"])] + [cols(A[n + "_in_scale"]) for n in ("q", "k", "v", "qx")] + [cols(A["proj_smooth"])]
    cst += [cols(A[n]) for n in ("qln_w", "qln_b", "kln_w", "kln_b", "qxln_w", "qxln_b", "kxln_w", "kxln_b")]
    cst += [np.broadcast_to(A[n].reshape(1, 1), (P, 1)) for n in
            ("wq_scale", "wk_scale", "wv_scale", "wqx_scale", "proj_in_scale", "proj_w_scale")]
    def const(v):
        return np.broadcast_to(np.asarray(v, np.float32), (P, len(v)))
    dest = np.arange(K_TOP)[None, None] * T_ALL + np.arange(B)[None, :, None] * S + np.arange(P)[:, None, None]
    cst += [const(np.arange(E_)), const(np.arange(E_) * REG), const(np.arange(NT)), np.arange(P, dtype=np.float32)[:, None],
            dest.reshape(P, -1).astype(np.float32)]
    pads = np.zeros((E_ + SPARE, P, RW), np.float32)
    pads[:, :, H + 1] = K_TOP * T_ALL + np.arange((E_ + SPARE) * P).reshape(E_ + SPARE, P)
    return {
        "x": A["x"],
        "ctxT": A["ctx_2048"].transpose(0, 2, 1).reshape(B, KC, P, S).transpose(0, 2, 1, 3),
        "wunit": np.stack(units), "wpunit": np.stack(outs), "wup": np.stack(up), "wdown": np.stack(down),
        "gateT": chunks(A["L0_ffn_gate_w"]), "cst": np.concatenate(cst, 1),
        "eye": np.eye(P, dtype=np.float32), "tri": np.triu(np.ones((P, P), np.float32), 1), "pads": pads,
    }


def kernel(**inputs):
    import concourse.bacc as _bacc
    from concourse.bass_utils import run_bass_kernel_spmd as _run

    nc = _bacc.Bacc("TRN2", target_bir_lowering=False, num_devices=1)
    arrays, args = {}, {}
    for name, a in _layout(inputs).items():
        a = np.ascontiguousarray(a)
        arrays[f"in_{name}"] = a
        args[name] = nc.dram_tensor(f"in_{name}", a.shape, mybir.dt.from_np(a.dtype), kind="ExternalInput").ap()
    args["out"] = nc.dram_tensor("out_0", (B, S, H), mybir.dt.float32, kind="ExternalOutput").ap()
    build(nc, **args)
    r = _run(nc, [arrays], core_ids=[0])
    return r.results[0]["out_0"]
```

```python
import numpy as np
import concourse.bass as bass
from concourse import mybir
from collections import namedtuple
from contextlib import ExitStack

B, S, H = 16, 128, 256
D, NH, G = 128, 16, 8
E_, F_ = 8, 512
P = 128
KC = H // P
UH = 4
UG = UH * G // NH
HALF = NH // UH
NU = 2 * HALF
QW, KW = UH * D, UG * D
NL = UH + UG
LW = NL * D
CORE, CROSS = 0, 1
R_SUM, R_STAT, R_T, R_LOGIT, R_TOP, R_RANK, R_PLACE, R_SEND0, R_SEND1 = 7, 0, 1, 2, 3, 4, 5, 5, 6
U_XQX, U_XT = 2, 3
L_NORM, L_QKT, L_SCORE, L_PT, L_HEAD, L_QUANT, L_OUT = 1, 2, 4, 5, 6, 7, 8
LEAD = 3
W_OUT = 6
PADS_SP = 4
PEELED = 3
FC = F_ // P
T_ALL = B * S
K_TOP = 2
REG = T_ALL + P
NT = K_TOP * T_ALL // P + E_ - 1
SPARE = E_ - 1
RW = H + 2
EPS = 1e-5
FP8_MAX = 448.0
FP8_TINY = 2.0 ** -6
SCORE = float(1.0 / np.sqrt(D))
WS = 16.0

C_LNW, C_LNB, C_IN, C_SMOOTH = 0, KC, 2 * KC, 2 * KC + 4 * KC
C_LN = C_SMOOTH + 2 * NH
C_S = C_LN + 8
C_E = C_S + 6
C_BASE = C_E + E_
C_TILE = C_BASE + E_
C_DEST = C_TILE + NT
NCST = C_DEST + B * K_TOP
V_Q, V_K, V_V, V_QX = range(4)


def attention(nc: bass.Bass, m, x, ctxT, wunit, wpunit, wup, wdown, gateT, tri, pads, cst, eye):
    h_all, ident, c_sb, w_hi, w_lo, wp_hi, wp_lo, cntb = m.h_all, m.ident, m.c_sb, m.w_hi, m.w_lo, m.wp_hi, m.wp_lo, m.cntb

    def w_whole(u):
        if u == NU - 1:
            return w_raw[:, 0, :, :]
        return m.w_parts[:, u + 1, :, :, :].rearrange("p t c n -> p (t c n)").bitcast(fp32).rearrange("p (c n) -> p c n", c=KC)

    def wp_whole(u):
        if u == NU - 1:
            return wp_raw[:, 0, :, :]
        return m.wp_parts[:, u + 1, :, :, :].rearrange("p t c n -> p (t c n)").bitcast(fp32).rearrange("p (c n) -> p c n", c=UH)

    def down_whole(e):
        if 2 <= e < 6:
            return w_raw[:, (e - 2) // 2, e % 2, :]
        return wp_raw[:, e % 2, :, :].rearrange("p c n -> p (c n)")

    def parts(u):
        return [(V_QX, 0, QW), (None, QW, 2 * KW)] if u >= HALF else [(V_Q, 0, QW), (V_K, QW, KW), (V_V, QW + KW, KW)]
    fp32, f16, bf16, u16 = mybir.dt.float32, mybir.dt.float16, mybir.dt.bfloat16, mybir.dt.uint16
    u32, i32 = mybir.dt.uint32, mybir.dt.int32
    ALU, ACT, AX = mybir.AluOpType, mybir.ActivationFunctionType, mybir.AxisListType

    with ExitStack() as es:
        def sb(name, shape, dt=fp32):
            return es.enter_context(nc.sbuf_tensor(name, shape, dt))

        def ps(name, shape, dt=fp32):
            return es.enter_context(nc.psum_tensor(name, shape, dt))

        def sem(name):
            return es.enter_context(nc.semaphore(name))

        mark = sb("mark", [P, 1])
        amark = sb("amark", [P, 1])
        pmark = sb("pmark", [P, K_TOP])
        rin = sb("rin", [P, 4 * KC])
        rsm = sb("rsm", [P, 2 * NH])
        ws = sb("ws", [P, 2, NL])
        epsw = sb("epsw", [P, 2, NL])
        neghalf = sb("neghalf", [P, NL])
        psc = sb("psc", [P, 1])
        w_raw = sb("w_raw", [P, 2, KC, QW + 2 * KW])
        wp_raw = sb("wp_raw", [P, 2, UH, H])
        w_sum = sb("w_sum", [P, NU, KC * NL])
        w_mean = sb("w_mean", [P, NU, KC * NL])
        xst = sb("xst", [P, 6])
        xmv = sb("xmv", [P, 2])
        xr = sb("xr", [P, 2])
        xc = sb("xc", [P, H])
        tT = sb("tT", [P, KC, P])
        xy = sb("xy", [P, 3 * KC, P])
        xyb = sb("xyb", [P, 3 * KC, P], bf16)
        xm = sb("xm", [P, 3 * KC, P], bf16)
        xs = sb("xs", [P, 3 * KC, P], bf16)
        xq = sb("xq", [P, 4, KC, P], bf16)
        ctx_raw = sb("ctx_raw", [P, KC, P])
        ctx_hi = sb("ctx_hi", [P, KC, P], f16)
        ctx_lo = sb("ctx_lo", [P, KC, P], f16)
        work = sb("work", [P, 4 * LW])
        raw = work[:, 0:2 * LW].rearrange("p (a n) -> p a n", a=2)
        qn = work[:, 2 * LW:].rearrange("p (a n) -> p a n", a=2)
        sq = sb("sq", [P, LW])
        ssum = sb("ssum", [P, NL])
        svar = sb("svar", [P, NL])
        sfac = sb("sfac", [P, NL])
        vv = sb("vv", [P, NU, KW])
        qkT = sb("qkT", [P, 2, LW])
        smax = sb("smax", [P, 2, UH])
        nmax = sb("nmax", [P, 2, UH])
        esum = sb("esum", [P, 2, UH])
        rinv = sb("rinv", [P, 2, UH])
        pp = sb("pp", [P, 2, UH, P])
        pT = sb("pT", [P, 2, UH, P])
        y32 = sb("y32", [P, 2, UH, P])
        yb = sb("yb", [P, UH * P], bf16)
        ym = sb("ym", [P, UH * P], bf16)
        ya = sb("ya", [P, UH * P], bf16)
        catq = sb("catq", [P, 2, UH * P], bf16)

        gate = sb("gate", [P, KC, E_])
        upper32 = sb("upper32", [P, P])
        upper = sb("upper", [P, P], bf16)
        ones = sb("ones", [P, P], bf16)
        hst = sb("hst", [P, 6])
        hmv = sb("hmv", [P, 2])
        hr = sb("hr", [P, 2])
        row = sb("row", [P, K_TOP, RW])
        x2T = sb("x2T", [P, KC, P])
        lg = sb("lg", [P, E_])
        top = sb("top", [P, 8])
        topi = sb("topi", [P, 8], u32)
        topf = sb("topf", [P, 8])
        dl = sb("dl", [P, 1])
        ed = sb("ed", [P, 1])
        den = sb("den", [P, 1])
        pr = sb("pr", [P, K_TOP])
        chosen = sb("chosen", [P, K_TOP, E_])
        member = sb("member", [P, E_], bf16)
        rank = sb("rank", [P, 2, E_])
        place = sb("place", [P, E_])
        placed = sb("placed", [P, K_TOP, E_])
        posf = sb("posf", [P, K_TOP])
        posi = sb("posi", [P, K_TOP], i32)
        padi = sb("padi", [P, E_], i32)
        cnt = sb("cnt", [P, E_])
        half = sb("half", [P, E_])
        tiles = sb("tiles", [P, E_])
        scan = [sb(f"scan{i}", [P, E_]) for i in range(3)]
        skip = sb("skip", [P, E_])
        expf = sb("expf", [P, NT])
        rowf = sb("rowf", [P, NT])
        rowg = sb("rowg", [P, NT])
        past = sq[:, 0:NT * E_].rearrange("p (t e) -> p t e", e=E_)
        jump = sq[:, NT * E_:2 * NT * E_].rearrange("p (t e) -> p t e", e=E_)
        tail = sb("tail", [P, K_TOP, 2])

        ps_q = ps("ps_q", [P, 512])
        ps_kv = ps("ps_kv", [P, 512])
        ps_qT = ps("ps_qT", [P, 512])
        ps_kT = ps("ps_kT", [P, 512])
        ps_s = ps("ps_s", [P, 512])
        ps_pT = ps("ps_pT", [P, 512])
        ps_o = ps("ps_o", [P, 512])
        ps_y = ps("ps_y", [P, 512])

        names = ("half_ok warmed c_in x0_in x_in wp_in ctx_in setup rsm_ok wsummed wmeaned wcentred w_hi_ok w_lo_ok wp_hi_ok wp_lo_ok "
                 "xstat xmean xvar xfac xc_ok xT_ok tT_ok xdiv xclip xmask xmagic xadd xq_core xq_cross "
                 "ctx_hi_ok ctx_ok proj copied squared summed var fac normed qkT_ps qkT_ok "
                     "scores maxed negmax exped inverted probs pT_ps pT_ok heads y_ok clipped masked magic added catq_ok "
                     "attn h_ok r_in h_st h_mv h_var h_fac x2_ok x2_copied x2T_ps x2T_ok lg_ps lg_ok top_ok topi_ok topf_ok dl_ok ed_ok "
                 "den_ok p0_ok p1_ok chosen_ok member_ok rank_ps rank_ok place_ok count_ok placed_ok posf_ok pos_ok "
                 "cnt_ok halved tiles_ok scan0 scan1 scan2 skip_ok past_ok jump_ok expf_ok rowf_ok rowg_ok exp_ok row_ok "
                 "tail_ok tail0 tail1 sent0 sent1 padi_ok pads_sent pads_sent1 spare_in "
                 "xw_in0 xw_in1 xw_hi xw_lo xp_hi xp_lo"
                 ).split()
        s = namedtuple("Semaphores", names)(*[sem(name) for name in names])
        w_in = [sem(f"w_in{u}") for u in range(NU)]

        def need(eng, sm, b, k):
            if isinstance(b, int):
                if NU * b + k > 0:
                    eng.wait_ge(sm, min(NU * b + k, NU * B))
            else:
                eng.wait_ge(sm, b * NU + k)

        def need_b(eng, sm, b, k=0, per=1):
            if isinstance(b, int):
                if per * (b + k) > 0:
                    eng.wait_ge(sm, per * (b + k))
            else:
                eng.wait_ge(sm, b * per + per * k)

        def live(b, k):
            return not isinstance(b, int) or 0 <= NU * b + k < B * NU

        def has(b):
            return not isinstance(b, int) or 0 <= b < B

        def batches(eng, slot):
            for b in range(PEELED):
                for u in range(NU):
                    slot(b, u)
            with eng.Fori(PEELED, B - 1) as b:
                for u in range(NU):
                    slot(b, u)
            for n in range(NU * (B - 1), NU * (B + 1) + R_SEND1 + 1):
                slot(n // NU, n % NU)

        block = es.enter_context(nc.Block())

        @block.sync
        def _(sp):
            sp.dma_start(c_sb[:, :], cst[:, :]).then_inc(s.c_in, 16)
            sp.dma_start(ident[:, :], eye[:, :]).then_inc(s.c_in, 16)
            sp.dma_start(h_all[:, 0, :], x[0]).then_inc(s.x0_in, 16)
            for u in range(NU):
                sp.dma_start(w_whole(u), wunit[u]).then_inc(w_in[u], 16)
                if u == 1:
                    sp.dma_start(ctx_raw[:, :, :], ctxT[0]).then_inc(s.ctx_in, 16)
                    sp.dma_start(gate[:, :, :], gateT[:, :, :]).then_inc(s.r_in, 16)
                    sp.dma_start(upper32[:, :], tri[:, :]).then_inc(s.r_in, 16)
                if u == 4:
                    sp.dma_start(h_all[:, 1:, :], x[1:].rearrange("b p i -> p b i")).then_inc(s.x_in, 16)
            for u in range(NU):
                sp.dma_start(wp_whole(u), wpunit[u]).then_inc(s.wp_in, 16)
            sp.dma_start(m.rows[E_ * REG:, :], pads[E_:].rearrange("t p r -> (t p) r")).then_inc(s.spare_in, 16)

            def expert_up(e):
                sp.dma_start(w_raw[:, e % 2, :, :].rearrange("p c n -> p (c n)"), wup[e]).then_inc((s.xw_in0, s.xw_in1)[e % 2], 16)

            def expert_down(e):
                sp.dma_start(down_whole(e), wdown[e]).then_inc(w_in[e], 16)

            sp.wait_ge(s.ctx_ok, 1)
            sp.dma_start(ctx_raw[:, :, :], ctxT[1]).then_inc(s.ctx_in, 16)
            sp.wait_ge(s.w_lo_ok, NU)
            sp.wait_ge(s.wp_lo_ok, NU)
            for e in range(2):
                expert_up(e)
                expert_down(e)
            with sp.Fori(2, B) as b:
                sp.wait_ge(s.ctx_ok, b)
                sp.dma_start(ctx_raw[:, :, :], ctxT[b]).then_inc(s.ctx_in, 16)
            for e in range(2, E_):
                sp.wait_ge(s.xw_lo, e - 1)
                expert_up(e)
            for e in range(2, E_):
                if e < 6:
                    sp.wait_ge(s.xw_lo, E_ - 1 + (e - 2) // 2)
                else:
                    sp.wait_ge(s.xp_lo, e - 5)
                expert_down(e)
            sp.wait_ge(s.padi_ok, 1)
            for e in range(PADS_SP):
                start = sp.value_load(padi[0:1, e:e + 1], min_val=0, max_val=E_ * REG - P)
                sp.dma_start(m.rows[bass.ds(start, P), :], pads[e]).then_inc(s.pads_sent, 16)
            sp.wait_ge(s.pads_sent, 16 * PADS_SP)
            sp.wait_ge(s.spare_in, 16)

        @block.tensor
        def _(pe):
            def input_transposed(bx):
                need_b(pe, s.xc_ok, bx, 1)
                for c in range(KC):
                    last = nc.tensor.transpose(ps_kT[:, KW + c * P:KW + (c + 1) * P], xc[:, c * P:(c + 1) * P], ident[:, :])
                last.then_inc(s.xT_ok, 1)

            def routing(b, u):
                if u == R_T and has(b - 2):
                    need(pe, s.qkT_ok, b, u - L_QKT)
                    need_b(pe, s.x2_ok, b, -1)
                    for c in range(KC):
                        last = nc.tensor.transpose(ps_kT[:, KW + c * P:KW + (c + 1) * P], row[:, 0, c * P:(c + 1) * P], ident[:, :])
                    last.then_inc(s.x2T_ps, 1)
                if u == R_LOGIT and has(b - 2):
                    need_b(pe, s.x2T_ok, b, -1)
                    for c in range(KC):
                        last = nc.tensor.matmul(ps_kT[:, KW:KW + E_], x2T[:, c, :], gate[:, c, :], start=(c == 0), stop=(c == KC - 1))
                    last.then_inc(s.lg_ps, 1)
                if u == R_LOGIT + 1 and has(b - 2):
                    need_b(pe, s.lg_ok, b, -1)
                if u == R_RANK and has(b - 2):
                    need_b(pe, s.member_ok, b, -1)
                    nc.tensor.matmul(ps_kT[:, KW:KW + E_], upper[:, :], member[:, :], start=True, stop=True)
                    nc.tensor.matmul(ps_kT[:, KW + E_:KW + 2 * E_], ones[:, :], member[:, :], start=True, stop=True).then_inc(s.rank_ps, 1)
                if u == R_RANK + 1 and has(b - 2):
                    need_b(pe, s.rank_ok, b, -1)

            def slot(b, u):
                k = u - L_SCORE
                if live(b, k):
                    need(pe, s.qkT_ok, b, k + 1)
                    need(pe, s.exped, b, k)
                    for j in range(UH):
                        kv = QW + (j // (UH // UG)) * D
                        last = nc.tensor.matmul(ps_s[:, j * P:(j + 1) * P], qkT[:, k % 2, j * P:(j + 1) * P],
                                                qkT[:, k % 2, kv:kv + P], start=True, stop=True)
                    last.then_inc(s.scores, 1)
                if live(b, u):
                    if isinstance(b, int) and b == 0:
                        pe.wait_ge(s.w_hi_ok, u + 1)
                        pe.wait_ge(s.w_lo_ok, u + 1)
                    if u == 0:
                        need_b(pe, s.xq_core, b, 1)
                    if u == HALF:
                        need_b(pe, s.xq_cross, b, 1)
                        need_b(pe, s.ctx_ok, b, 1)
                    need(pe, s.copied, b, u)
                    cross = u >= HALF
                    def project(dst, version, lo, w):
                        for c in range(KC):
                            for half, wt in enumerate((w_hi, w_lo)):
                                last = nc.tensor.matmul(dst, xq[:, version, c, :], wt[:, u, c, lo:lo + w],
                                                        start=(c == 0 and half == 0), stop=(c == KC - 1 and half == 1))
                        return last
                    last = project(ps_q[:, :], V_QX if cross else V_Q, 0, QW)
                    if not cross:
                        project(ps_kv[:, 0:KW], V_K, QW, KW)
                        last = project(ps_kv[:, KW:2 * KW], V_V, QW + KW, KW)
                    else:
                        for c in range(KC):
                            for i, (a, w) in enumerate(((ctx_hi, w_hi), (ctx_hi, w_lo), (ctx_lo, w_hi))):
                                last = nc.tensor.matmul(ps_kv[:, :], a[:, c, :], w[:, u, c, QW:QW + 2 * KW],
                                                        start=(c == 0 and i == 0), stop=(c == KC - 1 and i == 2))
                    last.then_inc(s.proj, 1)
                k = u - L_PT
                if live(b, k):
                    need(pe, s.probs, b, k + 1)
                    need(pe, s.pT_ok, b, k)
                    for j in range(UH):
                        last = nc.tensor.transpose(ps_pT[:, j * P:(j + 1) * P], pp[:, k % 2, j, :], ident[:, :])
                    last.then_inc(s.pT_ps, 1)
                k = u - L_QKT
                if live(b, k):
                    need(pe, s.normed, b, k + 1)
                    need(pe, s.qkT_ok, b, k)
                    if u == 2 and isinstance(b, int) and b == 0:
                        need_b(pe, s.tT_ok, 0, 1)
                    if u == U_XT + 1 and has(b + 1):
                        need_b(pe, s.tT_ok, b, 2)
                    routing(b, u)
                    if u == U_XT and has(b + 1):
                        input_transposed(b + 1)
                    for j in range(NL):
                        dst = ps_qT[:, j * P:(j + 1) * P] if j < UH else ps_kT[:, (j - UH) * P:(j - UH + 1) * P]
                        last = nc.tensor.transpose(dst, qn[:, k % 2, j * P:(j + 1) * P], ident[:, :])
                    last.then_inc(s.qkT_ps, 1)
                else:
                    routing(b, u)
                k = u - L_OUT
                if live(b, k):
                    uu = k % NU
                    need(pe, s.catq_ok, b, k + 1)
                    if isinstance(b, int) and NU * b + k < NU:
                        pe.wait_ge(s.wp_lo_ok, uu + 1)
                    if uu == 0:
                        need_b(pe, s.h_ok, b, -1)
                    for j in range(UH):
                        for half, wt in enumerate((wp_hi, wp_lo)):
                            last = nc.tensor.matmul(ps_y[:, 0:H], catq[:, k % 2, j * P:(j + 1) * P], wt[:, uu, j, :],
                                                    start=(uu == 0 and j == 0 and half == 0),
                                                    stop=(uu == NU - 1 and j == UH - 1 and half == 1))
                    last.then_inc(s.attn, 1)
                k = u - L_HEAD
                if live(b, k):
                    need(pe, s.pT_ok, b, k + 1)
                    need(pe, s.copied, b, k + 1)
                    need(pe, s.y_ok, b, k)
                    per = UH // UG
                    for g in range(UG):
                        last = nc.tensor.matmul(ps_o[:, g * per * P:(g + 1) * per * P], vv[:, k % NU, g * D:(g + 1) * D],
                                                pT[:, k % 2, g * per:(g + 1) * per, :], start=True, stop=True)
                    last.then_inc(s.heads, 1)

            pe.wait_ge(s.c_in, 32)
            pe.wait_ge(s.r_in, 32)
            input_transposed(0)
            batches(pe, slot)

        @block.scalar
        def _(act):
            def col(i):
                return c_sb[:, i:i + 1]

            def input_evacuated(bx):
                need_b(act, s.xT_ok, bx, 1)
                need_b(act, s.xdiv, bx, 0, 2)
                for c in range(KC):
                    last = nc.scalar.activation(tT[:, c, :], ps_kT[:, KW + c * P:KW + (c + 1) * P], ACT.Identity,
                                                bias=col(C_LNB + c), scale=col(C_LNW + c))
                last.then_inc(s.tT_ok, 1)

            def high_parts(u):
                act.wait_ge(s.wcentred, u + 1)
                if u > 0:
                    act.wait_ge(s.w_lo_ok, u)
                for v, lo, w in parts(u):
                    if v is None:
                        last = nc.scalar.activation(w_hi[:, u, :, lo:lo + w], w_whole(u)[:, :, lo:lo + w], ACT.Copy)
                        continue
                    for c in range(KC):
                        last = nc.scalar.activation(w_hi[:, u, c, lo:lo + w], w_whole(u)[:, c, lo:lo + w], ACT.Copy,
                                                    scale=col(C_IN + v * KC + c))
                last.then_inc(s.w_hi_ok, 1)

            def output_high_parts(u):
                act.wait_ge(s.wp_in, 16 * NU)
                if u > 0:
                    act.wait_ge(s.wp_lo_ok, u)
                nc.scalar.activation(wp_hi[:, u, :, :], wp_whole(u), ACT.Copy).then_inc(s.wp_hi_ok, 1)

            def expert_high_parts(n):
                e = n - NU * (B - 1) - 1
                if 0 <= e < E_:
                    act.wait_ge((s.xw_in0, s.xw_in1)[e % 2], 16 * (e // 2 + 1))
                    act.wait_ge(s.proj, NU * (B - 1) + e + 1)
                    nc.scalar.activation(w_hi[:, e, :, :], w_raw[:, e % 2, :, :], ACT.Copy, scale=WS).then_inc(s.xw_hi, 1)
                e -= L_OUT
                if 0 <= e < E_:
                    act.wait_ge(w_in[e], 32)
                    act.wait_ge(s.attn, NU * (B - 1) + e + 1)
                    nc.scalar.activation(wp_hi[:, e, :, :].rearrange("p c n -> p (c n)"), down_whole(e), ACT.Copy, scale=WS).then_inc(s.xp_hi, 1)

            def routing(b, u):
                if u == R_T and has(b - 2):
                    need_b(act, s.x2T_ps, b, -1)
                    nc.scalar.activation(x2T[:, :, :], ps_kT[:, KW:KW + KC * P].rearrange("p (c s) -> p c s", c=KC),
                                         ACT.Copy).then_inc(s.x2T_ok, 1)
                    need_b(act, s.sent1, b, -2, 16)
                    nc.scalar.activation(row[:, 1, 0:H], row[:, 0, 0:H], ACT.Copy).then_inc(s.x2_copied, 1)
                if u == R_LOGIT and has(b - 2):
                    need_b(act, s.lg_ps, b, -1)
                    nc.scalar.activation(lg[:, :], ps_kT[:, KW:KW + E_], ACT.Copy).then_inc(s.lg_ok, 1)
                if u == R_RANK and has(b - 2):
                    need_b(act, s.rank_ps, b, -1)
                    nc.scalar.activation(rank[:, :, :].rearrange("p a e -> p (a e)"), ps_kT[:, KW:KW + 2 * E_], ACT.Copy).then_inc(s.rank_ok, 1)
                    need_b(act, s.dl_ok, b, -1)
                    nc.scalar.activation(ed[:, :], dl[:, :], ACT.Exp).then_inc(s.ed_ok, 1)
                if u == R_SEND0 and has(b - 2):
                    need_b(act, s.tail_ok, b, -1)
                    nc.scalar.activation(row[:, 0, H:RW], tail[:, 0, :], ACT.Copy).then_inc(s.tail0, 1)
                if u == R_SEND1 and has(b - 2):
                    nc.scalar.activation(row[:, 1, H:RW], tail[:, 1, :], ACT.Copy).then_inc(s.tail1, 1)
                if isinstance(b, int) and (b, u) == (B + 1, R_PLACE + 1):
                    act.wait_ge(s.padi_ok, 1)
                    for e in range(PADS_SP, E_):
                        start = act.value_load(padi[0:1, e:e + 1], min_val=0, max_val=E_ * REG - P)
                        act.dma_start(m.rows[bass.ds(start, P), :], pads[e]).then_inc(s.pads_sent1, 16)

            def slot(b, u):
                if isinstance(b, int) and b == 0 and u + 1 < NU:
                    high_parts(u + 1)
                if u == 1 and live(b, 0):
                    need_b(act, s.ctx_in, b, 1, 16)
                    need(act, s.proj, b, 0)
                    nc.scalar.activation(ctx_hi[:, :, :], ctx_raw[:, :, :], ACT.Copy).then_inc(s.ctx_hi_ok, 1)
                k = u - L_SCORE
                if live(b, k):
                    need(act, s.negmax, b, k + 1)
                    need(act, s.pT_ps, b, k - 1)
                    for j in range(UH):
                        last = nc.scalar.activation(pp[:, k % 2, j, :], ps_s[:, j * P:(j + 1) * P], ACT.Exp,
                                                    bias=nmax[:, k % 2, j:j + 1], scale=SCORE,
                                                    accum_out=esum[:, k % 2, j:j + 1])
                    last.then_inc(s.exped, 1)
                if live(b, u):
                    need(act, s.proj, b, u + 1)
                    need(act, s.normed, b, u - 1)
                    need(act, s.squared, b, u - 1)
                    need(act, s.heads, b, u - NU + 1)
                    nc.scalar.activation(raw[:, u % 2, 0:QW], ps_q[:, :], ACT.Copy)
                    nc.scalar.activation(raw[:, u % 2, QW:LW], ps_kv[:, 0:KW], ACT.Copy)
                    nc.scalar.activation(vv[:, u, :], ps_kv[:, KW:2 * KW], ACT.Copy).then_inc(s.copied, 1)
                k = u - L_PT
                if live(b, k):
                    need(act, s.pT_ps, b, k + 1)
                    need(act, s.heads, b, k - 1)
                    nc.scalar.activation(pT[:, k % 2, :, :], ps_pT[:, :], ACT.Copy).then_inc(s.pT_ok, 1)
                k = u - L_QKT
                if live(b, k):
                    o = C_LN + 4 * (1 if k % NU >= HALF else 0)
                    need(act, s.qkT_ps, b, k + 1)
                    need(act, s.scores, b, k - 1)
                    nc.scalar.activation(qkT[:, k % 2, 0:QW], ps_qT[:, :], ACT.Identity, bias=col(o + 1), scale=col(o))
                    nc.scalar.activation(qkT[:, k % 2, QW:LW], ps_kT[:, 0:KW], ACT.Identity, bias=col(o + 3),
                                         scale=col(o + 2)).then_inc(s.qkT_ok, 1)
                    if u == U_XT and has(b + 1):
                        input_evacuated(b + 1)
                routing(b, u)
                k = u - L_HEAD
                if live(b, k):
                    need(act, s.heads, b, k + 1)
                    need(act, s.clipped, b, k - 1)
                    for j in range(UH):
                        h = (k % NU) * UH + j
                        last = nc.scalar.activation(y32[:, k % 2, j, :], ps_o[:, j * P:(j + 1) * P], ACT.Copy,
                                                    scale=rsm[:, h:h + 1])
                    last.then_inc(s.y_ok, 1)
                if isinstance(b, int) and 0 <= NU * b + u - W_OUT < NU:
                    output_high_parts(NU * b + u - W_OUT)
                if isinstance(b, int):
                    expert_high_parts(NU * b + u)

            act.wait_ge(s.half_ok, 1)
            nc.scalar.activation(amark[:, :], neghalf[:, 0:1], ACT.Exp).then_inc(s.warmed, 1)
            act.wait_ge(s.c_in, 32)
            act.wait_ge(s.rsm_ok, 2)
            input_evacuated(0)
            high_parts(0)
            batches(act, slot)
            act.wait_ge(s.pads_sent1, 16 * (E_ - PADS_SP))

        @block.vector
        def _(dve):
            def col(i):
                return c_sb[:, i:i + 1]

            def weights(u):
                dve.wait_ge(w_in[u], 16)
                for c in range(KC):
                    last = nc.vector.tensor_reduce(w_sum[:, u, c * NL:(c + 1) * NL],
                                                   w_whole(u)[:, c, 0:LW].rearrange("p (h d) -> p h d", d=D), AX.X, ALU.add)
                last.then_inc(s.wsummed, 1)
                dve.wait_ge(s.wsummed, u + 1)
                nc.vector.tensor_scalar(w_mean[:, u, :], w_sum[:, u, :], 1.0 / D, None, ALU.mult).then_inc(s.wmeaned, 1)

            def low_parts(u):
                dve.wait_ge(s.w_hi_ok, u + 1)
                for v, lo, w in parts(u):
                    if v is None:
                        last = nc.vector.tensor_tensor(w_lo[:, u, :, lo:lo + w], w_whole(u)[:, :, lo:lo + w],
                                                       w_hi[:, u, :, lo:lo + w], ALU.subtract)
                        continue
                    for c in range(KC):
                        last = nc.vector.scalar_tensor_tensor(out=w_lo[:, u, c, lo:lo + w], in0=w_whole(u)[:, c, lo:lo + w],
                                                              scalar=col(C_IN + v * KC + c), in1=w_hi[:, u, c, lo:lo + w],
                                                              op0=ALU.mult, op1=ALU.subtract)
                last.then_inc(s.w_lo_ok, 1)

            def output_low_parts(u):
                dve.wait_ge(s.wp_hi_ok, u + 1)
                nc.vector.tensor_tensor(wp_lo[:, u, :, :], wp_whole(u), wp_hi[:, u, :, :], ALU.subtract).then_inc(s.wp_lo_ok, 1)

            def expert_low_parts(n):
                e = n - NU * (B - 1) - 1
                if 0 <= e < E_:
                    dve.wait_ge(s.xw_hi, e + 1)
                    nc.vector.scalar_tensor_tensor(out=w_lo[:, e, :, :], in0=w_raw[:, e % 2, :, :], scalar=WS, in1=w_hi[:, e, :, :],
                                                   op0=ALU.mult, op1=ALU.subtract).then_inc(s.xw_lo, 1)
                e -= L_OUT
                if 0 <= e < E_:
                    dve.wait_ge(s.xp_hi, e + 1)
                    nc.vector.scalar_tensor_tensor(out=wp_lo[:, e, :, :].rearrange("p c n -> p (c n)"), in0=down_whole(e), scalar=WS,
                                                   in1=wp_hi[:, e, :, :].rearrange("p c n -> p (c n)"),
                                                   op0=ALU.mult, op1=ALU.subtract).then_inc(s.xp_lo, 1)

            def statistics(b):
                need_b(dve, s.h_ok, b, 0)
                nc.vector.memset(mark[:, :], 0.0)
                nc.vector.bn_stats(hst[:, :], h_all[:, b - 1, :]).then_inc(s.h_st, 1)
                need_b(dve, s.h_st, b, 0)
                nc.vector.memset(mark[:, :], 0.0)
                nc.vector.bn_aggr(hmv[:, :], hst[:, :]).then_inc(s.h_mv, 1)
                need_b(dve, s.h_mv, b, 0)
                nc.vector.tensor_scalar(hr[:, 0:1], hmv[:, 1:2], EPS, None, ALU.add).then_inc(s.h_var, 1)

            def choice(b):
                need_b(dve, s.lg_ok, b, -1)
                nc.vector.memset(mark[:, :], 0.0)
                nc.vector.max(top[:, :], lg[:, :]).then_inc(s.top_ok, 1)
                need_b(dve, s.top_ok, b, -1)
                need_b(dve, s.ed_ok, b, -2)
                nc.vector.tensor_tensor(dl[:, :], top[:, 1:2], top[:, 0:1], ALU.subtract).then_inc(s.dl_ok, 1)
                nc.vector.max_index(topi[:, :], top[:, :], lg[:, :]).then_inc(s.topi_ok, 1)
                need_b(dve, s.topi_ok, b, -1)
                nc.vector.tensor_copy(topf[:, :], topi[:, :]).then_inc(s.topf_ok, 1)
                need_b(dve, s.topf_ok, b, -1)
                shape = [P, K_TOP, E_]
                nc.vector.tensor_tensor(chosen[:, :, :], topf[:, 0:K_TOP].unsqueeze(2).to_broadcast(shape),
                                        c_sb[:, C_E:C_E + E_].unsqueeze(1).to_broadcast(shape), ALU.is_equal).then_inc(s.chosen_ok, 1)
                need_b(dve, s.chosen_ok, b, -1)
                nc.vector.tensor_tensor(member[:, :], chosen[:, 0, :], chosen[:, 1, :], ALU.add).then_inc(s.member_ok, 1)

            def placing(b):
                need_b(dve, s.rank_ok, b, -1)
                nc.vector.tensor_tensor(place[:, :], rank[:, 0, :], cntb[:, :], ALU.add).then_inc(s.place_ok, 1)
                need_b(dve, s.ed_ok, b, -1)
                nc.vector.tensor_scalar(den[:, :], ed[:, :], 1.0, WS, ALU.add, ALU.mult).then_inc(s.den_ok, 1)
                need_b(dve, s.place_ok, b, -1)
                nc.vector.tensor_tensor(cntb[:, :], cntb[:, :], rank[:, 1, :], ALU.add).then_inc(s.count_ok, 1)
                need_b(dve, s.den_ok, b, -1)
                nc.vector.reciprocal(pr[:, 0:1], den[:, :]).then_inc(s.p0_ok, 1)
                shape = [P, K_TOP, E_]
                nc.vector.tensor_tensor(placed[:, :, :], chosen[:, :, :], place[:, :].unsqueeze(1).to_broadcast(shape),
                                        ALU.mult).then_inc(s.placed_ok, 1)
                need_b(dve, s.p0_ok, b, -1)
                nc.vector.tensor_tensor(pr[:, 1:2], pr[:, 0:1], ed[:, :], ALU.mult).then_inc(s.p1_ok, 1)
                need_b(dve, s.placed_ok, b, -1)
                nc.vector.tensor_reduce(posf[:, :], placed[:, :, :], AX.X, ALU.add).then_inc(s.posf_ok, 1)
                need_b(dve, s.p1_ok, b, -1)
                need_b(dve, s.tail1, b, -2)
                nc.vector.tensor_copy(tail[:, :, 0], pr[:, :])
                dest = c_sb[:, C_DEST:C_DEST + B * K_TOP].rearrange("p (b k) -> p b k", k=K_TOP)
                nc.vector.tensor_copy(tail[:, :, 1], dest[:, b - 2, :]).then_inc(s.tail_ok, 1)
                need_b(dve, s.posf_ok, b, -1)
                need_b(dve, s.sent1, b, -2, 16)
                nc.vector.tensor_copy(posi[:, :], posf[:, :]).then_inc(s.pos_ok, 1)

            def input_statistics(bx):
                dve.wait_ge(s.x0_in if isinstance(bx, int) and bx == 0 else s.x_in, 16)
                nc.vector.bn_stats(xst[:, :], h_all[:, bx, :]).then_inc(s.xstat, 1)
                need_b(dve, s.xstat, bx, 1)
                nc.vector.memset(mark[:, :], 0.0)
                nc.vector.bn_aggr(xmv[:, :], xst[:, :]).then_inc(s.xmean, 1)
                need_b(dve, s.xmean, bx, 1)
                nc.vector.tensor_scalar(xr[:, 0:1], xmv[:, 1:2], 1.0 + EPS, EPS * EPS, ALU.mult, ALU.add).then_inc(s.xvar, 1)

            def input_normalised(bx):
                need_b(dve, s.xfac, bx, 1)
                need_b(dve, s.xT_ok, bx, 0)
                nc.vector.tensor_scalar(xc[:, :], h_all[:, bx, :], xmv[:, 0:1], xr[:, 1:2], ALU.subtract, ALU.mult).then_inc(s.xc_ok, 1)

            def input_quantised(bx, done, *steps):
                core = done is s.xq_core
                v, nv = (V_Q, 3) if core else (V_QX, 1)
                n = nv * KC

                def after(sm):
                    if isinstance(bx, int):
                        dve.wait_ge(sm, 2 * bx + (1 if core else 2))
                    else:
                        dve.wait_ge(sm, bx * 2 + (1 if core else 2))
                if 0 in steps:
                    need_b(dve, s.tT_ok, bx, 1)
                    scales = rin[:, v * KC:(v + nv) * KC].rearrange("p (v c) -> p v c", c=KC)
                    nc.vector.tensor_tensor(xy[:, 0:n, :].rearrange("p (v c) s -> p v c s", c=KC),
                                            tT[:, :, :].unsqueeze(1).to_broadcast([P, nv, KC, P]),
                                            scales.unsqueeze(3).to_broadcast([P, nv, KC, P]), ALU.mult).then_inc(s.xdiv, 1)
                if 1 in steps:
                    after(s.xdiv)
                    nc.vector.tensor_scalar(xyb[:, 0:n, :], xy[:, 0:n, :], FP8_MAX, -FP8_MAX, ALU.min, ALU.max).then_inc(s.xclip, 1)
                if 2 in steps:
                    after(s.xclip)
                    nc.vector.tensor_scalar(xm[:, 0:n, :].bitcast(u16), xyb[:, 0:n, :].bitcast(u16), 0x7F80, None,
                                            ALU.bitwise_and).then_inc(s.xmask, 1)
                if 3 in steps:
                    after(s.xmask)
                    nc.vector.tensor_scalar(xm[:, 0:n, :], xm[:, 0:n, :], FP8_TINY, 24.0, ALU.max, ALU.mult).then_inc(s.xmagic, 1)
                if 4 in steps:
                    after(s.xmagic)
                    nc.vector.tensor_tensor(xs[:, 0:n, :], xyb[:, 0:n, :], xm[:, 0:n, :], ALU.add).then_inc(s.xadd, 1)
                if 5 in steps:
                    after(s.xadd)
                    need(dve, s.proj, bx, HALF - NU if core else 0)
                    dst = (xq[:, 0:3, :, :] if core else xq[:, 3:4, :, :]).rearrange("p v c s -> p (v c) s")
                    nc.vector.tensor_tensor(dst, xs[:, 0:n, :], xm[:, 0:n, :], ALU.subtract).then_inc(done, 1)

            def inputs(b, u, place):
                if has(b):
                    if (u, place) == (0, 1):
                        input_quantised(b, s.xq_cross, 0)
                    if (u, place) == (0, 2):
                        input_quantised(b, s.xq_cross, 1)
                    if (u, place) == (1, 1):
                        input_quantised(b, s.xq_cross, 2)
                    if (u, place) == (2, 0):
                        input_quantised(b, s.xq_cross, 3)
                    if (u, place) == (2, 1):
                        input_quantised(b, s.xq_cross, 4)
                    if (u, place) == (2, 2):
                        input_quantised(b, s.xq_cross, 5)
                if has(b + 1):
                    if (u, place) == (U_XQX, 2):
                        input_statistics(b + 1)
                    if (u, place) == (4, 1):
                        input_quantised(b + 1, s.xq_core, 0)
                    if (u, place) == (4, 2):
                        input_quantised(b + 1, s.xq_core, 1)
                    if (u, place) == (5, 1):
                        input_quantised(b + 1, s.xq_core, 2)
                    if (u, place) == (6, 0):
                        input_quantised(b + 1, s.xq_core, 3)
                    if (u, place) == (6, 1):
                        input_quantised(b + 1, s.xq_core, 4)
                    if (u, place) == (7, 1):
                        input_quantised(b + 1, s.xq_core, 5)

            def slot(b, u):
                k = u - L_QKT
                if live(b, k):
                    need(dve, s.fac, b, k + 1)
                    need(dve, s.qkT_ps, b, k - 1)
                    nc.vector.tensor_tensor(qn[:, k % 2, :].rearrange("p (h d) -> p h d", d=D),
                                            raw[:, k % 2, :].rearrange("p (h d) -> p h d", d=D),
                                            sfac[:, :].unsqueeze(2).to_broadcast([P, NL, D]), ALU.mult).then_inc(s.normed, 1)
                inputs(b, u, 0)
                ko, ks, kv = u - L_QUANT, u - L_SCORE, u - L_NORM
                kind = CROSS if kv % NU >= HALF else CORE
                if live(b, ks):
                    need(dve, s.scores, b, ks + 1)
                    nc.vector.tensor_reduce(smax[:, ks % 2, :], ps_s[:, :].rearrange("p (h t) -> p h t", t=P), AX.X,
                                            ALU.max).then_inc(s.maxed, 1)
                if live(b, ks):
                    need(dve, s.maxed, b, ks + 1)
                    need(dve, s.exped, b, ks - 1)
                    nc.vector.tensor_scalar(nmax[:, ks % 2, :], smax[:, ks % 2, :], -SCORE, None, ALU.mult).then_inc(s.negmax, 1)
                if u == R_T and has(b - 2):
                    need_b(dve, s.h_fac, b, -1)
                    need_b(dve, s.sent0, b, -2, 16)
                    need_b(dve, s.x2_copied, b, -2)
                    need_b(dve, s.x2T_ps, b, -2)
                    nc.vector.tensor_scalar(row[:, 0, 0:H], h_all[:, b - 2, :], hmv[:, 0:1], hr[:, 1:2], ALU.subtract,
                                            ALU.mult).then_inc(s.x2_ok, 1)
                if u == U_XT and has(b + 1):
                    input_normalised(b + 1)
                if live(b, ko):
                    need(dve, s.y_ok, b, ko + 1)
                    nc.vector.tensor_scalar(yb[:, :], y32[:, ko % 2, :, :].rearrange("p h t -> p (h t)"), FP8_MAX, -FP8_MAX,
                                            ALU.min, ALU.max).then_inc(s.clipped, 1)
                if live(b, ko):
                    need(dve, s.clipped, b, ko + 1)
                    nc.vector.tensor_scalar(ym[:, :].bitcast(u16), yb[:, :].bitcast(u16), 0x7F80, None,
                                            ALU.bitwise_and).then_inc(s.masked, 1)
                if live(b, kv):
                    need(dve, s.squared, b, kv + 1)
                    nc.vector.tensor_reduce(ssum[:, :], sq[:, :].rearrange("p (h d) -> p h d", d=D), AX.X,
                                            ALU.add).then_inc(s.summed, 1)
                if live(b, ko):
                    need(dve, s.masked, b, ko + 1)
                    nc.vector.tensor_scalar(ym[:, :], ym[:, :], FP8_TINY, 24.0, ALU.max, ALU.mult).then_inc(s.magic, 1)
                if live(b, kv):
                    need(dve, s.summed, b, kv + 1)
                    need(dve, s.fac, b, kv)
                    nc.vector.scalar_tensor_tensor(out=svar[:, :], in0=ssum[:, :], scalar=1.0 / D, in1=epsw[:, kind, :],
                                                   op0=ALU.mult, op1=ALU.add).then_inc(s.var, 1)
                inputs(b, u, 1)
                if live(b, ko):
                    need(dve, s.magic, b, ko + 1)
                    nc.vector.tensor_tensor(ya[:, :], yb[:, :], ym[:, :], ALU.add).then_inc(s.added, 1)
                if live(b, ks):
                    need(dve, s.exped, b, ks + 1)
                    need(dve, s.probs, b, ks - 1)
                    nc.vector.reciprocal(rinv[:, ks % 2, :], esum[:, ks % 2, :]).then_inc(s.inverted, 1)
                if live(b, ko):
                    need(dve, s.added, b, ko + 1)
                    need(dve, s.attn, b, ko - 1)
                    nc.vector.tensor_tensor(catq[:, ko % 2, :], ya[:, :], ym[:, :], ALU.subtract).then_inc(s.catq_ok, 1)
                if u == R_SUM and has(b - 1):
                    need(dve, s.attn, b, 0)
                    h = h_all[:, b - 1, :]
                    nc.vector.scalar_tensor_tensor(out=h, in0=ps_y[:, 0:H], scalar=psc[:, :], in1=h,
                                                   op0=ALU.mult, op1=ALU.add).then_inc(s.h_ok, 1)
                if u == R_STAT and has(b - 2):
                    statistics(b - 1)
                if u == R_TOP and has(b - 2):
                    choice(b)
                if u == R_PLACE and has(b - 2):
                    placing(b)
                if isinstance(b, int) and (b, u) == (B + 1, R_PLACE):
                    dve.wait_ge(s.count_ok, B)
                    nc.vector.tensor_copy(padi[:, :], cntb[:, :]).then_inc(s.padi_ok, 1)
                inputs(b, u, 2)
                if isinstance(b, int) and 0 <= NU * b + u - W_OUT - 1 < NU:
                    output_low_parts(NU * b + u - W_OUT - 1)
                if isinstance(b, int):
                    expert_low_parts(NU * b + u - 1)
                if isinstance(b, int) and b == 0:
                    if u + 1 < NU:
                        low_parts(u + 1)
                    if u + LEAD < NU:
                        weights(u + LEAD)

            dve.wait_ge(s.c_in, 32)
            nc.vector.reciprocal(rsm[:, :], c_sb[:, C_SMOOTH:C_SMOOTH + 2 * NH])
            nc.vector.reciprocal(rin[:, :], c_sb[:, C_IN:C_IN + 4 * KC])
            nc.vector.tensor_tensor(psc[:, :], col(C_S + 4), col(C_S + 5), ALU.mult)
            nc.vector.memset(ws[:, CROSS, UH:NL], 1.0)
            for kind, lo, n, c in ((CORE, 0, UH, C_S), (CORE, UH, UG, C_S + 1), (CROSS, 0, UH, C_S + 3)):
                last = nc.vector.tensor_copy(ws[:, kind, lo:lo + n], col(c).to_broadcast([P, n]))
            last.then_inc(s.rsm_ok, 1)
            dve.wait_ge(s.rsm_ok, 1)
            nc.vector.tensor_scalar(rsm[:, 0:NH], rsm[:, 0:NH], col(C_S + 2), None, ALU.mult).then_inc(s.rsm_ok, 1)
            nc.vector.tensor_tensor(epsw[:, :, :], ws[:, :, :], ws[:, :, :], ALU.mult).then_inc(s.setup, 1)
            dve.wait_ge(s.setup, 1)
            nc.vector.reciprocal(epsw[:, :, :], epsw[:, :, :]).then_inc(s.setup, 1)
            dve.wait_ge(s.setup, 2)
            nc.vector.tensor_scalar(epsw[:, :, :], epsw[:, :, :], EPS, None, ALU.mult).then_inc(s.setup, 1)
            dve.wait_ge(s.setup, 3)
            nc.vector.tensor_copy(cntb[:, :], c_sb[:, C_BASE:C_BASE + E_]).then_inc(s.setup, 1)
            nc.vector.memset(ones[:, :], 1.0)
            input_statistics(0)
            weights(0)
            input_normalised(0)
            weights(1)
            input_quantised(0, s.xq_core, 0, 1, 2, 3, 4, 5)
            low_parts(0)
            for u in range(2, LEAD):
                weights(u)
            dve.wait_ge(s.r_in, 32)
            nc.vector.tensor_copy(upper[:, :], upper32[:, :])
            batches(dve, slot)
            nc.vector.tensor_tensor(cnt[:, :], cntb[:, :], c_sb[:, C_BASE:C_BASE + E_], ALU.subtract).then_inc(s.cnt_ok, 1)
            dve.wait_ge(s.cnt_ok, 1)
            nc.vector.tensor_scalar(half[:, :], cnt[:, :], 1.0 / P, 0.5 - 0.5 / P, ALU.mult, ALU.add).then_inc(s.halved, 1)
            dve.wait_ge(s.halved, 1)
            nc.vector.tensor_scalar(tiles[:, :], half[:, :], 2.0 ** 23, 2.0 ** 23, ALU.add, ALU.subtract).then_inc(s.tiles_ok, 1)
            dve.wait_ge(s.tiles_ok, 1)
            nc.vector.tensor_scalar(skip[:, :], tiles[:, :], -float(P), float(REG), ALU.mult, ALU.add).then_inc(s.skip_ok, 1)
            src = tiles
            for i, done in enumerate((s.scan0, s.scan1, s.scan2)):
                d = 1 << i
                nc.vector.tensor_copy(scan[i][:, 0:d], src[:, 0:d])
                nc.vector.tensor_tensor(scan[i][:, d:E_], src[:, d:E_], src[:, 0:E_ - d], ALU.add).then_inc(done, 1)
                dve.wait_ge(done, 1)
                src = scan[i]
            shape = [P, NT, E_]
            nc.vector.tensor_tensor(past[:, :, :], src[:, :].unsqueeze(1).to_broadcast(shape),
                                    c_sb[:, C_TILE:C_TILE + NT].unsqueeze(2).to_broadcast(shape), ALU.is_le).then_inc(s.past_ok, 1)
            dve.wait_ge(s.past_ok, 1)
            dve.wait_ge(s.skip_ok, 1)
            nc.vector.tensor_tensor(jump[:, :, :], past[:, :, :], skip[:, :].unsqueeze(1).to_broadcast(shape), ALU.mult).then_inc(s.jump_ok, 1)
            nc.vector.tensor_reduce(expf[:, :], past[:, :, :], AX.X, ALU.add).then_inc(s.expf_ok, 1)
            dve.wait_ge(s.jump_ok, 1)
            nc.vector.tensor_reduce(rowf[:, :], jump[:, :, :], AX.X, ALU.add).then_inc(s.rowf_ok, 1)
            dve.wait_ge(s.rowf_ok, 1)
            nc.vector.scalar_tensor_tensor(out=rowg[:, :], in0=c_sb[:, C_TILE:C_TILE + NT], scalar=float(P), in1=rowf[:, :],
                                           op0=ALU.mult, op1=ALU.add).then_inc(s.rowg_ok, 1)
            dve.wait_ge(s.rowg_ok, 1)
            nc.vector.tensor_copy(m.rowi[:, :], rowg[:, :]).then_inc(s.row_ok, 1)
            dve.wait_ge(s.expf_ok, 1)
            nc.vector.tensor_scalar(m.expi[:, :], expf[:, :], float(E_ - 1), None, ALU.min).then_inc(s.exp_ok, 1)

        @block.gpsimd
        def _(pool):
            def input_factor(bx):
                need_b(pool, s.xvar, bx, 1)
                nc.gpsimd.tensor_tensor(xr[:, 1:2], xr[:, 0:1], neghalf[:, 0:1], ALU.pow).then_inc(s.xfac, 1)

            def send(k, done):
                nc.gpsimd.tensor_tensor(pmark[:, k:k + 1], neghalf[:, 0:1], neghalf[:, 0:1], ALU.mult)
                nc.gpsimd.indirect_dma_start(out=m.rows[:, :], out_offset=bass.IndirectOffsetOnAxis(ap=posi[:, k:k + 1], axis=0),
                                             in_=row[:, k, :], in_offset=None).then_inc(done, 16)

            def centred(u):
                pool.wait_ge(s.wmeaned, u + 1)
                for c in range(KC):
                    v = w_whole(u)[:, c, 0:LW].rearrange("p (h d) -> p h d", d=D)
                    mean = w_mean[:, u, c * NL:(c + 1) * NL].unsqueeze(2).to_broadcast([P, NL, D])
                    last = nc.gpsimd.tensor_tensor(v, v, mean, ALU.subtract)
                last.then_inc(s.wcentred, 1)

            def slot(b, u):
                k = u - L_NORM
                if live(b, k):
                    need(pool, s.var, b, k + 1)
                    need(pool, s.normed, b, k)
                    nc.gpsimd.tensor_tensor(sfac[:, :], svar[:, :], neghalf[:, :], ALU.pow).then_inc(s.fac, 1)
                if u == 1 and live(b, 0):
                    need_b(pool, s.ctx_hi_ok, b, 1)
                    nc.gpsimd.tensor_tensor(ctx_lo[:, :, :], ctx_raw[:, :, :], ctx_hi[:, :, :], ALU.subtract).then_inc(s.ctx_ok, 1)
                k = u - L_SCORE
                if live(b, k):
                    need(pool, s.inverted, b, k + 1)
                    need(pool, s.exped, b, k + 1)
                    nc.gpsimd.tensor_tensor(pp[:, k % 2, :, :], pp[:, k % 2, :, :],
                                            rinv[:, k % 2, :].unsqueeze(2).to_broadcast([P, UH, P]),
                                            ALU.mult).then_inc(s.probs, 1)
                if u == U_XQX and has(b + 1):
                    input_factor(b + 1)
                if u == R_STAT and has(b - 2):
                    need_b(pool, s.h_var, b, -1)
                    nc.gpsimd.tensor_tensor(hr[:, 1:2], hr[:, 0:1], neghalf[:, 0:1], ALU.pow).then_inc(s.h_fac, 1)
                if live(b, u):
                    need(pool, s.copied, b, u + 1)
                    need(pool, s.summed, b, u)
                    nc.gpsimd.tensor_tensor(sq[:, :], raw[:, u % 2, :], raw[:, u % 2, :], ALU.mult).then_inc(s.squared, 1)
                if u == R_SEND0 and has(b - 2):
                    need_b(pool, s.tail0, b, -1)
                    need_b(pool, s.pos_ok, b, -1)
                    send(0, s.sent0)
                if u == R_SEND1 and has(b - 2):
                    need_b(pool, s.tail1, b, -1)
                    send(1, s.sent1)
                if isinstance(b, int) and b == 0:
                    if u + LEAD < NU:
                        centred(u + LEAD)

            nc.gpsimd.memset(neghalf[:, :], -0.5).then_inc(s.half_ok, 1)
            pool.wait_ge(s.half_ok, 1)
            input_factor(0)
            for u in range(LEAD):
                centred(u)
            batches(pool, slot)
            pool.wait_ge(s.sent0, 16 * B)
            pool.wait_ge(s.sent1, 16 * B)


def experts(nc: bass.Bass, m, out):
    fp32, f16, i32 = mybir.dt.float32, mybir.dt.float16, mybir.dt.int32
    ALU, ACT, AX = mybir.AluOpType, mybir.ActivationFunctionType, mybir.AxisListType
    R = 4
    L_UP, L_HT, L_DOWN = 1, 2, 3
    LAST = NT + L_DOWN
    ROUNDS = NT // R

    with ExitStack() as es:
        def sb(name, shape, dt=fp32):
            return es.enter_context(nc.sbuf_tensor(name, shape, dt))

        def ps(name, shape, dt=fp32):
            return es.enter_context(nc.psum_tensor(name, shape, dt))

        xg = sb("t_xg", [P, R, RW])
        xT_hi = sb("t_xT_hi", [P, 2, KC, P], f16)
        xT_lo = sb("t_xT_lo", [P, 2, KC, P], f16)
        sg = sb("t_sg", [P, 2, F_])
        hf = sb("t_hf", [P, 2, F_])
        hT_hi = sb("t_hT_hi", [P, 2, FC, P], f16)
        hT_lo = sb("t_hT_lo", [P, 2, FC, P], f16)
        y = sb("t_y", [P, R, H])
        meta = sb("t_meta", [P, R, 2])
        dest = sb("t_dest", [P, R], i32)
        pmark = sb("t_mark", [P, 1])
        yy = sb("t_yy", [P, R, K_TOP, H])
        warm = sb("t_warm", [P, 1])
        ps_x = ps("t_ps_x", [P, 512])
        ps_g = [ps(f"t_ps_g{i}", [P, F_]) for i in range(2)]
        ps_u = [ps(f"t_ps_u{i}", [P, F_]) for i in range(2)]
        ps_h = ps("t_ps_h", [P, F_])
        ps_d = ps("t_ps_d", [P, 512])

        names = ("warmed in0 in1 in2 in3 xT_ps x_hi x_lo g_ok u_ok silu h_ok hT_ps h_hi h_lo down y_ok meta_ok dest_ok marked sent0 sent1 sent2 sent3 "
                 "y_in0 y_in1 y_in2 y_in3 sum0 sum1 stored").split()
        s = namedtuple("Semaphores", names)(*[es.enter_context(nc.semaphore("t_" + name)) for name in names])
        x_in = (s.in0, s.in1, s.in2, s.in3)
        y_in = (s.y_in0, s.y_in1, s.y_in2, s.y_in3)
        sent = (s.sent0, s.sent1, s.sent2, s.sent3)

        def need(eng, sm, r, k, per=1):
            if isinstance(r, int):
                if R * r + k > 0:
                    eng.wait_ge(sm, per * min(R * r + k, NT))
            else:
                eng.wait_ge(sm, r * (R * per) + per * k)

        def live(r, k):
            return not isinstance(r, int) or 0 <= R * r + k < NT

        def at(r, k):
            return R * r + k if isinstance(r, int) else r * R + k

        def rounds(eng, slot, last):
            for n in range(2 * R):
                slot(n // R, n % R)
            with eng.Fori(2, ROUNDS) as r:
                for u in range(R):
                    slot(r, u)
            for n in range(R * ROUNDS, last):
                slot(n // R, n % R)

        block = es.enter_context(nc.Block())

        @block.sync
        def _(sp):
            def slot(r, u):
                if live(r, u):
                    start = sp.value_load(m.rowi[0:1, bass.ds(at(r, u), 1)], min_val=0, max_val=E_ * REG + (SPARE - 1) * P)
                    need(sp, s.xT_ps, r, u - R + 1)
                    need(sp, s.meta_ok, r, u - R + 1)
                    sp.dma_start(xg[:, u, :], m.rows[bass.ds(start, P), :]).then_inc(x_in[u], 16)

            rounds(sp, slot, NT)
            for i in range(R):
                sp.wait_ge(sent[i], 16 * ((NT - i + R - 1) // R))
            src = m.ybuf[0:K_TOP * T_ALL, :].rearrange("(k b s) d -> b s k d", k=K_TOP, b=B)
            for b in range(B):
                if b >= R:
                    sp.wait_ge(s.sum1, b - R + 1)
                sp.dma_start(yy[:, b % R, :, :], src[b]).then_inc(y_in[b % R], 16)

        @block.tensor
        def _(pe):
            def slot(r, u):
                k = u - L_UP
                if live(r, k):
                    e = pe.value_load(m.expi[0:1, bass.ds(at(r, k), 1)], min_val=0, max_val=E_ - 1)
                    need(pe, s.x_hi, r, k + 1)
                    need(pe, s.x_lo, r, k + 1)
                    need(pe, s.h_ok, r, k - 1)
                    for first, bank, done in ((0, ps_g, s.g_ok), (1, ps_u, s.u_ok)):
                        for c in range(KC):
                            for i, (a, w) in enumerate(((xT_hi, m.w_hi), (xT_lo, m.w_hi), (xT_hi, m.w_lo))):
                                last = nc.tensor.matmul(bank[k % 2][:, :], a[:, k % 2, c, :], w[:, e, first, c * F_:(c + 1) * F_],
                                                        start=(c == 0 and i == 0), stop=(c == KC - 1 and i == 2))
                        last.then_inc(done, 1)
                if live(r, u):
                    pe.wait_ge(x_in[u], (r + 1) * 16) if isinstance(r, int) else pe.wait_ge(x_in[u], r * 16 + 16)
                    need(pe, s.x_lo, r, u)
                    for c in range(KC):
                        last = nc.tensor.transpose(ps_x[:, c * P:(c + 1) * P], xg[:, u, c * P:(c + 1) * P], m.ident[:, :])
                    last.then_inc(s.xT_ps, 1)
                k = u - L_HT
                if live(r, k):
                    need(pe, s.h_ok, r, k + 1)
                    need(pe, s.h_lo, r, k)
                    for f in range(FC):
                        last = nc.tensor.transpose(ps_h[:, f * P:(f + 1) * P], hf[:, k % 2, f * P:(f + 1) * P], m.ident[:, :])
                    last.then_inc(s.hT_ps, 1)
                k = u - L_DOWN
                if live(r, k):
                    e = pe.value_load(m.expi[0:1, bass.ds(at(r, k), 1)], min_val=0, max_val=E_ - 1)
                    need(pe, s.h_lo, r, k + 1)
                    need(pe, s.h_hi, r, k + 1)
                    need(pe, s.y_ok, r, k)
                    for f in range(FC):
                        for i, (a, w) in enumerate(((hT_hi, m.wp_hi), (hT_lo, m.wp_hi), (hT_hi, m.wp_lo))):
                            last = nc.tensor.matmul(ps_d[:, 0:H], a[:, k % 2, f, :], w[:, e, f, :],
                                                    start=(f == 0 and i == 0), stop=(f == FC - 1 and i == 2))
                    last.then_inc(s.down, 1)

            rounds(pe, slot, LAST)

        @block.scalar
        def _(act):
            def slot(r, u):
                k = u - L_UP
                if live(r, k):
                    need(act, s.g_ok, r, k + 1)
                    need(act, s.h_ok, r, k - 1)
                    nc.scalar.activation(sg[:, k % 2, :], ps_g[k % 2][:, :], ACT.Silu, scale=1.0 / WS).then_inc(s.silu, 1)
                if live(r, u):
                    need(act, s.xT_ps, r, u + 1)
                    need(act, s.u_ok, r, u - 1)
                    nc.scalar.activation(xT_hi[:, u % 2, :, :], ps_x[:, 0:KC * P].rearrange("p (c s) -> p c s", c=KC),
                                         ACT.Copy).then_inc(s.x_hi, 1)
                k = u - L_HT
                if live(r, k):
                    need(act, s.hT_ps, r, k + 1)
                    need(act, s.down, r, k - 1)
                    nc.scalar.activation(hT_hi[:, k % 2, :, :], ps_h[:, :].rearrange("p (f s) -> p f s", f=FC),
                                         ACT.Copy).then_inc(s.h_hi, 1)
                k = u - L_DOWN
                if live(r, k):
                    need(act, s.down, r, k + 1)
                    uses = r + k // R
                    if not isinstance(r, int) or uses > 0:
                        act.wait_ge(sent[k % R], uses * 16)
                    nc.scalar.activation(y[:, k % R, :], ps_d[:, 0:H], ACT.Copy, scale=meta[:, k % R, 0:1]).then_inc(s.y_ok, 1)

            nc.scalar.activation(warm[:, :], m.ident[:, 0:1], ACT.Silu).then_inc(s.warmed, 1)
            rounds(act, slot, LAST)
            for b in range(B):
                act.wait_ge(s.sum1, b + 1)
                act.dma_start(out[b], m.h_all[:, b, :]).then_inc(s.stored, 16)
            act.wait_ge(s.stored, 16 * B)

        @block.vector
        def _(dve):
            def c(lo, n):
                return m.c_sb[:, lo:lo + n]

            def slot(r, u):
                k = u - L_UP
                if live(r, k):
                    need(dve, s.silu, r, k + 1)
                    need(dve, s.u_ok, r, k + 1)
                    need(dve, s.hT_ps, r, k - 1)
                    nc.vector.scalar_tensor_tensor(out=hf[:, k % 2, :], in0=sg[:, k % 2, :], scalar=1.0 / WS, in1=ps_u[k % 2][:, :],
                                                   op0=ALU.mult, op1=ALU.mult).then_inc(s.h_ok, 1)
                if live(r, u):
                    need(dve, s.x_hi, r, u + 1)
                    need(dve, s.y_ok, r, u - R + 1)
                    need(dve, s.dest_ok, r, u - R + 1)
                    nc.vector.tensor_copy(meta[:, u, :], xg[:, u, H:RW]).then_inc(s.meta_ok, 1)
                    nc.vector.tensor_tensor(xT_lo[:, u % 2, :, :], ps_x[:, 0:KC * P].rearrange("p (c s) -> p c s", c=KC),
                                            xT_hi[:, u % 2, :, :], ALU.subtract).then_inc(s.x_lo, 1)
                k = u - L_HT
                if live(r, k):
                    need(dve, s.h_hi, r, k + 1)
                    nc.vector.tensor_tensor(hT_lo[:, k % 2, :, :], ps_h[:, :].rearrange("p (f s) -> p f s", f=FC),
                                            hT_hi[:, k % 2, :, :], ALU.subtract).then_inc(s.h_lo, 1)
                k = u - L_DOWN
                if live(r, k):
                    need(dve, s.meta_ok, r, k + 1)
                    uses = r + k // R
                    if not isinstance(r, int) or uses > 0:
                        dve.wait_ge(sent[k % R], uses * 16)
                    nc.vector.tensor_copy(dest[:, k % R:k % R + 1], meta[:, k % R, 1:2]).then_inc(s.dest_ok, 1)

            rounds(dve, slot, LAST)
            for b in range(B):
                dve.wait_ge(y_in[b % R], 16 * (b // R + 1))
                h = m.h_all[:, b, :]
                nc.vector.tensor_tensor(h, h, yy[:, b % R, 0, :], ALU.add).then_inc(s.sum0, 1)
                dve.wait_ge(s.sum0, b + 1)
                nc.vector.tensor_tensor(h, h, yy[:, b % R, 1, :], ALU.add).then_inc(s.sum1, 1)

        @block.gpsimd
        def _(pool):
            def slot(r, u):
                k = u - L_DOWN
                if live(r, k):
                    need(pool, s.y_ok, r, k + 1)
                    need(pool, s.dest_ok, r, k + 1)
                    need(pool, s.marked, r, k)
                    nc.gpsimd.tensor_tensor(pmark[:, 0:1], m.ident[:, 0:1], m.ident[:, 0:1], ALU.mult).then_inc(s.marked, 1)
                    nc.gpsimd.indirect_dma_start(out=m.ybuf[:, :], out_offset=bass.IndirectOffsetOnAxis(ap=dest[:, k % R:k % R + 1], axis=0),
                                                 in_=y[:, k % R, :], in_offset=None).then_inc(sent[k % R], 16)

            rounds(pool, slot, LAST)


def build(nc: bass.Bass, x, ctxT, wunit, wpunit, wup, wdown, gateT, tri, pads, cst, eye, out):
    fp32, f16 = mybir.dt.float32, mybir.dt.float16
    with ExitStack() as es:
        def sb(name, shape, dt=fp32):
            return es.enter_context(nc.sbuf_tensor(name, shape, dt))

        w_parts = sb("w_parts", [P, NU, 2, KC, QW + 2 * KW], f16)
        wp_parts = sb("wp_parts", [P, NU, 2, UH, H], f16)
        names = "h_all ident c_sb w_parts wp_parts w_hi w_lo wp_hi wp_lo cntb expi rowi rows ybuf"
        m = namedtuple("Memory", names)(
            sb("h_all", [P, B, H]),
            sb("ident", [P, P]),
            sb("c_sb", [P, NCST]),
            w_parts, wp_parts,
            w_parts[:, :, 0, :, :], w_parts[:, :, 1, :, :],
            wp_parts[:, :, 0, :, :], wp_parts[:, :, 1, :, :],
            sb("cntb", [P, E_]),
            sb("expi", [P, NT], mybir.dt.int32),
            sb("rowi", [P, NT], mybir.dt.int32),
            nc.dram_tensor("rows", (E_ * REG + SPARE * P, RW), fp32).ap(),
            nc.dram_tensor("ybuf", (K_TOP * T_ALL + (E_ + SPARE) * P, H), fp32).ap(),
        )
        attention(nc, m, x, ctxT, wunit, wpunit, wup, wdown, gateT, tri, pads, cst, eye)
        experts(nc, m, out)


def _layout(a):
    def chunks(w):
        o, i = w.shape
        return w.T.reshape(i // P, P, o).transpose(1, 0, 2)

    A = {k.replace("L0_xattn_", ""): np.asarray(v) for k, v in a.items()}
    kx, vx = A["w_kv_x"][:G * D], A["w_kv_x"][G * D:]
    units, outs = [], []
    wp = A["wproj"].T.reshape(2 * NH, P, H).transpose(1, 0, 2)
    for u in range(NU):
        j = u % HALF
        q, k, v = (A["wq"], A["wk"], A["wv"]) if u < HALF else (A["wqx"], kx, vx)
        w = np.concatenate([q[j * QW:(j + 1) * QW], k[j * KW:(j + 1) * KW], v[j * KW:(j + 1) * KW]], 0)
        units.append(chunks(w))
        outs.append(wp[:, u * UH:(u + 1) * UH])
    up = [np.concatenate([chunks(A["L0_ffn_w1"][e]).reshape(P, -1), chunks(A["L0_ffn_w3"][e]).reshape(P, -1)], 1) for e in range(E_)]
    down = [chunks(A["L0_ffn_w2"][e]).reshape(P, -1) for e in range(E_)]

    def cols(v):
        return v.reshape(-1, P).T
    cst = [cols(A["ln_w"]), cols(A["ln_b"])] + [cols(A[n + "_in_scale"]) for n in ("q", "k", "v", "qx")] + [cols(A["proj_smooth"])]
    cst += [cols(A[n]) for n in ("qln_w", "qln_b", "kln_w", "kln_b", "qxln_w", "qxln_b", "kxln_w", "kxln_b")]
    cst += [np.broadcast_to(A[n].reshape(1, 1), (P, 1)) for n in
            ("wq_scale", "wk_scale", "wv_scale", "wqx_scale", "proj_in_scale", "proj_w_scale")]
    def const(v):
        return np.broadcast_to(np.asarray(v, np.float32), (P, len(v)))
    dest = np.arange(K_TOP)[None, None] * T_ALL + np.arange(B)[None, :, None] * S + np.arange(P)[:, None, None]
    cst += [const(np.arange(E_)), const(np.arange(E_) * REG), const(np.arange(NT)),
            dest.reshape(P, -1).astype(np.float32)]
    pads = np.zeros((E_ + SPARE, P, RW), np.float32)
    pads[:, :, H + 1] = K_TOP * T_ALL + np.arange((E_ + SPARE) * P).reshape(E_ + SPARE, P)
    return {
        "x": A["x"],
        "ctxT": A["ctx_2048"].transpose(0, 2, 1).reshape(B, KC, P, S).transpose(0, 2, 1, 3),
        "wunit": np.stack(units), "wpunit": np.stack(outs), "wup": np.stack(up), "wdown": np.stack(down),
        "gateT": chunks(A["L0_ffn_gate_w"]), "cst": np.concatenate(cst, 1),
        "eye": np.eye(P, dtype=np.float32), "tri": np.triu(np.ones((P, P), np.float32), 1), "pads": pads,
    }


def kernel(**inputs):
    import concourse.bacc as _bacc
    from concourse.bass_utils import run_bass_kernel_spmd as _run

    nc = _bacc.Bacc("TRN2", target_bir_lowering=False, num_devices=1)
    arrays, args = {}, {}
    for name, a in _layout(inputs).items():
        a = np.ascontiguousarray(a)
        arrays[f"in_{name}"] = a
        args[name] = nc.dram_tensor(f"in_{name}", a.shape, mybir.dt.from_np(a.dtype), kind="ExternalInput").ap()
    args["out"] = nc.dram_tensor("out_0", (B, S, H), mybir.dt.float32, kind="ExternalOutput").ap()
    build(nc, **args)
    r = _run(nc, [arrays], core_ids=[0])
    return r.results[0]["out_0"]
```
